# Optimizing a Trainium2 kernel written in Bass

```python
import numpy as np
import jax
import jax.numpy as jnp

def _softmax(x, axis=-1):
    return jax.nn.softmax(x, axis=axis)

def _gelu(x):
    return jax.nn.gelu(x, approximate=True)

def _silu(x):
    return jax.nn.silu(x)

def _sigmoid(x):
    return jax.nn.sigmoid(x)

def _layernorm(x, axis=-1, eps=1e-05):
    m = jnp.mean(x, axis=axis, keepdims=True)
    v = jnp.var(x, axis=axis, keepdims=True)
    return (x - m) / jnp.sqrt(v + eps)

def _scatter_add(tgt, idx, src, axis=0):
    return tgt.at[idx].add(src)

def _segment_sum(src, seg, n):
    return jax.ops.segment_sum(src, seg, n)
kernel_name = 'mk_audio_tower_d1_tok_audfeat512_r4_8bbcc0'

def setup_inputs(seed: int=0):
    np.random.seed(seed)
    _w = jnp.asarray

    def _rec_inputs():
        import jax
        import jax.numpy as jnp
        _rk = jax.random.key(seed)
        x = -0.000292821 + 1.00034 * jax.random.normal(jax.random.fold_in(_rk, 1), (8, 750, 128), jnp.float32)
        return x
    x = _rec_inputs()

    def _L0_tok_setup():
        import jax, jax.numpy as jnp
        import numpy as np
        from jax import lax
        N_HEAD = 8

        def _conv1d_valid(x, w):
            return lax.conv_general_dilated(x, w, window_strides=(1,), padding='VALID', dimension_numbers=('NWC', 'WIO', 'NWC'))

        def _proj(x, w, b, n_head):
            y = jax.nn.elu(_conv1d_valid(x, w) + b)
            B, L, D = y.shape
            y = y.reshape(B, L, n_head, D // n_head)
            return y.transpose(0, 2, 1, 3)
        key = jax.random.key(seed)
        ks = jax.random.split(key, 7)
        d_in, d_out, kern = (128, 128, 3)
        s = 0.05
        return {'x': jax.random.normal(ks[0], (4, 512, d_in), jnp.float32), 'WQ': jax.random.normal(ks[1], (kern, d_in, d_out), jnp.float32) * s, 'WK': jax.random.normal(ks[2], (kern, d_in, d_out), jnp.float32) * s, 'WV': jax.random.normal(ks[3], (kern, d_in, d_out), jnp.float32) * s, 'BQ': jax.random.normal(ks[4], (d_out,), jnp.float32) * s, 'BK': jax.random.normal(ks[5], (d_out,), jnp.float32) * s, 'BV': jax.random.normal(ks[6], (d_out,), jnp.float32) * s}
    _L0_tok_all = _L0_tok_setup()
    _L0_tok_in = {k: v for k, v in _L0_tok_all.items() if k in ('WQ', 'WK', 'WV', 'BQ', 'BK', 'BV')}
    del _L0_tok_all

    def _L0_attn_setup():
        import jax, jax.numpy as jnp
        import numpy as np
        DIM = 128
        QK_DIM = DIM // 8
        EXPAND_DIM = DIM * 2
        LN_EPS = 1e-05

        def _layer_norm(x):
            mu = jnp.mean(x, axis=-1, keepdims=True)
            var = jnp.mean(jnp.square(x - mu), axis=-1, keepdims=True)
            return (x - mu) * jax.lax.rsqrt(var + LN_EPS)
        key = jax.random.key(seed)
        k1, k2, k3 = jax.random.split(key, 3)
        B, N = (8, 512)
        x = jax.random.normal(k1, (B, N, DIM), dtype=jnp.float32)
        out_e = 2 * QK_DIM + 2 * EXPAND_DIM
        be = float(np.sqrt(6.0 / (DIM + out_e)))
        expand = jax.random.uniform(k2, (DIM, out_e), minval=-be, maxval=be, dtype=jnp.float32)
        bp = float(np.sqrt(6.0 / (EXPAND_DIM + DIM)))
        project = jax.random.uniform(k3, (EXPAND_DIM, DIM), minval=-bp, maxval=bp, dtype=jnp.float32)
        position_bias_mult = jnp.array(4.0, dtype=jnp.float32)
        return {'x': x, 'expand': expand, 'project': project, 'position_bias_mult': position_bias_mult}
    _L0_attn_all = _L0_attn_setup()
    _L0_attn_in = {k: v for k, v in _L0_attn_all.items() if k in ('expand', 'project', 'position_bias_mult')}
    del _L0_attn_all

    def _L0_ffn_setup():
        import jax, jax.numpy as jnp
        import numpy as np
        E = 64
        K = 2
        CAP = 128
        H = 128
        FFN = 512
        B, S = (8, 1024)
        key = jax.random.key(seed)
        ks = jax.random.split(key, 6)
        hidden_states = jax.random.normal(ks[0], (B, S, H), dtype=jnp.float32)
        router_w = jax.random.normal(ks[1], (E, H), dtype=jnp.float32) * (0.01 / np.sqrt(H))
        w1 = jax.random.normal(ks[2], (FFN, H), dtype=jnp.float32) * (1.0 / np.sqrt(H))
        b1 = jnp.zeros((FFN,), dtype=jnp.float32)
        w2 = jax.random.normal(ks[3], (H, FFN), dtype=jnp.float32) * (1.0 / np.sqrt(FFN))
        b2 = jnp.zeros((H,), dtype=jnp.float32)
        return {'hidden_states': hidden_states, 'router_w': router_w, 'w1': w1, 'b1': b1, 'w2': w2, 'b2': b2}
    _L0_ffn_all = _L0_ffn_setup()
    _L0_ffn_in = {k: v for k, v in _L0_ffn_all.items() if k in ('router_w', 'w1', 'b1', 'w2', 'b2')}
    del _L0_ffn_all
    return {'x': x, 'L0_tok_WQ': _L0_tok_in['WQ'], 'L0_tok_WK': _L0_tok_in['WK'], 'L0_tok_WV': _L0_tok_in['WV'], 'L0_tok_BQ': _L0_tok_in['BQ'], 'L0_tok_BK': _L0_tok_in['BK'], 'L0_tok_BV': _L0_tok_in['BV'], 'L0_attn_expand': _L0_attn_in['expand'], 'L0_attn_project': _L0_attn_in['project'], 'L0_attn_position_bias_mult': _L0_attn_in['position_bias_mult'], 'L0_ffn_router_w': _L0_ffn_in['router_w'], 'L0_ffn_w1': _L0_ffn_in['w1'], 'L0_ffn_b1': _L0_ffn_in['b1'], 'L0_ffn_w2': _L0_ffn_in['w2'], 'L0_ffn_b2': _L0_ffn_in['b2']}

def reference(x, L0_tok_WQ, L0_tok_WK, L0_tok_WV, L0_tok_BQ, L0_tok_BK, L0_tok_BV, L0_attn_expand, L0_attn_project, L0_attn_position_bias_mult, L0_ffn_router_w, L0_ffn_w1, L0_ffn_b1, L0_ffn_w2, L0_ffn_b2):
    import jax
    import jax.numpy as jnp

    def _L0_tok_ref(x, WQ, WK, WV, BQ, BK, BV):
        import jax, jax.numpy as jnp
        import numpy as np
        from jax import lax
        N_HEAD = 8

        def _conv1d_valid(x, w):
            return lax.conv_general_dilated(x, w, window_strides=(1,), padding='VALID', dimension_numbers=('NWC', 'WIO', 'NWC'))

        def _proj(x, w, b, n_head):
            y = jax.nn.elu(_conv1d_valid(x, w) + b)
            B, L, D = y.shape
            y = y.reshape(B, L, n_head, D // n_head)
            return y.transpose(0, 2, 1, 3)
        q = _proj(x, WQ, BQ, N_HEAD)
        k = _proj(x, WK, BK, N_HEAD)
        v = _proj(x, WV, BV, N_HEAD)
        dh = q.shape[-1]
        scores = jnp.einsum('bhqd,bhkd->bhqk', q, k) / jnp.sqrt(jnp.float32(dh))
        attn = jax.nn.softmax(scores, axis=-1)
        out = jnp.einsum('bhqk,bhkd->bhqd', attn, v)
        B, H, L, D = out.shape
        return out.transpose(0, 2, 1, 3).reshape(B, L, H * D)

    def _L0_attn_ref(x, expand, project, position_bias_mult):
        import jax, jax.numpy as jnp
        import numpy as np
        DIM = 128
        QK_DIM = DIM // 8
        EXPAND_DIM = DIM * 2
        LN_EPS = 1e-05

        def _layer_norm(x):
            mu = jnp.mean(x, axis=-1, keepdims=True)
            var = jnp.mean(jnp.square(x - mu), axis=-1, keepdims=True)
            return (x - mu) * jax.lax.rsqrt(var + LN_EPS)
        B, N, _ = x.shape
        nx = _layer_norm(x)
        h = nx @ expand
        q = h[..., :QK_DIM]
        k = h[..., QK_DIM:2 * QK_DIM]
        linear = h[..., 2 * QK_DIM:2 * QK_DIM + EXPAND_DIM]
        pre_gelu = h[..., 2 * QK_DIM + EXPAND_DIM:]
        gated = linear * jax.nn.gelu(pre_gelu, approximate=False)
        local = gated[..., :EXPAND_DIM - DIM]
        v = gated[..., EXPAND_DIM - DIM:]
        pos = jnp.arange(N)
        rel = (pos[None, :] - pos[:, None]).astype(x.dtype)
        causal = pos[None, :] <= pos[:, None]
        mask = jnp.where(causal, jax.nn.sigmoid(rel + position_bias_mult), -jnp.inf)
        logits = jnp.einsum('bqd,bkd->bqk', q, k) / jnp.sqrt(jnp.array(QK_DIM, dtype=x.dtype)) + mask
        scores = jax.nn.softmax(logits, axis=-1)
        attn = jnp.einsum('bqk,bkd->bqd', scores, v)
        return x + jnp.concatenate([local, attn], axis=-1) @ project

    def _L0_ffn_ref(hidden_states, router_w, w1, b1, w2, b2):
        import jax, jax.numpy as jnp
        import numpy as np
        E = 64
        K = 2
        CAP = 128
        H = 128
        FFN = 512
        B, S = (8, 1024)
        orig_shape = hidden_states.shape
        x = hidden_states.reshape(-1, orig_shape[-1])
        T = x.shape[0]
        N = T * K
        logits = jnp.einsum('th,eh->te', x, router_w)
        probs_full = jax.nn.softmax(logits, axis=-1)
        probs, idx = jax.lax.top_k(probs_full, K)
        flat_e = idx.reshape(-1)
        flat_p = probs.reshape(-1)
        order = jnp.argsort(flat_e, stable=True)
        sorted_e = flat_e[order]
        counts = jnp.zeros((E,), jnp.int32).at[flat_e].add(1)
        offsets = jnp.concatenate([jnp.zeros((1,), jnp.int32), jnp.cumsum(counts)[:-1]])
        pos = jnp.arange(N, dtype=jnp.int32) - offsets[sorted_e]
        keep = pos < CAP
        slot = sorted_e * CAP + jnp.minimum(pos, CAP - 1)
        dest = jnp.where(keep, slot, E * CAP)
        tok = order // K
        buf = jnp.zeros((E * CAP + 1, x.shape[-1]), x.dtype).at[dest].set(x[tok])
        buf = buf[:-1]
        h = jax.nn.gelu(jnp.einsum('nh,fh->nf', buf, w1) + b1, approximate=False)
        y = jnp.einsum('nf,hf->nh', h, w2) + b2
        gate = jnp.where(keep, flat_p[order], 0.0)
        contrib = y[jnp.minimum(slot, E * CAP - 1)] * gate[:, None]
        out = jnp.zeros_like(x).at[tok].add(contrib)
        return out.reshape(orig_shape)
    h = _L0_tok_ref(x, L0_tok_WQ, L0_tok_WK, L0_tok_WV, L0_tok_BQ, L0_tok_BK, L0_tok_BV)
    h = h + _L0_attn_ref(_layernorm(h, axis=-1), L0_attn_expand, L0_attn_project, L0_attn_position_bias_mult)
    h = h + _L0_ffn_ref(_layernorm(h, axis=-1), L0_ffn_router_w, L0_ffn_w1, L0_ffn_b1, L0_ffn_w2, L0_ffn_b2)
    return h

_drawn_inputs = setup_inputs


def setup_inputs(seed=0):
    import zlib

    import numpy as np

    out = dict(_drawn_inputs(seed))
    spreads = {'L0_ffn_b1': (0.0, 0.8), 'L0_ffn_b2': (0.0, 0.8)}
    factors = {'L0_tok_BK': 5.729, 'L0_ffn_router_w': 8.0, 'L0_ffn_w1': 7.506, 'L0_ffn_w2': 6.851}
    for name, (base, spread) in spreads.items():
        noise = np.random.default_rng([zlib.crc32(name.encode()), seed]).standard_normal(out[name].shape)
        drawn = base * np.exp(spread * noise) if base else spread * noise
        out[name] = jnp.asarray(drawn.astype(out[name].dtype))
    for name, factor in factors.items():
        out[name] = (out[name] * factor).astype(out[name].dtype)
    return out
```

```python
from contextlib import ExitStack

import concourse.bass as bass
from concourse import mybir

F32 = mybir.dt.float32
BF16 = mybir.dt.bfloat16
U32 = mybir.dt.uint32
ALU = mybir.AluOpType
ACT = mybir.ActivationFunctionType
AX = mybir.AxisListType

P = 128
B, LX = 8, 750
TAPS = 3
L = LX - TAPS + 1
NT = -(-L // P)
LP = NT * P
REST = L - (NT - 1) * P
XREST = LX - (NT - 1) * P
HALF = L // 2
NH, DH = 8, 16
GH = 4
NG = NH // GH
KS = 6 * DH
KM = KS + 2
STEPS = NG * 2 * NT
RING = 12


def rows(t):
    return P if t < NT - 1 else REST


def token_attention(nc, ctx, hall, x, wq, wk, wv, bq, bk, bv):
    def sb(name, shape, dt):
        return ctx.enter_context(nc.sbuf_tensor(name, shape, dt))

    def psum(name, shape, dt):
        return ctx.enter_context(nc.psum_tensor(name, shape, dt))

    def sem(name):
        return ctx.enter_context(nc.semaphore(name))

    w_sb = {n: sb("w_" + n, [P, TAPS, P], F32) for n in "qkv"}
    b_col = {n: sb("b_" + n, [P, 1], F32) for n in "qk"}
    bv_row = sb("bv_row", [P, P], F32)
    ident = sb("ident", [P, P], F32)
    ident_bf = sb("ident_bf", [P, P], BF16)
    x_in = sb("x_in", [P, NT, P], F32)
    xT = sb("xT", [P, 2, LX + 2], F32)
    elu_exp = sb("elu_exp", [P, 2, HALF], F32)
    elu_neg = sb("elu_neg", [P, 2, HALF], F32)
    elu_out = sb("elu_out", [P, 2, HALF], F32)
    resid = sb("resid", [P, HALF], F32)
    parts = {n: sb("parts_" + n, [P, 3, LP], BF16) for n in "qk"}
    q_rep = sb("q_rep", [KM, 2, NH, LP], BF16)
    k_rep = sb("k_rep", [KM, 2, NH, LP], BF16)
    v_z = sb("v_z", [P, 4 * P], F32)
    v_exp = sb("v_exp", [P, 4 * P], F32)
    v_neg = sb("v_neg", [P, 4 * P], F32)
    v_hat = sb("v_hat", [P, 2, NT * NH, 32], F32)
    probs = sb("probs", [P, RING, HALF], F32)
    out_T = sb("out_T", [P, NG, LP], F32)
    inv_sum = sb("inv_sum", [P, 2, 4 * GH], F32)
    neg_max = sb("neg_max", [P, NH * NT], F32)
    max_parts = sb("max_parts", [P, P], BF16)
    max_T = sb("max_T", [2 * GH * NT, P], BF16)

    ps_max = psum("ps_max", [P, 2, 2, 512], F32)
    ps_st = psum("ps_st", [P, 2, 512], F32)
    ps_pv = psum("ps_pv", [P, 512], F32)
    ps_misc = psum("ps_misc", [P, 512], F32)

    scratch = {n: nc.dram_tensor("scratch_" + n, (3, DH, NH, LP), BF16, kind="Internal").ap() for n in "qk"}

    loaded = sem("a_loaded")
    consts = sem("a_consts")
    x_loaded = sem("a_x_loaded")
    x_turned = sem("a_x_turned")
    xT_ready = sem("a_xT_ready")
    qk_full = sem("a_qk_full")
    qk_exp = sem("a_qk_exp")
    qk_neg = sem("a_qk_neg")
    qk_elu = sem("a_qk_elu")
    pool_chain = sem("a_pool_chain")
    qk_split = sem("a_qk_split")
    scr_done = sem("a_scr_done")
    rep_done = [sem(f"a_rep_done{g}") for g in range(NG)]
    sc_full = sem("b_sc_full")
    sc_max = sem("b_sc_max")
    mx_hi = sem("b_mx_hi")
    mx_split = sem("b_mx_split")
    mx_turned = sem("b_mx_turned")
    mx_copied = sem("b_mx_copied")
    mx_rows = [sem(f"b_mx_rows{g}") for g in range(NG)]
    v_full = sem("b_v_full")
    v_biased = sem("b_v_biased")
    v_exped = sem("b_v_exped")
    v_negd = sem("b_v_negd")
    v_ready = sem("b_v_ready")
    st_full = sem("c_st_full")
    p_ready = sem("c_p_ready")
    pv_done = sem("c_pv_done")
    pv_copied = sem("c_pv_copied")
    o_turned = sem("c_o_turned")
    o_inv = sem("c_o_inv")
    o_done = sem("c_o_done")

    block = ctx.enter_context(nc.Block())
    LOOP0, LOOPS = 1, 3

    def run(eng, body):
        for it in (-1, 0):
            body(it, it % 2, (True, it >= 0, False, False))
        with eng.Fori(0, LOOPS) as r:
            for u in range(2):
                body(r * 2 + (LOOP0 + u), (LOOP0 + u) % 2, (True, True, True, True))
        for it in (B - 1, B):
            body(it, it % 2, (False, it < B, True, True))

    def wait_apart(eng, sem, value):
        if not isinstance(value, int):
            value = eng.to_reg(value)
            eng.wait_ge(loaded, 16 * 6)
        eng.wait_ge(sem, value)

    @block.sync
    def _(sp):
        sp.dma_start(x_in[:, 0:NT - 1, :], x[0, 0:(NT - 1) * P, :].rearrange("(t p) c -> p t c", p=P)).then_inc(x_loaded, 16)
        sp.dma_start(x_in[0:XREST, NT - 1, :], x[0, (NT - 1) * P:LX, :]).then_inc(x_loaded, 16)
        for n, w in (("q", wq), ("k", wk), ("v", wv)):
            sp.dma_start(w_sb[n][:, :, :], w.rearrange("t i o -> i t o")).then_inc(loaded, 16)
        for n, b in (("q", bq), ("k", bk)):
            sp.dma_start(b_col[n][:, :], b.rearrange("(c o) -> c o", o=1)).then_inc(loaded, 16)
        sp.dma_start(bv_row[:, :], bass.AP(tensor=bv.tensor, offset=0, ap=[[0, P], [1, P]])).then_inc(loaded, 16)

        def replicate(odd, g):
            gs = slice(GH * g, GH * g + GH)
            for n, rep in (("q", q_rep), ("k", k_rep)):
                for r0, n_terms in ((0, 3), (3 * DH, 2), (5 * DH, 1)):
                    part = {0: 0, 3 * DH: 1, 5 * DH: 2}[r0] if n == "q" else 0
                    step = 0 if n == "q" else DH * NH * LP
                    src = bass.AP(tensor=scratch[n].tensor, offset=part * DH * NH * LP + GH * g * LP,
                                  ap=[[step, n_terms], [NH * LP, DH], [1, GH * LP]])
                    sp.dma_start(rep[r0:r0 + n_terms * DH, odd, gs, :], src).then_inc(rep_done[g], 16)

        def maxima_rows(it, odd, g):
            wait_apart(sp, mx_copied, it * NG + g + 1)
            for j in range(2):
                sp.dma_start(q_rep[KS + j:KS + j + 1, odd, GH * g:GH * g + GH, :],
                             max_T[j * GH * NT:(j + 1) * GH * NT, :]).then_inc(mx_rows[g], 16)

        def body(it, odd, stages):
            a, b, b1, c = stages
            nxt = 1 - odd
            if a and not (isinstance(it, int) and it < 0):
                wait_apart(sp, x_turned, (it + 1) * 2)
                sp.dma_start(x_in[:, 0:NT - 1, :],
                             x[bass.ds(it + 1, 1), 0:(NT - 1) * P, :].rearrange("b (t p) c -> p (b t) c", p=P)).then_inc(x_loaded, 16)
                sp.dma_start(x_in[0:XREST, NT - 1, :],
                             x[bass.ds(it + 1, 1), (NT - 1) * P:LX, :].rearrange("b p c -> p (b c)")).then_inc(x_loaded, 16)
            if b1:
                maxima_rows(it - 1, nxt, 1)
            if a:
                wait_apart(sp, qk_split, (it + 1) * 4 + 4)
                if not isinstance(it, int) or it >= 0:
                    wait_apart(sp, rep_done[1], (it + 1) * 96)
                for n in "qk":
                    for j in range(3):
                        sp.dma_start(scratch[n][j].rearrange("d h l -> h d l"), parts[n][:, j, :]).then_inc(scr_done, 16)
                wait_apart(sp, scr_done, (it + 1) * 96 + 96)
                if c:
                    wait_apart(sp, p_ready, (it - 1) * 96 + 48)
                replicate(nxt, 0)
            if b:
                maxima_rows(it, odd, 0)
            if a:
                if c:
                    wait_apart(sp, p_ready, (it - 1) * 96 + 96)
                replicate(nxt, 1)

        run(sp, body)

    @block.gpsimd
    def _(pool):
        pool.memset(ident[:, :], 0.0).then_inc(pool_chain, 1)
        pool.wait_ge(pool_chain, 1)
        pool.affine_select(out=ident[:, :], in_=ident[:, :], compare_op=ALU.not_equal, fill=1.0, base=0,
                           pattern=[[-1, P]], channel_multiplier=1).then_inc(pool_chain, 1)
        pool.wait_ge(pool_chain, 2)
        pool.tensor_copy(ident_bf[:, :], ident[:, :]).then_inc(consts, 1)

        def body(it, odd, stages):
            a, b, b1, _ = stages
            if a:
                for i in range(4):
                    n, hh = "qk"[i // 2], i % 2
                    cols = slice(HALF * hh, HALF * hh + HALF)
                    base = (it + 1) * 12 + (2 + 3 * i)
                    wait_apart(pool, qk_exp, (it + 1) * 4 + i + 1)
                    if i >= 2:
                        wait_apart(pool, qk_elu, (it + 1) * 4 + i - 1)
                    pool.tensor_scalar(elu_neg[:, i % 2, :], elu_exp[:, i % 2, :], 1.0, -1.0, ALU.min, ALU.add).then_inc(qk_neg, 1)
                    wait_apart(pool, qk_elu, (it + 1) * 4 + i + 1)
                    if not isinstance(it, int) or it >= 0:
                        wait_apart(pool, scr_done, (it + 1) * 96)
                    pool.tensor_copy(parts[n][:, 0, cols], elu_out[:, i % 2, :]).then_inc(pool_chain, 1)
                    wait_apart(pool, pool_chain, base + 1)
                    pool.tensor_tensor(resid[:, :], elu_out[:, i % 2, :], parts[n][:, 0, cols], ALU.subtract).then_inc(pool_chain, 1)
                    wait_apart(pool, pool_chain, base + 2)
                    pool.tensor_copy(parts[n][:, 1, cols], resid[:, :]).then_inc(pool_chain, 1)
                    wait_apart(pool, pool_chain, base + 3)
                    pool.tensor_tensor(parts[n][:, 2, cols], resid[:, :], parts[n][:, 1, cols], ALU.subtract).then_inc(qk_split, 1)
            if b:
                for r, nt in ((0, 4), (1, 2)):
                    wait_apart(pool, v_exped, it * 2 + r + 1)
                    if r:
                        wait_apart(pool, v_ready, it * 2 + r)
                    pool.tensor_scalar(v_neg[:, 0:nt * P], v_exp[:, 0:nt * P], 1.0, -1.0, ALU.min, ALU.add).then_inc(v_negd, 1)

        run(pool, body)

    @block.scalar
    def _(act):
        act.wait_ge(loaded, 16 * 6)

        def body(it, odd, stages):
            a, b, b1, c = stages
            nxt = 1 - odd

            def before(s):
                if a and s in (2, 3):
                    r = s - 2
                    lo, hi = (0, 4 * P) if r == 0 else (4 * P, LX)
                    act.wait_ge(x_turned, (it + 1) * 2 + r + 1)
                    act.copy(xT[:, nxt, lo:hi], ps_misc[:, 0:hi - lo]).then_inc(xT_ready, 1)
                if a and s in (5, 7, 9, 11):
                    i = (s - 5) // 2
                    act.wait_ge(qk_full, (it + 1) * 4 + i + 1)
                    if i >= 2:
                        act.wait_ge(qk_neg, (it + 1) * 4 + i - 1)
                    act.activation(elu_exp[:, i % 2, :], ps_misc[:, 0:HALF], ACT.Exp,
                                   bias=b_col["qk"[i // 2]][:, 0:1]).then_inc(qk_exp, 1)
                if c and s in (8, 14, 20, STEPS + 1):
                    i = (s - 7) // 6
                    act.wait_ge(pv_done, (it - 1) * STEPS + 6 * i + 6)
                    act.copy(out_T[:, i // 2, HALF * (i % 2):HALF * (i % 2) + HALF], ps_pv[:, 0:HALF]).then_inc(pv_copied, 1)
                if (b and s == 17) or (b1 and s == 4):
                    g, mb = (0, it) if s == 17 else (1, it - 1)
                    act.wait_ge(mx_turned, mb * NG + g + 1)
                    if g:
                        act.wait_ge(mx_rows[0], mb * 32 + 32)
                    elif b1:
                        act.wait_ge(mx_rows[1], (mb - 1) * 32 + 32)
                    act.copy(max_T[:, :], ps_misc[0:2 * GH * NT, 0:P // 2].bitcast(BF16)).then_inc(mx_copied, 1)
                if b and s in (20, 22):
                    r, nt = ((0, 4), (1, 2))[(s - 20) // 2]
                    act.wait_ge(v_biased, it * 2 + r + 1)
                    if r:
                        act.wait_ge(v_negd, it * 2 + r)
                    act.activation(v_exp[:, 0:nt * P], v_z[:, 0:nt * P], ACT.Exp).then_inc(v_exped, 1)

            for s in range(STEPS + 3):
                before(s)
                if c and s < STEPS:
                    kt = s % NT
                    for j in range(GH):
                        n = GH * s + j
                        act.wait_ge(st_full, (it - 1) * 96 + n + 1)
                        if s >= 3 and j == 0:
                            act.wait_ge(pv_done, (it - 1) * STEPS + s - 2)
                        act.activation(probs[0:rows(kt), n % RING, :], ps_st[0:rows(kt), n % 2, 0:HALF], ACT.Exp,
                                       scale=DH ** -0.5).then_inc(p_ready, 1)

        run(act, body)

    @block.vector
    def _(dve):
        for n in "qk":
            dve.memset(parts[n][:, :, L:LP], 0.0).then_inc(consts, 1)
        dve.memset(k_rep[KS:KM, :, :, :], 1.0).then_inc(consts, 1)
        dve.memset(out_T[:, :, L:LP], 1.0).then_inc(consts, 1)
        dve.memset(neg_max[:, :], 0.0).then_inc(consts, 1)
        dve.memset(max_parts[:, :], 0.0).then_inc(consts, 1)
        dve.memset(inv_sum[:, :, :], 1.0).then_inc(o_done, 4)
        dve.memset(v_hat[:, :, :, DH:32], 0.0).then_inc(consts, 1)
        dve.wait_ge(consts, 8)
        dve.memset(v_hat[:, :, :, DH:DH + 1], 1.0).then_inc(consts, 1)
        dve.wait_ge(loaded, 16 * 6)

        def body(it, odd, stages):
            a, b, b1, c = stages

            def outputs(i, r):
                nt, k = ((4, 2)[r], 2 * i + r)
                dve.wait_ge(o_turned, (it - 1) * 4 + k + 1)
                bank = ps_pv if k == 3 else ps_misc
                o = bank[:, 0:nt * P].rearrange("p (n d) -> p n d", d=32)
                dve.reciprocal(inv_sum[:, r, 0:nt * GH], o[:, :, DH]).then_inc(o_inv, 1)
                dve.wait_ge(o_inv, (it - 1) * 4 + k + 1)
                h = hall[:, bass.ds((it - 1) * LP + 4 * r * P, nt * P)].rearrange("p (t c) -> p t c", c=P)
                dve.tensor_tensor(h[:, :, GH * DH * i:GH * DH * (i + 1)].rearrange("p t (n d) -> p t n d", d=DH),
                                  o[:, :, 0:DH].rearrange("p (t n) d -> p t n d", t=nt),
                                  inv_sum[:, r, 0:nt * GH].rearrange("p (t n) -> p t n", t=nt).unsqueeze(3).broadcast_to([P, nt, GH, DH]),
                                  ALU.mult).then_inc(o_done, 1)

            def maxima(g):
                w = GH * NT
                dve.wait_ge(sc_max, it * 48 + 24 * g + 24)
                if not (isinstance(it, int) and it == 0 and g == 0):
                    dve.wait_ge(mx_turned, it * NG + g)
                dve.tensor_copy(max_parts[:, 0:w], neg_max[:, w * g:w * g + w]).then_inc(mx_hi, 1)
                dve.wait_ge(mx_hi, it * NG + g + 1)
                dve.tensor_tensor(max_parts[:, w:2 * w], neg_max[:, w * g:w * g + w], max_parts[:, 0:w], ALU.subtract).then_inc(mx_split, 1)

            def before(s):
                if a and s in (6, 8, 10, 12):
                    i = (s - 6) // 2
                    dve.wait_ge(qk_neg, (it + 1) * 4 + i + 1)
                    if i >= 2:
                        dve.wait_ge(qk_split, (it + 1) * 4 + i - 1)
                    dve.scalar_tensor_tensor(elu_out[:, i % 2, :], ps_misc[:, 0:HALF], b_col["qk"[i // 2]][:, 0:1],
                                             elu_neg[:, i % 2, :], ALU.add, ALU.max).then_inc(qk_elu, 1)
                if b and s == 12:
                    maxima(0)
                if b and s == STEPS:
                    maxima(1)
                if c and s in (15, 16):
                    outputs(0, s - 15)
                if c and s in (STEPS + 1, STEPS + 2):
                    outputs(1, s - STEPS - 1)
                if b and s in (21, 23):
                    r, nt = ((0, 4), (1, 2))[(s - 21) // 2]
                    dve.wait_ge(v_negd, it * 2 + r + 1)
                    dve.tensor_tensor(v_hat[:, odd, 4 * r * NH:(4 * r + nt) * NH, 0:DH],
                                      v_z[:, 0:nt * P].rearrange("p (n d) -> p n d", d=DH),
                                      v_neg[:, 0:nt * P].rearrange("p (n d) -> p n d", d=DH), ALU.max).then_inc(v_ready, 1)
                if b and s in (19, 21):
                    r, nt = ((0, 4), (1, 2))[(s - 19) // 2]
                    dve.wait_ge(v_full, it * 2 + r + 1)
                    if r:
                        dve.wait_ge(v_ready, it * 2 + r)
                    dve.tensor_tensor(v_z[:, 0:nt * P].rearrange("p (n d) -> p n d", d=P),
                                      ps_misc[:, 0:nt * P].rearrange("p (n d) -> p n d", d=P),
                                      bv_row[:, :].unsqueeze(1).broadcast_to([P, nt, P]), ALU.add).then_inc(v_biased, 1)

            for s in range(STEPS + 3):
                before(s)
                if b and s < STEPS:
                    for n in (2 * s, 2 * s + 1):
                        g, t, j = n // 24, n % 24 // GH, n % GH
                        col = (g * GH + j) * NT + t
                        dve.wait_ge(sc_full, it * 48 + n + 1)
                        dve.tensor_reduce(neg_max[0:rows(t), col:col + 1], ps_max[0:rows(t), n % 2, :, 0:HALF],
                                          AX.XY, ALU.max, negate=True).then_inc(sc_max, 1)

        run(dve, body)

    @block.tensor
    def _(pe):
        pe.wait_ge(loaded, 16 * 6)
        pe.wait_ge(consts, 9)

        def body(it, odd, stages):
            a, b, b1, c = stages
            nxt = 1 - odd
            tenant = [(o_done, it * 4 - 1) if not isinstance(it, int) or it > 0 else None]

            def take_misc(reader, value):
                if tenant[0]:
                    pe.wait_ge(*tenant[0])
                tenant[0] = (reader, value)

            def scores_T(s, j):
                g, qh, kt = s // 12, s % 12 // NT, s % NT
                n, h = GH * s + j, GH * g + j
                if n >= 2:
                    pe.wait_ge(p_ready, (it - 1) * 96 + n - 1)
                if s % 12 == 0 and j == 0:
                    pe.wait_ge(mx_rows[g], (it - 1) * 32 + 32)
                pe.matmul(ps_st[0:rows(kt), n % 2, 0:HALF], k_rep[0:KM, nxt, h, kt * P:kt * P + rows(kt)],
                          q_rep[0:KM, nxt, h, qh * HALF:qh * HALF + HALF], start=True, stop=True).then_inc(st_full, 1)

            def scores(n):
                g, t, j = n // 24, n % 24 // GH, n % GH
                h = GH * g + j
                if n >= 2 or not isinstance(it, int) or it > 0:
                    pe.wait_ge(sc_max, it * 48 + n - 1)
                if n % 24 == 0:
                    pe.wait_ge(rep_done[g], it * 96 + 96)
                for hh in range(2):
                    last = pe.matmul(ps_max[0:rows(t), n % 2, hh, 0:HALF], q_rep[0:KS, odd, h, t * P:t * P + rows(t)],
                                     k_rep[0:KS, odd, h, hh * HALF:hh * HALF + HALF], start=True, stop=True)
                last.then_inc(sc_full, 1)

            def apply(s):
                g, kt = s // 12, s % NT
                pe.wait_ge(p_ready, (it - 1) * 96 + 4 * s + 4)
                if s == 0:
                    pe.wait_ge(o_done, (it - 1) * 4 + 4)
                    pe.wait_ge(v_ready, (it - 1) * 2 + 2)
                if kt == 0 and s > 0:
                    pe.wait_ge(pv_copied, (it - 1) * 4 + s // NT)
                for j in range(GH):
                    n = GH * s + j
                    last = pe.matmul(ps_pv[32 * j:32 * j + 32, 0:HALF], v_hat[0:rows(kt), nxt, kt * NH + GH * g + j, :],
                                     probs[0:rows(kt), n % RING, :], start=(kt == 0), stop=(kt == NT - 1),
                                     tile_position=(0, 32 * j))
                last.then_inc(pv_done, 1)

            def turn_outputs(g, r):
                nt = (4, 2)[r]
                if 2 * g + r < 3:
                    bank = ps_misc
                    take_misc(o_done, it * 4 + 2 * g + r + 1)
                else:
                    bank = ps_pv
                pe.wait_ge(pv_copied, (it - 1) * 4 + 2 * g + 2)
                for t in range(nt):
                    last = pe.transpose(bank[:, t * P:(t + 1) * P], out_T[:, g, (4 * r + t) * P:(4 * r + t + 1) * P], ident[:, :])
                last.then_inc(o_turned, 1)

            def turn_maxima(mb, g):
                take_misc(mx_copied, mb * NG + g + 1)
                pe.wait_ge(mx_split, mb * NG + g + 1)
                pe.transpose(ps_misc[:, 0:P // 2].bitcast(BF16), max_parts[:, :], ident_bf[:, :]).then_inc(mx_turned, 1)

            def after(s):
                if a and s in (1, 2):
                    take_misc(xT_ready, (it + 1) * 2 + s)
                    if s == 1:
                        pe.wait_ge(x_loaded, (it + 1) * 32 + 32)
                    for t in ((0, 1, 2, 3), (4, 5))[s - 1]:
                        n = P if t < NT - 1 else XREST
                        last = pe.transpose(ps_misc[:, (t % 4) * P:(t % 4) * P + n], x_in[0:n, t, :], ident[0:n, 0:n])
                    last.then_inc(x_turned, 1)
                if a and s in (4, 6, 8, 10):
                    i = (s - 4) // 2
                    take_misc(qk_elu, (it + 1) * 4 + i + 1)
                    if i == 0:
                        pe.wait_ge(xT_ready, (it + 1) * 2 + 2)
                    for tap in range(TAPS):
                        lo = tap + HALF * (i % 2)
                        last = pe.matmul(ps_misc[:, 0:HALF], w_sb["qk"[i // 2]][:, tap, :], xT[:, nxt, lo:lo + HALF],
                                         start=(tap == 0), stop=(tap == TAPS - 1))
                    last.then_inc(qk_full, 1)
                if b1 and s == 3:
                    turn_maxima(it - 1, 1)
                if c and s in (14, 15):
                    turn_outputs(0, s - 14)
                if b and s == 16:
                    turn_maxima(it, 0)
                if b and s in (18, 20):
                    r, nt = ((0, 4), (1, 2))[(s - 18) // 2]
                    take_misc(v_biased, it * 2 + r + 1)
                    for t in range(4 * r, 4 * r + nt):
                        for tap in range(TAPS):
                            last = pe.matmul(ps_misc[0:rows(t), (t % 4) * P:(t % 4 + 1) * P], xT[:, odd, tap + t * P:tap + t * P + rows(t)],
                                             w_sb["v"][:, tap, :], start=(tap == 0), stop=(tap == TAPS - 1))
                    last.then_inc(v_full, 1)

            for s in range(STEPS):
                if c:
                    scores_T(s, 0)
                if b:
                    scores(2 * s)
                if c:
                    scores_T(s, 1)
                    if s >= 2:
                        apply(s - 2)
                    scores_T(s, 2)
                if b:
                    scores(2 * s + 1)
                if c:
                    scores_T(s, 3)
                after(s)
            if c:
                apply(STEPS - 2)
                apply(STEPS - 1)
                turn_outputs(1, 0)
                turn_outputs(1, 1)

        run(pe, body)


QK = 16
E2 = 256
NE, CAP = 64, 128
FFN = 512
NF = FFN // P
EPS = 1e-5
NEG = -1e30

PLACES = ([("scores", i) for i in range(NT)] + [("turn3", 0), ("logits", 0)] + [("ffn1", 0), ("ffn1", 1)]
          + [("turn_max", 0)] + [("ffn1", 2), ("ffn1", 3)] + [("scores_T", i) for i in range(NT)]
          + [("ranks", 0), ("ffn2", 0), ("attend", 0), ("turn2", 0), ("turn_att", 0), ("qk", 0), ("qk", 1),
             ("project", 0), ("values", 0), ("values", 1), ("local", 0), ("local", 1)])
SLOT = {place: n % 4 for n, place in enumerate(PLACES)}


def gated_units(nc, ctx, hall, expand, project, pos_mult, router_T, w1_T, b1, w2_T, b2, out):
    def sb(name, shape, dt):
        return ctx.enter_context(nc.sbuf_tensor(name, shape, dt))

    def sem(name):
        return ctx.enter_context(nc.semaphore(name))

    expand_sb = sb("expand_sb", [P, 2 * QK + 2 * E2], F32)
    qk_w = sb("qk_w", [P, 2, 6, QK], F32)
    project_sb = sb("project_sb", [P, 2, P], F32)
    router_sb = sb("router_sb", [P, NE], F32)
    w1_sb = sb("w1_sb", [P, FFN], F32)
    w2_sb = sb("w2_sb", [P, NF, P], F32)
    b1_col = sb("b1_col", [P, NF], F32)
    b2_row = sb("b2_row", [P, P], F32)
    mult_col = sb("mult_col", [P, 1], F32)
    ident = sb("ident2", [P, P], F32)
    ident_bf = sb("ident2_bf", [P, P], BF16)
    mask_q = sb("mask_q", [P, P], BF16)
    mask_k = sb("mask_k", [P, P], BF16)
    before_bf = sb("before_bf", [P, P], BF16)
    ones_bf = sb("ones_bf", [P, P], BF16)
    expert_i = sb("expert_i", [P, NE], mybir.dt.int32)
    expert = sb("expert", [P, NE], F32)
    dist_i = sb("dist_i", [P, L], mybir.dt.int32)
    bias_fac = sb("bias_fac", [P, L], F32)
    take_out = sb("take_out", [KS, 2, 2], F32)
    half_neg = sb("half_neg", [P, NT], F32)
    mv2 = sb("mv2", [P, NT, 2], F32)
    st2 = sb("st2", [P, NT, 6], F32)
    rs = {n: sb("rs_" + n, [P, NT], F32) for n in ("v", "r", "nmr", "v2", "v3", "r2", "z", "zr", "znmr")}
    nx1 = sb("nx1", [P, NT, P], F32)
    nx2 = sb("nx2", [P, NT, P], F32)
    hn = sb("hn", [P, NT, P], F32)
    nx2T = sb("nx2T", [P, LP], F32)
    part_a = sb("part_a", [KS, L], BF16)
    left_a = sb("left_a", [KS, L], F32)
    part_b = sb("part_b", [KS, L], BF16)
    qk_rep = sb("qk_rep", [KM, 2, LP], BF16)
    gel = sb("gel", [P, 4, P], F32)
    vals = sb("vals", [P, NT, P + 1], F32)
    gel_l = sb("gel_l", [P, HALF], F32)
    localT = sb("localT", [P, LP], F32)
    nmax = sb("nmax", [P, NT], F32)
    nmax_parts = sb("nmax_parts", [P, P], BF16)
    nmax_T = sb("nmax_T", [2 * NT, P], BF16)
    p_raw = sb("p_raw", [P, 2, L], F32)
    p_off = [sum(LP - P * j for j in range(k)) for k in range(NT + 1)]
    p_T = sb("p_T", [P, p_off[NT]], F32)
    inv = sb("inv", [P, NT], F32)
    att = sb("att", [P, NT, P], F32)
    attT = sb("attT", [P, LP], F32)
    h2 = sb("h2", [P, NT, P], F32)
    mv3 = sb("mv3", [P, NT, 2], F32)
    st3 = sb("st3", [P, NT, 6], F32)
    nx3 = sb("nx3", [P, NT, P], F32)
    nx3T = sb("nx3T", [P, LP], F32)
    lg = sb("lg", [P, NT, NE], F32)
    top = sb("top", [P, NT, 8], F32)
    top_i = sb("top_i", [P, NT, 8], U32)
    top_f = sb("top_f", [P, NT, 2], F32)
    is_1 = sb("is_1", [P, NT, NE], F32)
    is_2 = sb("is_2", [P, NT, NE], F32)
    chosen = sb("chosen", [P, NT, NE], BF16)
    lg_d = sb("lg_d", [P, NT, NE + 1], F32)
    lg_e = sb("lg_e", [P, NT, NE + 1], F32)
    sum_e = sb("sum_e", [P, NT], F32)
    prob_1 = sb("prob_1", [P, NT], F32)
    prob_2 = sb("prob_2", [P, NT], F32)
    rank = sb("rank", [P, NT, NE], F32)
    kept = sb("kept", [P, NT, NE], F32)
    carry = sb("carry", [P, 2, NE], F32)
    gate = sb("gate", [P, NT], F32)
    hid = sb("hid", [P, NF, LP], F32)
    y_b = sb("y_b", [P, NT, P], F32)
    y_g = sb("y_g", [P, NT, P], F32)
    y_out = sb("y_out", [P, NT, P], F32)

    slots = ctx.enter_context(nc.psum_tensor("slots", [P, 4, 1024], F32))

    loaded = sem("g_loaded")
    setup = sem("g_setup")
    setup_act = sem("g_setup_act")
    setup_dve = sem("g_setup_dve")
    N_SETUP = 35

    S = {n: sem("g_" + n) for n in (
        "x_stat", "x_agg", "x_nx1", "x_pool", "x_nx2", "x_hn", "x_turned", "x_nx2T", "x_qk", "x_part_a", "x_left",
        "x_part_b", "x_rep", "x_val", "x_gel", "x_vals", "x_loc", "x_gel_l", "x_localT",
        "y_sc", "y_max", "y_hi", "y_split", "y_turned_max", "y_maxT", "y_rows", "y_st", "y_raw", "y_p", "y_att",
        "y_inv", "y_norm", "y_turned", "y_attT", "y_proj", "y_h2",
        "z_stat", "z_agg", "z_pool", "z_nx3", "z_turned", "z_nx3T", "z_logit", "z_lg", "z_top", "z_topi", "z_topf",
        "z_is", "z_d", "z_e", "z_sum", "z_p1", "z_p2", "z_w", "z_chosen", "z_weights", "z_ranked", "z_rank",
        "z_kept", "z_gate", "z_f1", "z_hid", "z_f2", "z_yb", "z_yg", "z_out", "z_stored")}

    block = ctx.enter_context(nc.Block())

    def run(eng, body):
        body(-1, (True, False, False))
        body(0, (True, True, False))
        body(1, (True, True, True))
        with eng.Fori(2, B - 1) as r:
            body(r, (True, True, True))
        body(B - 1, (False, True, True))
        body(B, (False, False, True))

    def wait_apart(eng, sem, value):
        if not isinstance(value, int):
            value = eng.to_reg(value)
            eng.wait_ge(loaded, 16 * 8)
        eng.wait_ge(sem, value)

    def first(it, at):
        return isinstance(it, int) and it <= at

    @block.sync
    def _(sp):
        for dst, src in ((expand_sb[:, :], expand), (project_sb[:, :, :], project.rearrange("(a p) n -> p a n", a=2)),
                         (router_sb[:, :], router_T), (w1_sb[:, :], w1_T), (w2_sb[:, :, :], w2_T.rearrange("(f p) n -> p f n", f=NF)),
                         (b1_col[:, :], b1), (b2_row[:, :], bass.AP(tensor=b2.tensor, offset=0, ap=[[0, P], [1, P]])),
                         (mult_col[:, :], bass.AP(tensor=pos_mult.tensor, offset=0, ap=[[0, P], [1, 1]]))):
            sp.dma_start(dst, src).then_inc(loaded, 16)

        def body(it, stages):
            _, y, z = stages
            if y:
                wait_apart(sp, S["y_maxT"], it + 1)
                for j in range(2):
                    sp.dma_start(qk_rep[KS + j:KS + j + 1, 0, :], nmax_T[j * NT:(j + 1) * NT, :]).then_inc(S["y_rows"], 16)
            if z:
                wait_apart(sp, S["z_out"], it)
                sp.dma_start(out[bass.ds(it - 1, 1), 0:(NT - 1) * P, :].rearrange("b (t p) c -> p (b t) c", p=P),
                             y_out[:, 0:NT - 1, :]).then_inc(S["z_stored"], 16)
                sp.dma_start(out[bass.ds(it - 1, 1), (NT - 1) * P:L, :].rearrange("b p c -> p (b c)"),
                             y_out[0:REST, NT - 1, :]).then_inc(S["z_stored"], 16)

        run(sp, body)
        sp.wait_ge(S["z_stored"], 32 * B)

    @block.gpsimd
    def _(pool):
        count = [0]

        def step(ins):
            count[0] += 1
            ins.then_inc(setup, 1)
            pool.wait_ge(setup, count[0])

        def select(t, op, fill, base, per_partition, per_column):
            step(pool.affine_select(out=t, in_=t, compare_op=op, fill=fill, base=base,
                                    pattern=[[per_column, t.shape[-1]]], channel_multiplier=per_partition))

        step(pool.memset(ident[:, :], 0.0))
        select(ident[:, :], ALU.not_equal, 1.0, 0, 1, -1)
        step(pool.tensor_copy(ident_bf[:, :], ident[:, :]))
        step(pool.memset(half_neg[:, :], -0.5))
        step(pool.memset(mask_q[:, :], 0.0))
        select(mask_q[:, :], ALU.is_ge, NEG, 0, 1, -1)
        step(pool.memset(mask_k[:, :], 0.0))
        select(mask_k[:, :], ALU.is_ge, NEG, 0, -1, 1)
        step(pool.memset(before_bf[:, :], 1.0))
        select(before_bf[:, :], ALU.is_ge, 0.0, -1, -1, 1)
        step(pool.memset(ones_bf[:, :], 1.0))
        step(pool.memset(carry[:, :, :], 0.0))
        step(pool.memset(take_out[:, :, :], 0.0))
        for n, which, edges in ((0, 0, ((3, -1.0),)), (0, 1, ((5, -1.0),)),
                                (1, 0, ((1, -1.0), (3, 0.0), (4, -1.0), (5, 0.0))), (1, 1, ((2, -1.0), (3, 0.0)))):
            for term, fill in edges:
                select(take_out[:, n, which:which + 1], ALU.is_ge, fill, term * QK - 1, -1, 0)
        step(pool.iota(expert_i[:, :], pattern=[[1, NE]], base=0, channel_multiplier=0))
        step(pool.tensor_copy(expert[:, :], expert_i[:, :]))
        step(pool.iota(dist_i[:, :], pattern=[[-1, L]], base=0, channel_multiplier=1))
        step(pool.tensor_copy(bias_fac[:, :], dist_i[:, :]))
        step(pool.memset(nmax_parts[:, :], 0.0))
        step(pool.memset(qk_rep[KS:KM, 1, :], 1.0))
        pool.wait_ge(loaded, 16 * 8)
        step(pool.tensor_scalar(mult_col[:, :], mult_col[:, :], -1.0, None, ALU.mult))
        step(pool.tensor_scalar(bias_fac[:, :], bias_fac[:, :], -1.0, mult_col[:, 0:1], ALU.mult, ALU.add))
        step(pool.tensor_scalar(bias_fac[:, :], bias_fac[:, :], 80.0, None, ALU.min))
        step(pool.memset(vals[:, :, P:P + 1], 1.0))
        step(pool.memset(p_T[:, :], 1.0))
        step(pool.memset(localT[:, L:LP], 0.0))
        step(pool.memset(hid[:, :, L:LP], 0.0))
        step(pool.memset(nmax[:, :], 0.0))
        assert count[0] == N_SETUP

        def chain(sem, per, n, k, ins):
            ins.then_inc(sem, 1)
            wait_apart(pool, sem, n * per + k + 1)

        def body(it, stages):
            x, y, z = stages
            if z:
                n = it - 1
                wait_apart(pool, S["z_agg"], n * NT + NT)
                if not first(it, 1):
                    wait_apart(pool, S["z_nx3"], n)
                chain(S["z_pool"], 4, n, 0, pool.tensor_scalar(rs["z"][:, :], mv3[:, :, 1], EPS, None, ALU.add))
                chain(S["z_pool"], 4, n, 1, pool.tensor_tensor(rs["zr"][:, :], rs["z"][:, :], half_neg[:, :], ALU.pow))
                chain(S["z_pool"], 4, n, 2, pool.tensor_scalar(rs["z"][:, :], mv3[:, :, 0], -1.0, None, ALU.mult))
                pool.tensor_tensor(rs["znmr"][:, :], rs["z"][:, :], rs["zr"][:, :], ALU.mult).then_inc(S["z_pool"], 1)
            if x:
                n = it + 1
                wait_apart(pool, S["x_agg"], n * NT + NT)
                if not first(it, -1):
                    wait_apart(pool, S["x_nx1"], n)
                c = lambda k, ins: chain(S["x_pool"], 9, n, k, ins)
                c(0, pool.tensor_scalar(rs["v"][:, :], mv2[:, :, 1], EPS, None, ALU.add))
                c(1, pool.tensor_tensor(rs["r"][:, :], rs["v"][:, :], half_neg[:, :], ALU.pow))
                c(2, pool.tensor_scalar(rs["v"][:, :], mv2[:, :, 0], -1.0, None, ALU.mult))
                c(3, pool.tensor_tensor(rs["nmr"][:, :], rs["v"][:, :], rs["r"][:, :], ALU.mult))
                c(4, pool.tensor_tensor(rs["v2"][:, :], rs["r"][:, :], rs["r"][:, :], ALU.mult))
                c(5, pool.tensor_tensor(rs["v3"][:, :], rs["v2"][:, :], mv2[:, :, 1], ALU.mult))
                c(6, pool.tensor_scalar(rs["v2"][:, :], rs["v3"][:, :], EPS, None, ALU.add))
                c(7, pool.tensor_tensor(rs["r2"][:, :], rs["v2"][:, :], half_neg[:, :], ALU.pow))
                c(8, pool.memset(rs["v3"][:, :], 0.0))
                wait_apart(pool, S["x_nx1"], n + 1)
                if not first(it, -1):
                    wait_apart(pool, S["x_turned"], n)
                pool.tensor_tensor(nx2[:, :, :], nx1[:, :, :], rs["r2"][:, :].unsqueeze(2).broadcast_to([P, NT, P]),
                                   ALU.mult).then_inc(S["x_nx2"], 1)
            if z:
                n = it - 1
                wait_apart(pool, S["z_top"], n * NT + NT)
                if not first(it, 1):
                    wait_apart(pool, S["z_e"], n)
                pool.tensor_tensor(lg_d[:, :, 0:NE], lg[:, :, :], top[:, :, 0:1].broadcast_to([P, NT, NE]),
                                   ALU.subtract).then_inc(S["z_d"], 1)
                pool.tensor_tensor(lg_d[:, :, NE:NE + 1], top[:, :, 1:2], top[:, :, 0:1], ALU.subtract).then_inc(S["z_d"], 1)
                wait_apart(pool, S["z_is"], n * 2 + 2)
                if not first(it, 1):
                    wait_apart(pool, S["z_ranked"], n)
                pool.tensor_tensor(chosen[:, :, :], is_1[:, :, :], is_2[:, :, :], ALU.add).then_inc(S["z_chosen"], 1)
            if y:
                for k in range(NT):
                    w = L - P * k
                    wait_apart(pool, S["y_raw"], it * NT + k + 1)
                    if k == 0 and not first(it, 0):
                        wait_apart(pool, S["y_att"], it)
                    pool.tensor_tensor(p_T[0:rows(k), p_off[k]:p_off[k] + w], p_raw[0:rows(k), k % 2, 0:w],
                                       bias_fac[0:rows(k), 0:w], ALU.mult).then_inc(S["y_p"], 1)
            if z:
                n = it - 1
                wait_apart(pool, S["z_p1"], n + 1)
                pool.tensor_tensor(prob_2[:, :], lg_e[:, :, NE], prob_1[:, :], ALU.mult).then_inc(S["z_p2"], 1)
                pool.tensor_tensor(is_1[:, :, :], is_1[:, :, :], prob_1[:, :].unsqueeze(2).broadcast_to([P, NT, NE]),
                                   ALU.mult).then_inc(S["z_w"], 1)
                wait_apart(pool, S["z_p2"], n + 1)
                pool.tensor_tensor(is_2[:, :, :], is_2[:, :, :], prob_2[:, :].unsqueeze(2).broadcast_to([P, NT, NE]),
                                   ALU.mult).then_inc(S["z_w"], 1)
                wait_apart(pool, S["z_w"], n * 2 + 2)
                pool.tensor_tensor(is_1[:, :, :], is_1[:, :, :], is_2[:, :, :], ALU.add).then_inc(S["z_weights"], 1)
                wait_apart(pool, S["z_gate"], n + 1)
                wait_apart(pool, S["z_yb"], n + 1)
                pool.tensor_tensor(y_g[:, :, :], y_b[:, :, :], gate[:, :].unsqueeze(2).broadcast_to([P, NT, P]),
                                   ALU.mult).then_inc(S["z_yg"], 1)
                wait_apart(pool, S["z_yg"], n + 1)
                if not first(it, 1):
                    wait_apart(pool, S["z_stored"], n * 32)
                pool.tensor_tensor(y_out[:, :, :], y_g[:, :, :], h2[:, :, :], ALU.add).then_inc(S["z_out"], 1)
            if x:
                n = it + 1
                if y:
                    wait_apart(pool, S["y_h2"], n)
                pool.tensor_tensor(hn[:, :, :], nx1[:, :, :], hall[:, bass.ds(n * LP, LP)].rearrange("p (t c) -> p t c", c=P),
                                   ALU.add).then_inc(S["x_hn"], 1)

        run(pool, body)

    @block.scalar
    def _(act):
        act.wait_ge(setup, N_SETUP)
        act.activation(bias_fac[:, :], bias_fac[:, :], ACT.Exp).then_inc(setup_act, 1)
        act.wait_ge(setup_dve, 4)
        act.activation(bias_fac[:, :], bias_fac[:, :], ACT.Exp).then_inc(setup_act, 1)
        act.wait_ge(loaded, 16 * 8)

        def body(it, stages):
            x, y, z = stages
            if z:
                n = it - 1
                act.wait_ge(S["z_turned"], n + 1)
                if not first(it, 1):
                    act.wait_ge(S["z_f1"], n * NF)
                act.copy(nx3T[:, :], slots[:, SLOT["turn3", 0], 0:LP]).then_inc(S["z_nx3T"], 1)
                for f in range(NF):
                    act.wait_ge(S["z_f1"], n * NF + f + 1)
                    if f == 0 and not first(it, 1):
                        act.wait_ge(S["z_f2"], n)
                    act.activation(hid[:, f, 0:L].rearrange("p (a l) -> p a l", a=2),
                                   slots[:, SLOT["ffn1", f], :].rearrange("p (a l) -> p a l", a=2)[:, :, 0:HALF],
                                   ACT.Gelu, bias=b1_col[:, f:f + 1]).then_inc(S["z_hid"], 1)
                    if y and f == 1:
                        maxima(it)
            elif y:
                maxima(it)
            if y:
                for k in range(NT):
                    w = L - P * k
                    act.wait_ge(S["y_st"], it * NT + k + 1)
                    if k >= 2:
                        act.wait_ge(S["y_p"], it * NT + k - 1)
                    act.activation(p_raw[0:rows(k), k % 2, 0:w], slots[0:rows(k), SLOT["scores_T", k], 0:w], ACT.Exp,
                                   scale=QK ** -0.5).then_inc(S["y_raw"], 1)
            if z:
                n = it - 1
                act.wait_ge(S["z_d"], n * 2 + 2)
                if not first(it, 1):
                    act.wait_ge(S["z_p2"], n)
                act.activation(lg_e[:, :, :], lg_d[:, :, :], ACT.Exp).then_inc(S["z_e"], 1)
            if x:
                n = it + 1
                act.wait_ge(S["x_turned"], n + 1)
                act.copy(nx2T[:, :], slots[:, SLOT["turn2", 0], 0:LP]).then_inc(S["x_nx2T"], 1)
            if y:
                act.wait_ge(S["y_turned"], it + 1)
                act.copy(attT[:, :], slots[:, SLOT["turn_att", 0], 0:LP]).then_inc(S["y_attT"], 1)
            if x:
                n = it + 1
                for j in range(2):
                    act.wait_ge(S["x_qk"], n * 2 + j + 1)
                    if n_prev(it, j):
                        act.wait_ge(S["x_rep"], n * 2 + j)
                    act.copy(part_a[:, :].rearrange("p (a l) -> p a l", a=2),
                             slots[0:KS, SLOT["qk", j], :].rearrange("p (a l) -> p a l", a=2)[:, :, 0:HALF]).then_inc(S["x_part_a"], 1)
                    act.wait_ge(S["x_left"], n * 2 + j + 1)
                    act.copy(part_b[:, :], left_a[:, :]).then_inc(S["x_part_b"], 1)
                for j, (t0, nt) in enumerate(((0, 4), (4, 2))):
                    act.wait_ge(S["x_val"], n * 2 + j + 1)
                    if n_prev(it, j):
                        act.wait_ge(S["x_vals"], n * 2 + j)
                    act.activation(gel[:, 0:nt, :], slots[:, SLOT["values", j], 0:nt * E2].rearrange("p (t c) -> p t c", c=E2)[:, :, P:E2],
                                   ACT.Gelu).then_inc(S["x_gel"], 1)
                for j in range(2):
                    act.wait_ge(S["x_loc"], n * 2 + j + 1)
                    if n_prev(it, j):
                        act.wait_ge(S["x_localT"], n * 2 + j)
                    act.activation(gel_l[:, :], slots[:, SLOT["local", j], 512:512 + HALF], ACT.Gelu).then_inc(S["x_gel_l"], 1)

        def n_prev(it, j):
            return j or not first(it, -1)

        def maxima(it):
            act.wait_ge(S["y_turned_max"], it + 1)
            if not first(it, 0):
                act.wait_ge(S["y_rows"], it * 32)
            act.copy(nmax_T[:, :], slots[0:2 * NT, SLOT["turn_max", 0], 0:P // 2].bitcast(BF16)).then_inc(S["y_maxT"], 1)

        run(act, body)

    @block.vector
    def _(dve):
        dve.wait_ge(loaded, 16 * 8)
        for j in range(2):
            dve.tensor_copy(qk_w[:, j, :, :], expand_sb[:, QK * j:QK * j + QK].unsqueeze(1).broadcast_to([P, 6, QK])).then_inc(setup_dve, 1)
        dve.wait_ge(setup_act, 1)
        dve.tensor_scalar(p_raw[:, 0, :], bias_fac[:, :], 1.0, None, ALU.add).then_inc(setup_dve, 1)
        dve.wait_ge(setup_dve, 3)
        dve.reciprocal(bias_fac[:, :], p_raw[:, 0, :]).then_inc(setup_dve, 1)
        dve.wait_ge(setup, N_SETUP)

        def body(it, stages):
            x, y, z = stages
            if z:
                n = it - 1
                dve.wait_ge(S["y_h2"], n + 1)
                for t in range(NT):
                    dve.bn_stats(st3[:, t, :], h2[:, t, :]).then_inc(S["z_stat"], 1)
                wait_apart(dve, S["z_stat"], n * NT + NT)
                for t in range(NT):
                    dve.bn_aggr(mv3[:, t, :], st3[:, t, :]).then_inc(S["z_agg"], 1)
            if x:
                n = it + 1
                for t in range(NT):
                    dve.bn_stats(st2[:, t, :], hall[:, bass.ds(n * LP + t * P, P)]).then_inc(S["x_stat"], 1)
                if not first(it, -1):
                    wait_apart(dve, S["x_pool"], n * 9)
                wait_apart(dve, S["x_stat"], n * NT + NT)
                for t in range(NT):
                    dve.bn_aggr(mv2[:, t, :], st2[:, t, :]).then_inc(S["x_agg"], 1)

            def maxima(t):
                dve.wait_ge(S["y_sc"], it * NT + t + 1)
                dve.tensor_reduce(nmax[0:rows(t), t:t + 1], slots[0:rows(t), SLOT["scores", t], 0:min(P * (t + 1), L)],
                                  AX.X, ALU.max, negate=True).then_inc(S["y_max"], 1)

            if y:
                for t in range(3):
                    maxima(t)
            if z:
                n = it - 1
                dve.wait_ge(S["z_pool"], n * 4 + 4)
                if not first(it, 1):
                    dve.wait_ge(S["z_turned"], n)
                for t in range(NT):
                    last = dve.tensor_scalar(nx3[:, t, :], h2[:, t, :], rs["zr"][:, t:t + 1], rs["znmr"][:, t:t + 1], ALU.mult, ALU.add)
                last.then_inc(S["z_nx3"], 1)
            if x:
                n = it + 1
                dve.wait_ge(S["x_pool"], n * 9 + 4)
                if not first(it, -1):
                    dve.wait_ge(S["x_hn"], n)
                for t in range(NT):
                    last = dve.tensor_scalar(nx1[:, t, :], hall[:, bass.ds(n * LP + t * P, P)], rs["r"][:, t:t + 1],
                                             rs["nmr"][:, t:t + 1], ALU.mult, ALU.add)
                last.then_inc(S["x_nx1"], 1)
            if y:
                for t in range(3, NT):
                    maxima(t)
                dve.wait_ge(S["y_max"], it * NT + NT)
                if not first(it, 0):
                    dve.wait_ge(S["y_turned_max"], it)
                dve.tensor_copy(nmax_parts[:, 0:NT], nmax[:, :]).then_inc(S["y_hi"], 1)
                dve.wait_ge(S["y_hi"], it + 1)
                dve.tensor_tensor(nmax_parts[:, NT:2 * NT], nmax[:, :], nmax_parts[:, 0:NT], ALU.subtract).then_inc(S["y_split"], 1)
            if z:
                n = it - 1
                dve.wait_ge(S["z_logit"], n + 1)
                if not first(it, 1):
                    dve.wait_ge(S["z_d"], n * 2)
                dve.tensor_copy(lg[:, :, :], slots[:, SLOT["logits", 0], 0:NT * NE].rearrange("p (t e) -> p t e", e=NE)).then_inc(S["z_lg"], 1)
                wait_apart(dve, S["z_lg"], n + 1)
                for t in range(NT):
                    dve.max(top[:, t, :], lg[:, t, :]).then_inc(S["z_top"], 1)
                wait_apart(dve, S["z_top"], n * NT + NT)
                for t in range(NT):
                    last = dve.max_index(top_i[:, t, :], top[:, t, :], lg[:, t, :])
                last.then_inc(S["z_topi"], 1)
                dve.wait_ge(S["z_topi"], n + 1)
                dve.tensor_copy(top_f[:, :, :], top_i[:, :, 0:2]).then_inc(S["z_topf"], 1)
                dve.wait_ge(S["z_topf"], n + 1)
                if not first(it, 1):
                    dve.wait_ge(S["z_kept"], n)
                for j, onehot in enumerate((is_1, is_2)):
                    dve.tensor_tensor(onehot[:, :, :], expert[:, :].unsqueeze(1).broadcast_to([P, NT, NE]),
                                      top_f[:, :, j:j + 1].broadcast_to([P, NT, NE]), ALU.is_equal).then_inc(S["z_is"], 1)
                dve.wait_ge(S["z_e"], n + 1)
                dve.tensor_reduce(sum_e[:, :], lg_e[:, :, 0:NE], AX.X, ALU.add).then_inc(S["z_sum"], 1)
                dve.wait_ge(S["z_sum"], n + 1)
                if not first(it, 1):
                    dve.wait_ge(S["z_w"], n * 2)
                dve.reciprocal(prob_1[:, :], sum_e[:, :]).then_inc(S["z_p1"], 1)
                dve.wait_ge(S["z_ranked"], n + 1)
                dve.tensor_tensor(rank[:, :, :], slots[:, SLOT["ranks", 0], 0:NT * NE].rearrange("p (t e) -> p t e", e=NE),
                                  carry[:, 0, :].unsqueeze(1).broadcast_to([P, NT, NE]), ALU.add).then_inc(S["z_rank"], 1)
                dve.tensor_tensor(carry[:, 1, :], carry[:, 0, :], slots[:, SLOT["ranks", 0], 512:512 + NE], ALU.add).then_inc(S["z_rank"], 1)
                dve.wait_ge(S["z_rank"], n * 3 + 2)
                dve.tensor_copy(carry[:, 0, :], carry[:, 1, :]).then_inc(S["z_rank"], 1)
                dve.wait_ge(S["z_weights"], n + 1)
                dve.scalar_tensor_tensor(kept[:, :, :], rank[:, :, :], float(CAP), is_1[:, :, :], ALU.is_lt, ALU.mult).then_inc(S["z_kept"], 1)
                dve.wait_ge(S["z_kept"], n + 1)
                if not first(it, 1):
                    dve.wait_ge(S["z_yg"], n)
                dve.tensor_reduce(gate[:, :], kept[:, :, :], AX.X, ALU.add).then_inc(S["z_gate"], 1)
                dve.wait_ge(S["z_f2"], n + 1)
                dve.tensor_tensor(y_b[:, :, :], slots[:, SLOT["ffn2", 0], 0:NT * P].rearrange("p (t c) -> p t c", c=P),
                                  b2_row[:, :].unsqueeze(1).broadcast_to([P, NT, P]), ALU.add).then_inc(S["z_yb"], 1)
            if y:
                dve.wait_ge(S["y_att"], it + 1)
                o = slots[:, SLOT["attend", 0], :].rearrange("p (a l) -> p a l", a=2)[:, :, 0:3 * (P + 1)].rearrange("p a (t c) -> p a t c", c=P + 1)
                dve.reciprocal(inv[:, :].rearrange("p (a t) -> p a t", a=2), o[:, :, :, P]).then_inc(S["y_inv"], 1)
                dve.wait_ge(S["y_inv"], it + 1)
                if not first(it, 0):
                    dve.wait_ge(S["y_turned"], it)
                for a in range(2):
                    last = dve.tensor_tensor(att[:, 3 * a:3 * a + 3, :], o[:, a, :, 0:P],
                                             inv[:, 3 * a:3 * a + 3].unsqueeze(2).broadcast_to([P, 3, P]), ALU.mult)
                last.then_inc(S["y_norm"], 1)

            def split(j):
                n = it + 1
                z_ps = slots[0:KS, SLOT["qk", j], :].rearrange("p (a l) -> p a l", a=2)[:, :, 0:HALF]
                dve.wait_ge(S["x_part_a"], n * 2 + j + 1)
                dve.scalar_tensor_tensor(left_a[:, :].rearrange("p (a l) -> p a l", a=2), part_a[:, :].rearrange("p (a l) -> p a l", a=2),
                                         take_out[:, j, 0:1], z_ps, ALU.mult, ALU.add).then_inc(S["x_left"], 1)
                dve.wait_ge(S["x_part_b"], n * 2 + j + 1)
                dve.scalar_tensor_tensor(qk_rep[0:KS, j, 0:L], part_b[:, :], take_out[:, j, 1:2], left_a[:, :],
                                         ALU.mult, ALU.add).then_inc(S["x_rep"], 1)

            if x:
                split(0)
                split(1)
            if y:
                dve.wait_ge(S["y_proj"], it + 1)
                dve.wait_ge(S["x_hn"], it + 1)
                if z:
                    dve.wait_ge(S["z_out"], it)
                dve.tensor_tensor(h2[:, :, :], slots[:, SLOT["project", 0], 0:NT * P].rearrange("p (t c) -> p t c", c=P), hn[:, :, :],
                                  ALU.add).then_inc(S["y_h2"], 1)
            if x:
                n = it + 1
                for j, (t0, nt) in enumerate(((0, 4), (4, 2))):
                    dve.wait_ge(S["x_gel"], n * 2 + j + 1)
                    dve.tensor_tensor(vals[:, t0:t0 + nt, 0:P], slots[:, SLOT["values", j], 0:nt * E2].rearrange("p (t c) -> p t c", c=E2)[:, :, 0:P],
                                      gel[:, 0:nt, :], ALU.mult).then_inc(S["x_vals"], 1)
                for j in range(2):
                    dve.wait_ge(S["x_gel_l"], n * 2 + j + 1)
                    dve.tensor_tensor(localT[:, HALF * j:HALF * j + HALF], slots[:, SLOT["local", j], 0:HALF], gel_l[:, :],
                                      ALU.mult).then_inc(S["x_localT"], 1)

        run(dve, body)

    @block.tensor
    def _(pe):
        pe.wait_ge(loaded, 16 * 8)
        pe.wait_ge(setup, N_SETUP)
        pe.wait_ge(setup_dve, 4)
        tenants = {}

        def body(it, stages):
            x, y, z = stages
            if not first(it, 0) and not (isinstance(it, int) and it > B - 1):
                for place, reader, value in ((("values", 0), "x_vals", it * 2 + 1), (("values", 1), "x_vals", it * 2 + 2),
                                             (("local", 0), "x_localT", it * 2 + 1), (("local", 1), "x_localT", it * 2 + 2)):
                    tenants[SLOT[place]] = (S[reader], value)

            def take(name, i, reader, value):
                k = SLOT[name, i]
                if k in tenants:
                    pe.wait_ge(*tenants[k])
                tenants[k] = (S[reader], value)
                return slots[:, k, :]

            def pieces(lo, hi):
                return [(a, min(b, hi)) for a, b in ((lo, 512), (512, 1024)) if a < min(b, hi)] if lo < 512 else [(lo, hi)]

            def turn(slot, src):
                for t in range(NT):
                    last = pe.transpose(slot[:, t * P:(t + 1) * P], src[:, t, :], ident[:, :])
                return last

            def ffn1(f):
                n = it - 1
                o = take("ffn1", f, "z_hid", n * NF + f + 1)
                for h in range(2):
                    last = pe.matmul(o[:, 512 * h:512 * h + HALF], w1_sb[:, f * P:(f + 1) * P], nx3T[:, h * HALF:(h + 1) * HALF],
                                     start=True, stop=True)
                last.then_inc(S["z_f1"], 1)

            if y:
                for t in range(NT):
                    o = take("scores", t, "y_max", it * NT + t + 1)
                    if t == 0:
                        pe.wait_ge(S["x_rep"], it * 2 + 2)
                    w = min(P * (t + 1), L)
                    for a, b in pieces(0, w):
                        diag = b == w
                        last = pe.matmul(o[0:rows(t), a:b], qk_rep[0:KS, 0, t * P:t * P + rows(t)], qk_rep[0:KS, 1, a:b],
                                         start=True, stop=not diag)
                        if diag:
                            last = pe.matmul(o[0:rows(t), t * P:w], ident_bf[0:rows(t), 0:rows(t)], mask_q[0:rows(t), 0:rows(t)],
                                             start=False, stop=True)
                    last.then_inc(S["y_sc"], 1)
            if z:
                n = it - 1
                o = take("turn3", 0, "z_nx3T", n + 1)
                pe.wait_ge(S["z_nx3"], n + 1)
                turn(o, nx3).then_inc(S["z_turned"], 1)
                o = take("logits", 0, "z_lg", n + 1)
                pe.wait_ge(S["z_nx3T"], n + 1)
                for t in range(NT):
                    last = pe.matmul(o[:, t * NE:(t + 1) * NE], nx3T[:, t * P:(t + 1) * P], router_sb[:, :], start=True, stop=True)
                last.then_inc(S["z_logit"], 1)
                ffn1(0)
                ffn1(1)
            if y:
                o = take("turn_max", 0, "y_maxT", it + 1)
                pe.wait_ge(S["y_split"], it + 1)
                pe.transpose(o[:, 0:P // 2].bitcast(BF16), nmax_parts[:, :], ident_bf[:, :]).then_inc(S["y_turned_max"], 1)
            if z:
                ffn1(2)
                ffn1(3)
            if y:
                for k in range(NT):
                    o = take("scores_T", k, "y_raw", it * NT + k + 1)
                    if k == 0:
                        pe.wait_ge(S["y_rows"], it * 32 + 32)
                    w = L - P * k
                    for a, b in pieces(0, w):
                        diag = a == 0
                        last = pe.matmul(o[0:rows(k), a:b], qk_rep[0:KM, 1, k * P:k * P + rows(k)], qk_rep[0:KM, 0, k * P + a:k * P + b],
                                         start=True, stop=not diag)
                        if diag:
                            last = pe.matmul(o[0:rows(k), 0:rows(k)], ident_bf[0:rows(k), 0:rows(k)], mask_k[0:rows(k), 0:rows(k)],
                                             start=False, stop=True)
                    last.then_inc(S["y_st"], 1)
            if z:
                n = it - 1
                o = take("ranks", 0, "z_rank", n * 3 + 2)
                pe.wait_ge(S["z_chosen"], n + 1)
                for t in range(NT):
                    for u in range(t + 1):
                        last = pe.matmul(o[:, t * NE:(t + 1) * NE], (before_bf if u == t else ones_bf)[0:rows(u), :],
                                         chosen[0:rows(u), u, :], start=(u == 0), stop=(u == t))
                for u in range(NT):
                    last = pe.matmul(o[:, 512:512 + NE], ones_bf[0:rows(u), :], chosen[0:rows(u), u, :], start=(u == 0), stop=(u == NT - 1))
                last.then_inc(S["z_ranked"], 1)
                o = take("ffn2", 0, "z_yb", n + 1)
                pe.wait_ge(S["z_hid"], n * NF + NF)
                for t in range(NT):
                    for f in range(NF):
                        last = pe.matmul(o[:, t * P:(t + 1) * P], hid[:, f, (t * P):(t + 1) * P], w2_sb[:, f, :],
                                         start=(f == 0), stop=(f == NF - 1))
                last.then_inc(S["z_f2"], 1)
            if y:
                o = take("attend", 0, "y_norm", it + 1)
                pe.wait_ge(S["x_vals"], it * 2 + 2)
                pe.wait_ge(S["y_p"], it * NT + NT)
                for t in range(NT):
                    c = 512 * (t // 3) + (P + 1) * (t % 3)
                    for k in range(t + 1):
                        q = p_off[k] + P * (t - k)
                        last = pe.matmul(o[:, c:c + P + 1], p_T[0:rows(k), q:q + P], vals[0:rows(k), k, :],
                                         start=(k == 0), stop=(k == t))
                last.then_inc(S["y_att"], 1)
            if x:
                n = it + 1
                o = take("turn2", 0, "x_nx2T", n + 1)
                pe.wait_ge(S["x_nx2"], n + 1)
                turn(o, nx2).then_inc(S["x_turned"], 1)
            if y:
                o = take("turn_att", 0, "y_attT", it + 1)
                pe.wait_ge(S["y_norm"], it + 1)
                turn(o, att).then_inc(S["y_turned"], 1)
            if x:
                for j in range(2):
                    o = take("qk", j, "x_left", n * 2 + j + 1)
                    if j == 0:
                        pe.wait_ge(S["x_nx2T"], n + 1)
                    for h in range(2):
                        last = pe.matmul(o[0:KS, 512 * h:512 * h + HALF], qk_w[:, j, :, :].rearrange("p a c -> p (a c)"),
                                         nx2T[:, h * HALF:(h + 1) * HALF], start=True, stop=True)
                    last.then_inc(S["x_qk"], 1)
            if y:
                o = take("project", 0, "y_h2", it + 1)
                pe.wait_ge(S["y_attT"], it + 1)
                pe.wait_ge(S["x_localT"], it * 2 + 2)
                for t in range(NT):
                    for a, src in enumerate((localT, attT)):
                        last = pe.matmul(o[:, t * P:(t + 1) * P], src[:, t * P:(t + 1) * P], project_sb[:, a, :],
                                         start=(a == 0), stop=(a == 1))
                last.then_inc(S["y_proj"], 1)
            if x:
                for j, (t0, nt) in enumerate(((0, 4), (4, 2))):
                    o = take("values", j, "x_vals", n * 2 + j + 1)
                    for t in range(t0, t0 + nt):
                        c = (t - t0) * E2
                        last = pe.matmul(o[:, c:c + E2].rearrange("p (a c) -> p a c", a=2), nx2T[:, t * P:(t + 1) * P],
                                         expand_sb[:, 2 * QK:2 * QK + 2 * E2].rearrange("p (a c) -> p a c", a=2)[:, :, P:E2],
                                         start=True, stop=True)
                    last.then_inc(S["x_val"], 1)
                for j in range(2):
                    o = take("local", j, "x_localT", n * 2 + j + 1)
                    for a in range(2):
                        c = 2 * QK + a * E2
                        last = pe.matmul(o[:, 512 * a:512 * a + HALF], expand_sb[:, c:c + P], nx2T[:, j * HALF:(j + 1) * HALF],
                                         start=True, stop=True)
                    last.then_inc(S["x_loc"], 1)

        run(pe, body)


def build(nc, x, wq, wk, wv, bq, bk, bv, expand, project, pos_mult, router_T, w1_T, b1, w2_T, b2, out):
    with ExitStack() as whole:
        hall = whole.enter_context(nc.sbuf_tensor("hall", [P, B * LP], F32))
        with ExitStack() as ctx:
            token_attention(nc, ctx, hall, x, wq, wk, wv, bq, bk, bv)
        with ExitStack() as ctx:
            gated_units(nc, ctx, hall, expand, project, pos_mult, router_T, w1_T, b1, w2_T, b2, out)


def kernel(**inputs):
    import numpy as np
    import concourse.bacc as bacc
    from concourse.bass_utils import run_bass_kernel_spmd

    def plain(name):
        return np.ascontiguousarray(inputs[name])

    nc = bacc.Bacc("TRN2", target_bir_lowering=False, num_devices=1)
    arrays = {
        "x": plain("x"),
        "wq": plain("L0_tok_WQ"), "wk": plain("L0_tok_WK"), "wv": plain("L0_tok_WV"),
        "bq": plain("L0_tok_BQ"), "bk": plain("L0_tok_BK"), "bv": plain("L0_tok_BV"),
        "expand": plain("L0_attn_expand"), "project": plain("L0_attn_project"),
        "pos_mult": plain("L0_attn_position_bias_mult").reshape(1),
        "router_T": np.ascontiguousarray(plain("L0_ffn_router_w").T),
        "w1_T": np.ascontiguousarray(plain("L0_ffn_w1").T),
        "b1": np.ascontiguousarray(plain("L0_ffn_b1").reshape(NF, P).T),
        "w2_T": np.ascontiguousarray(plain("L0_ffn_w2").T),
        "b2": plain("L0_ffn_b2"),
    }
    arrays = {"in_" + n: a for n, a in arrays.items()}
    args = [nc.dram_tensor(n, a.shape, mybir.dt.from_np(a.dtype), kind="ExternalInput").ap() for n, a in arrays.items()]
    args.append(nc.dram_tensor("out_h", (B, L, P), F32, kind="ExternalOutput").ap())
    build(nc, *args)
    return run_bass_kernel_spmd(nc, [arrays], core_ids=[0]).results[0]["out_h"]
```

```python
from contextlib import ExitStack

import concourse.bass as bass
from concourse import mybir

F32 = mybir.dt.float32
BF16 = mybir.dt.bfloat16
U32 = mybir.dt.uint32
ALU = mybir.AluOpType
ACT = mybir.ActivationFunctionType
AX = mybir.AxisListType

P = 128
B, LX = 8, 750
TAPS = 3
L = LX - TAPS + 1
NT = -(-L // P)
LP = NT * P
REST = L - (NT - 1) * P
XREST = LX - (NT - 1) * P
HALF = L // 2
NH, DH = 8, 16
GH = 4
NG = NH // GH
KS = 6 * DH
KM = KS + 2
STEPS = NG * 2 * NT
LAG = 15
RING = 12


def rows(t):
    return P if t < NT - 1 else REST


def token_attention(nc, ctx, hall, ahead, x, wq, wk, wv, bq, bk, bv):
    def sb(name, shape, dt):
        return ctx.enter_context(nc.sbuf_tensor(name, shape, dt))

    def psum(name, shape, dt):
        return ctx.enter_context(nc.psum_tensor(name, shape, dt))

    def sem(name):
        return ctx.enter_context(nc.semaphore(name))

    w_sb = {n: sb("w_" + n, [P, TAPS, P], F32) for n in "qkv"}
    b_col = {n: sb("b_" + n, [P, 1], F32) for n in "qk"}
    bv_row = sb("bv_row", [P, P], F32)
    ident = sb("ident", [P, P], F32)
    ident_bf = sb("ident_bf", [P, P], BF16)
    x_in = sb("x_in", [P, NT, P], F32)
    xT = sb("xT", [P, 2, LX + 2], F32)
    elu_exp = sb("elu_exp", [P, 2, HALF], F32)
    elu_neg = sb("elu_neg", [P, 2, HALF], F32)
    elu_out = sb("elu_out", [P, 2, HALF], F32)
    resid = sb("resid", [P, 2, HALF], F32)
    parts = {n: sb("parts_" + n, [P, 3, LP], BF16) for n in "qk"}
    q_rep = sb("q_rep", [KM, 2, NH, LP], BF16)
    k_rep = sb("k_rep", [KM, 2, NH, LP], BF16)
    v_z = sb("v_z", [P, 4 * P], F32)
    v_exp = sb("v_exp", [P, 4 * P], F32)
    v_neg = sb("v_neg", [P, 4 * P], F32)
    v_hat = sb("v_hat", [P, 2, NT * NH, 32], F32)
    probs = sb("probs", [P, RING, HALF], F32)
    out_T = sb("out_T", [P, NG, LP], F32)
    inv_sum = sb("inv_sum", [P, 2, 4 * GH], F32)
    neg_max = sb("neg_max", [P, NH * NT], F32)
    max_parts = sb("max_parts", [P, P], BF16)
    max_T = sb("max_T", [2 * GH * NT, P], BF16)

    ps_max = psum("ps_max", [P, 2, 2, 512], F32)
    ps_st = psum("ps_st", [P, 2, 512], F32)
    ps_pv = psum("ps_pv", [P, 512], F32)
    ps_misc = psum("ps_misc", [P, 512], F32)

    scratch = {n: nc.dram_tensor("scratch_" + n, (3, DH, NH, LP), BF16, kind="Internal").ap() for n in "qk"}

    loaded = sem("a_loaded")
    ident_set = sem("a_ident_set")
    ones_set = sem("a_ones_set")
    padded = sem("a_padded")
    x_loaded = sem("a_x_loaded")
    x_turned = sem("a_x_turned")
    xT_ready = sem("a_xT_ready")
    qk_full = sem("a_qk_full")
    qk_exp = sem("a_qk_exp")
    qk_neg = sem("a_qk_neg")
    qk_elu = sem("a_qk_elu")
    part_1 = sem("a_part_1")
    qk_resid = sem("a_qk_resid")
    part_2 = sem("a_part_2")
    qk_split = sem("a_qk_split")
    ident_steps = sem("a_ident_steps")
    scr_done = sem("a_scr_done")
    rep_done = [sem(f"a_rep_done{g}") for g in range(NG)]
    sc_full = sem("b_sc_full")
    sc_max = sem("b_sc_max")
    mx_hi = sem("b_mx_hi")
    mx_split = sem("b_mx_split")
    mx_turned = sem("b_mx_turned")
    mx_copied = sem("b_mx_copied")
    mx_rows = [sem(f"b_mx_rows{g}") for g in range(NG)]
    v_full = sem("b_v_full")
    v_biased = sem("b_v_biased")
    v_exped = sem("b_v_exped")
    v_negd = sem("b_v_negd")
    v_ready = sem("b_v_ready")
    st_full = sem("c_st_full")
    p_ready = sem("c_p_ready")
    pv_done = sem("c_pv_done")
    pv_copied = sem("c_pv_copied")
    o_turned = sem("c_o_turned")
    o_inv = sem("c_o_inv")
    o_done = sem("c_o_done")

    block = ctx.enter_context(nc.Block())
    PADDED = 7
    LOOP0, LOOPS = 1, 3

    def run(eng, body):
        for it in (-1, 0):
            body(it, it % 2, (True, it >= 0, False))
        with eng.Fori(0, LOOPS) as r:
            for u in range(2):
                body(r * 2 + (LOOP0 + u), (LOOP0 + u) % 2, (True, True, True))
        for it in (B - 1, B):
            body(it, it % 2, (False, it < B, True))

    def probs_step(it, s, stages):
        _, b, b1 = stages
        if s < LAG:
            return (it - 1, s + STEPS - LAG) if b1 else None
        return (it, s - LAG) if b and s < STEPS else None

    def first_of(it):
        return isinstance(it, int) and it < 0

    def misc(it, task):
        if not first_of(it):
            return ps_misc
        return ps_max[:, task % 4 // 2, task % 2, :] if task < 6 else ps_st[:, 0, :]

    def wait_apart(eng, sem, value):
        if not isinstance(value, int):
            value = eng.to_reg(value)
            eng.wait_ge(loaded, 16 * 6)
        eng.wait_ge(sem, value)

    @block.sync
    def _(sp):
        sp.dma_start(x_in[:, 0:NT - 1, :], x[0, 0:(NT - 1) * P, :].rearrange("(t p) c -> p t c", p=P)).then_inc(x_loaded, 16)
        sp.dma_start(x_in[0:XREST, NT - 1, :], x[0, (NT - 1) * P:LX, :]).then_inc(x_loaded, 16)
        for n, w in (("q", wq), ("k", wk), ("v", wv)):
            sp.dma_start(w_sb[n][:, :, :], w.rearrange("t i o -> i t o")).then_inc(loaded, 16)
        for n, b in (("q", bq), ("k", bk)):
            sp.dma_start(b_col[n][:, :], b.rearrange("(c o) -> c o", o=1)).then_inc(loaded, 16)
        sp.dma_start(bv_row[:, :], bass.AP(tensor=bv.tensor, offset=0, ap=[[0, P], [1, P]])).then_inc(loaded, 16)

        def replicate(odd, g):
            gs = slice(GH * g, GH * g + GH)
            for n, rep in (("q", q_rep), ("k", k_rep)):
                for r0, n_terms in ((0, 3), (3 * DH, 2), (5 * DH, 1)):
                    part = {0: 0, 3 * DH: 1, 5 * DH: 2}[r0] if n == "q" else 0
                    step = 0 if n == "q" else DH * NH * LP
                    src = bass.AP(tensor=scratch[n].tensor, offset=part * DH * NH * LP + GH * g * LP,
                                  ap=[[step, n_terms], [NH * LP, DH], [1, GH * LP]])
                    sp.dma_start(rep[r0:r0 + n_terms * DH, odd, gs, :], src).then_inc(rep_done[g], 16)

        def maxima_rows(it, odd, g):
            wait_apart(sp, mx_copied, it * NG + g + 1)
            for j in range(2):
                sp.dma_start(q_rep[KS + j:KS + j + 1, odd, GH * g:GH * g + GH, :],
                             max_T[j * GH * NT:(j + 1) * GH * NT, :]).then_inc(mx_rows[g], 16)

        def body(it, odd, stages):
            a, b, b1 = stages
            nxt = 1 - odd
            if a and not (isinstance(it, int) and it < 0):
                wait_apart(sp, x_turned, (it + 1) * 2)
                sp.dma_start(x_in[:, 0:NT - 1, :],
                             x[bass.ds(it + 1, 1), 0:(NT - 1) * P, :].rearrange("b (t p) c -> p (b t) c", p=P)).then_inc(x_loaded, 16)
                sp.dma_start(x_in[0:XREST, NT - 1, :],
                             x[bass.ds(it + 1, 1), (NT - 1) * P:LX, :].rearrange("b p c -> p (b c)")).then_inc(x_loaded, 16)
            if b:
                if b1:
                    wait_apart(sp, o_done, it * 4)
                replicate(odd, 1)
            if b1:
                maxima_rows(it - 1, nxt, 1)
            if b:
                maxima_rows(it, odd, 0)
            if a:
                wait_apart(sp, qk_split, (it + 1) * 4 + 4)
                if not isinstance(it, int) or it >= 0:
                    wait_apart(sp, rep_done[1], (it + 1) * 96)
                else:
                    sp.wait_ge(padded, PADDED)
                for n in "qk":
                    for j in range(3):
                        sp.dma_start(scratch[n][j].rearrange("d h l -> h d l"), parts[n][:, j, :]).then_inc(scr_done, 16)
                wait_apart(sp, scr_done, (it + 1) * 96 + 96)
                if b1:
                    wait_apart(sp, p_ready, (it - 1) * 96 + 48)
                replicate(nxt, 0)

            if isinstance(it, int) and it == B - 1:
                ahead["load"](sp)

        run(sp, body)

    @block.gpsimd
    def _(pool):
        pool.memset(ident[:, :], 0.0).then_inc(ident_steps, 1)
        pool.wait_ge(ident_steps, 1)
        pool.affine_select(out=ident[:, :], in_=ident[:, :], compare_op=ALU.not_equal, fill=1.0, base=0,
                           pattern=[[-1, P]], channel_multiplier=1).then_inc(ident_steps, 1)
        pool.wait_ge(ident_steps, 2)
        pool.tensor_copy(ident_bf[:, :], ident[:, :]).then_inc(ident_set, 1)
        pool.wait_ge(ident_set, 1)

        def body(it, odd, stages):
            a, b, b1 = stages
            if a:
                for i in range(4):
                    n, hh = "qk"[i // 2], i % 2
                    cols = slice(HALF * hh, HALF * hh + HALF)
                    k = (it + 1) * 4 + i + 1
                    wait_apart(pool, part_1, k)
                    pool.tensor_tensor(resid[:, i % 2, :], elu_out[:, i % 2, :], parts[n][:, 0, cols], ALU.subtract).then_inc(qk_resid, 1)
                    wait_apart(pool, part_2, k)
                    pool.tensor_tensor(parts[n][:, 2, cols], resid[:, i % 2, :], parts[n][:, 1, cols], ALU.subtract).then_inc(qk_split, 1)
                if first_of(it):
                    pool.wait_ge(qk_split, 4)
                    pool.memset(k_rep[KS:KM, :, :, :], 1.0).then_inc(ones_set, 1)
                    pool.wait_ge(ones_set, 1)
                for r, nt in ((0, 4), (1, 2)):
                    wait_apart(pool, v_exped, (it + 1) * 2 + r + 1)
                    if r or not first_of(it):
                        wait_apart(pool, v_ready, (it + 1) * 2 + r)
                    pool.tensor_scalar(v_neg[:, 0:nt * P], v_exp[:, 0:nt * P], 1.0, -1.0, ALU.min, ALU.add).then_inc(v_negd, 1)

        run(pool, body)
        ahead["constants"](pool)
        ahead["scales"](pool, 0, wait_apart)
        ahead["residual"](pool, 0)

    @block.scalar
    def _(act):
        act.wait_ge(loaded, 16 * 6)

        def body(it, odd, stages):
            a, b, b1 = stages
            nxt = 1 - odd

            def before(s):
                if a and s in (2, 3):
                    r = s - 2
                    lo, hi = (0, 4 * P) if r == 0 else (4 * P, LX)
                    act.wait_ge(x_turned, (it + 1) * 2 + r + 1)
                    act.copy(xT[:, nxt, lo:hi], misc(it, r)[:, 0:hi - lo]).then_inc(xT_ready, 1)
                if a and s in (4, 6, 8, 10):
                    i = (s - 4) // 2
                    act.wait_ge(qk_full, (it + 1) * 4 + i + 1)
                    if i >= 2 or not first_of(it):
                        act.wait_ge(qk_neg, (it + 1) * 4 + i - 1)
                    act.activation(elu_exp[:, i % 2, :], misc(it, 2 + i)[:, 0:HALF], ACT.Exp,
                                   bias=b_col["qk"[i // 2]][:, 0:1]).then_inc(qk_exp, 1)
                if isinstance(it, int) and it == B and s == 2:
                    ahead["bias_exp"](act, 0)
                if a and s in (6, 8, 10, 12):
                    i = (s - 6) // 2
                    act.wait_ge(qk_elu, (it + 1) * 4 + i + 1)
                    if not first_of(it) and i % 2 == 0:
                        act.wait_ge(scr_done, (it + 1) * 96)
                    act.copy(parts["qk"[i // 2]][:, 0, HALF * (i % 2):HALF * (i % 2) + HALF], elu_out[:, i % 2, :]).then_inc(part_1, 1)
                if a and s in (7, 9, 11, 13):
                    i = (s - 7) // 2
                    act.wait_ge(qk_resid, (it + 1) * 4 + i + 1)
                    act.copy(parts["qk"[i // 2]][:, 1, HALF * (i % 2):HALF * (i % 2) + HALF], resid[:, i % 2, :]).then_inc(part_2, 1)
                if (b and s == 13) or (b1 and s == 1):
                    g, mb = (0, it) if s == 13 else (1, it - 1)
                    act.wait_ge(mx_turned, mb * NG + g + 1)
                    if g:
                        act.wait_ge(mx_rows[0], mb * 32 + 32)
                    elif b1:
                        act.wait_ge(mx_rows[1], (mb - 1) * 32 + 32)
                    act.copy(max_T[:, :], ps_misc[0:2 * GH * NT, 0:P // 2].bitcast(BF16)).then_inc(mx_copied, 1)
                if a and s in (18, 22):
                    r, nt = ((0, 4), (1, 2))[(s - 18) // 4]
                    act.wait_ge(v_biased, (it + 1) * 2 + r + 1)
                    if r or not first_of(it):
                        act.wait_ge(v_negd, (it + 1) * 2 + r)
                    act.activation(v_exp[:, 0:nt * P], v_z[:, 0:nt * P], ACT.Exp).then_inc(v_exped, 1)

            def copy_outputs(s):
                cs = (s - LAG) % STEPS
                if cs % NT == 1 and (b1 if s <= LAG + 1 else b):
                    cb, i = (it - 1, cs // NT - 1) if s < LAG else (it, cs // NT - 1)
                    if i < 0:
                        cb, i = cb - 1, NG * 2 - 1
                    if isinstance(cb, int) and cb < 0:
                        return
                    act.wait_ge(pv_done, cb * STEPS + NT * i + NT)
                    act.copy(out_T[:, i // 2, HALF * (i % 2):HALF * (i % 2) + HALF], ps_pv[:, 0:HALF]).then_inc(pv_copied, 1)

            for s in range(STEPS):
                before(s)
                c = probs_step(it, s, stages)
                if not c:
                    copy_outputs(s)
                if c:
                    cb, cs = c
                    kt = cs % NT
                    for j in range(GH):
                        n = GH * cs + j
                        if j == GH - 1:
                            copy_outputs(s)
                        act.wait_ge(st_full, cb * 96 + n + 1)
                        if j == 0 and not (isinstance(cb, int) and cb == 0 and cs < 3):
                            act.wait_ge(pv_done, cb * STEPS + cs - 2)
                        act.activation(probs[0:rows(kt), n % RING, :], ps_st[0:rows(kt), n % 2, 0:HALF], ACT.Exp,
                                       scale=DH ** -0.5).then_inc(p_ready, 1)

        run(act, body)

    @block.vector
    def _(dve):
        for n in "qk":
            dve.memset(parts[n][:, :, L:LP], 0.0).then_inc(padded, 1)
        dve.memset(out_T[:, :, L:LP], 1.0).then_inc(padded, 1)
        dve.memset(neg_max[:, :], 0.0).then_inc(padded, 1)
        dve.memset(max_parts[:, :], 0.0).then_inc(padded, 1)
        dve.memset(inv_sum[:, :, :], 1.0).then_inc(o_done, 4)
        dve.memset(v_hat[:, :, :, DH:32], 0.0).then_inc(padded, 1)
        dve.wait_ge(padded, PADDED - 1)
        dve.memset(v_hat[:, :, :, DH:DH + 1], 1.0).then_inc(padded, 1)
        dve.wait_ge(loaded, 16 * 6)

        def body(it, odd, stages):
            a, b, b1 = stages
            nxt = 1 - odd

            def outputs(i, r):
                nt, k = ((4, 2)[r], 2 * i + r)
                dve.wait_ge(o_turned, (it - 1) * 4 + k + 1)
                o = ps_misc[:, 0:nt * P].rearrange("p (n d) -> p n d", d=32)
                dve.reciprocal(inv_sum[:, r, 0:nt * GH], o[:, :, DH]).then_inc(o_inv, 1)
                dve.wait_ge(o_inv, (it - 1) * 4 + k + 1)
                h = hall[:, bass.ds((it - 1) * LP + 4 * r * P, nt * P)].rearrange("p (t c) -> p t c", c=P)
                dve.tensor_tensor(h[:, :, GH * DH * i:GH * DH * (i + 1)].rearrange("p t (n d) -> p t n d", d=DH),
                                  o[:, :, 0:DH].rearrange("p (t n) d -> p t n d", t=nt),
                                  inv_sum[:, r, 0:nt * GH].rearrange("p (t n) -> p t n", t=nt).unsqueeze(3).broadcast_to([P, nt, GH, DH]),
                                  ALU.mult).then_inc(o_done, 1)

            def maxima(mb, g):
                w = GH * NT
                dve.wait_ge(sc_max, mb * 48 + 24 * g + 24)
                if not (isinstance(mb, int) and mb == 0 and g == 0):
                    dve.wait_ge(mx_turned, mb * NG + g)
                dve.tensor_copy(max_parts[:, 0:w], neg_max[:, w * g:w * g + w]).then_inc(mx_hi, 1)
                dve.wait_ge(mx_hi, mb * NG + g + 1)
                dve.tensor_tensor(max_parts[:, w:2 * w], neg_max[:, w * g:w * g + w], max_parts[:, 0:w], ALU.subtract).then_inc(mx_split, 1)

            def before(s):
                if a and s in (5, 7, 9, 11):
                    i = (s - 5) // 2
                    dve.wait_ge(qk_exp, (it + 1) * 4 + i + 1)
                    dve.tensor_scalar(elu_neg[:, i % 2, :], elu_exp[:, i % 2, :], 1.0, -1.0, ALU.min, ALU.add).then_inc(qk_neg, 1)
                    dve.wait_ge(qk_neg, (it + 1) * 4 + i + 1)
                    if i >= 2 or not first_of(it):
                        dve.wait_ge(qk_split, (it + 1) * 4 + i - 1)
                    dve.scalar_tensor_tensor(elu_out[:, i % 2, :], misc(it, 2 + i)[:, 0:HALF], b_col["qk"[i // 2]][:, 0:1],
                                             elu_neg[:, i % 2, :], ALU.add, ALU.max).then_inc(qk_elu, 1)
                if b and s == 12:
                    maxima(it, 0)
                if b1 and s == 0:
                    maxima(it - 1, 1)
                if isinstance(it, int) and it == B and s == 2:
                    ahead["repeat_weights"](dve)
                    dve.wait_ge(o_done, 8)
                    ahead["statistics"](dve, 0, wait_apart)
                    ahead["normalise"](dve, 0)
                    ahead["bias_sigmoid"](dve)
                if b1 and s in (15, 16):
                    outputs(0, s - 15)
                if b1 and s in (LAG + 3, LAG + 4):
                    outputs(1, s - LAG - 3)
                if a and s in (19, 23):
                    r, nt = ((0, 4), (1, 2))[(s - 19) // 4]
                    dve.wait_ge(v_negd, (it + 1) * 2 + r + 1)
                    if b1 and r == 0:
                        dve.wait_ge(pv_done, it * STEPS)
                    dve.tensor_tensor(v_hat[:, nxt, 4 * r * NH:(4 * r + nt) * NH, 0:DH],
                                      v_z[:, 0:nt * P].rearrange("p (n d) -> p n d", d=DH),
                                      v_neg[:, 0:nt * P].rearrange("p (n d) -> p n d", d=DH), ALU.max).then_inc(v_ready, 1)
                if a and s in (17, 21):
                    r, nt = ((0, 4), (1, 2))[(s - 17) // 4]
                    dve.wait_ge(v_full, (it + 1) * 2 + r + 1)
                    if r or not first_of(it):
                        dve.wait_ge(v_ready, (it + 1) * 2 + r)
                    dve.tensor_tensor(v_z[:, 0:nt * P].rearrange("p (n d) -> p n d", d=P),
                                      misc(it, 6 + r)[:, 0:nt * P].rearrange("p (n d) -> p n d", d=P),
                                      bv_row[:, :].unsqueeze(1).broadcast_to([P, nt, P]), ALU.add).then_inc(v_biased, 1)

            for s in range(STEPS):
                before(s)
                if b:
                    for n in (2 * s, 2 * s + 1):
                        g, t, j = n // 24, n % 24 // GH, n % GH
                        col = (g * GH + j) * NT + t
                        dve.wait_ge(sc_full, it * 48 + n + 1)
                        dve.tensor_reduce(neg_max[0:rows(t), col:col + 1], ps_max[0:rows(t), n % 2, :, 0:HALF],
                                          AX.XY, ALU.max, negate=True).then_inc(sc_max, 1)

        run(dve, body)

    @block.tensor
    def _(pe):
        pe.wait_ge(ident_set, 1)

        def body(it, odd, stages):
            a, b, b1 = stages
            nxt = 1 - odd
            tenants = {}
            if not (isinstance(it, int) and it <= 0):
                tenants[0] = (v_biased, it * 2 + 2) if a or b else (o_done, it * 4)

            def take(task, reader, value):
                k = (4 if task >= 6 else task % 4) if first_of(it) else 0
                if k in tenants:
                    pe.wait_ge(*tenants[k])
                tenants[k] = (reader, value)
                return misc(it, task)

            def constants():
                pe.wait_ge(padded, PADDED)
                pe.wait_ge(ones_set, 1)
                pe.wait_ge(qk_elu, 4)

            def scores_T(cb, cs, j):
                g, qh, kt = cs // 12, cs % 12 // NT, cs % NT
                n, h = GH * cs + j, GH * g + j
                slot = odd if cb is it else nxt
                if not (isinstance(cb, int) and cb == 0 and n < 2):
                    pe.wait_ge(p_ready, cb * 96 + n - 1)
                elif n == 0:
                    pe.wait_ge(v_biased, 2)
                if cs % 12 == 0 and j == 0:
                    pe.wait_ge(mx_rows[g], cb * 32 + 32)
                pe.matmul(ps_st[0:rows(kt), n % 2, 0:HALF], k_rep[0:KM, slot, h, kt * P:kt * P + rows(kt)],
                          q_rep[0:KM, slot, h, qh * HALF:qh * HALF + HALF], start=True, stop=True).then_inc(st_full, 1)

            def scores(n):
                g, t, j = n // 24, n % 24 // GH, n % GH
                h = GH * g + j
                if n >= 2 or not isinstance(it, int) or it > 0:
                    pe.wait_ge(sc_max, it * 48 + n - 1)
                if n % 24 == 0:
                    pe.wait_ge(rep_done[g], it * 96 + 96)
                for hh in range(2):
                    last = pe.matmul(ps_max[0:rows(t), n % 2, hh, 0:HALF], q_rep[0:KS, odd, h, t * P:t * P + rows(t)],
                                     k_rep[0:KS, odd, h, hh * HALF:hh * HALF + HALF], start=True, stop=True)
                last.then_inc(sc_full, 1)

            def apply(cb, s):
                g, kt = s // 12, s % NT
                slot = odd if cb is it else nxt
                pe.wait_ge(p_ready, cb * 96 + 4 * s + 4)
                if s == 0:
                    pe.wait_ge(v_ready, cb * 2 + 2)
                if kt == 0 and not (isinstance(cb, int) and cb == 0 and s == 0):
                    pe.wait_ge(pv_copied, cb * 4 + s // NT)
                for j in range(GH):
                    n = GH * s + j
                    last = pe.matmul(ps_pv[32 * j:32 * j + 32, 0:HALF], v_hat[0:rows(kt), slot, kt * NH + GH * g + j, :],
                                     probs[0:rows(kt), n % RING, :], start=(kt == 0), stop=(kt == NT - 1),
                                     tile_position=(0, 32 * j))
                last.then_inc(pv_done, 1)

            def turn_outputs(g, r):
                nt = (4, 2)[r]
                bank = take(0, o_done, it * 4 + 2 * g + r + 1)
                pe.wait_ge(pv_copied, (it - 1) * 4 + 2 * g + 2)
                for t in range(nt):
                    last = pe.transpose(bank[:, t * P:(t + 1) * P], out_T[:, g, (4 * r + t) * P:(4 * r + t + 1) * P], ident[:, :])
                last.then_inc(o_turned, 1)

            def turn_maxima(mb, g):
                bank = take(0, mx_copied, mb * NG + g + 1)
                pe.wait_ge(mx_split, mb * NG + g + 1)
                pe.transpose(bank[:, 0:P // 2].bitcast(BF16), max_parts[:, :], ident_bf[:, :]).then_inc(mx_turned, 1)

            def after(s):
                if b1 and s == 0:
                    turn_maxima(it - 1, 1)
                if a and s in (1, 2):
                    bank = take(s - 1, xT_ready, (it + 1) * 2 + s)
                    if s == 1:
                        pe.wait_ge(x_loaded, (it + 1) * 32 + 32)
                    for t in ((0, 1, 2, 3), (4, 5))[s - 1]:
                        n = P if t < NT - 1 else XREST
                        last = pe.transpose(bank[:, (t % 4) * P:(t % 4) * P + n], x_in[0:n, t, :], ident[0:n, 0:n])
                    last.then_inc(x_turned, 1)
                if a and s in (3, 5, 7, 9):
                    i = (s - 3) // 2
                    bank = take(2 + i, qk_elu, (it + 1) * 4 + i + 1)
                    if i == 0:
                        if first_of(it):
                            pe.wait_ge(loaded, 16 * 6)
                        pe.wait_ge(xT_ready, (it + 1) * 2 + 2)
                    for tap in range(TAPS):
                        lo = tap + HALF * (i % 2)
                        last = pe.matmul(bank[:, 0:HALF], w_sb["qk"[i // 2]][:, tap, :], xT[:, nxt, lo:lo + HALF],
                                         start=(tap == 0), stop=(tap == TAPS - 1))
                    last.then_inc(qk_full, 1)
                if b and s == 12:
                    turn_maxima(it, 0)
                if b1 and s in (14, 15):
                    turn_outputs(0, s - 14)
                if b1 and s in (LAG + 2, LAG + 3):
                    turn_outputs(1, s - LAG - 2)
                if a and s in (16, 20):
                    r, nt = ((0, 4), (1, 2))[(s - 16) // 4]
                    bank = take(6 + r, v_biased, (it + 1) * 2 + r + 1)
                    for t in range(4 * r, 4 * r + nt):
                        for tap in range(TAPS):
                            last = pe.matmul(bank[0:rows(t), (t % 4) * P:(t % 4 + 1) * P], xT[:, nxt, tap + t * P:tap + t * P + rows(t)],
                                             w_sb["v"][:, tap, :], start=(tap == 0), stop=(tap == TAPS - 1))
                    last.then_inc(v_full, 1)

            if b and not b1:
                constants()
            for s in range(STEPS):
                c = probs_step(it, s, stages)
                if c:
                    scores_T(*c, 0)
                if b:
                    scores(2 * s)
                if c:
                    scores_T(*c, 1)
                if LAG <= s < LAG + 2:
                    if b1:
                        apply(it - 1, s - LAG + STEPS - 2)
                elif c:
                    apply(c[0], c[1] - 2)
                if c:
                    scores_T(*c, 2)
                if b:
                    scores(2 * s + 1)
                if c:
                    scores_T(*c, 3)
                after(s)

        run(pe, body)


QK = 16
E2 = 256
NE, CAP = 64, 128
FFN = 512
NF = FFN // P
EPS = 1e-5
NEG = -1e30

PLACES = ([("scores", i) for i in range(NT)] + [("turn3", 0), ("logits", 0)] + [("ffn1", 0), ("ffn1", 1)]
          + [("turn_max", 0)] + [("ffn1", 2), ("ffn1", 3)] + [("scores_T", i) for i in range(NT)]
          + [("ranks", 0), ("ffn2", 0), ("attend", 0), ("turn2", 0), ("turn_att", 0), ("qk", 0), ("qk", 1),
             ("project", 0), ("values", 0), ("values", 1), ("local", 0), ("local", 1)])
SLOT = {place: n % 4 for n, place in enumerate(PLACES)}


def gated_ahead(nc, ctx, hall, expand, project, pos_mult, router_T, w1_T, b1, w2_T, b2):
    def sb(name, shape, dt):
        return ctx.enter_context(nc.sbuf_tensor(name, shape, dt))

    def sem(name):
        return ctx.enter_context(nc.semaphore(name))

    expand_sb = sb("expand_sb", [P, 2 * QK + 2 * E2], F32)
    qk_w = sb("qk_w", [P, 2, 6, QK], F32)
    project_sb = sb("project_sb", [P, 2, P], F32)
    router_sb = sb("router_sb", [P, NE], F32)
    w1_sb = sb("w1_sb", [P, FFN], F32)
    w2_sb = sb("w2_sb", [P, NF, P], F32)
    b1_col = sb("b1_col", [P, NF], F32)
    b2_row = sb("b2_row", [P, P], F32)
    mult_col = sb("mult_col", [P, 1], F32)
    ident = sb("ident2", [P, P], F32)
    ident_bf = sb("ident2_bf", [P, P], BF16)
    mask_q = sb("mask_q", [P, P], BF16)
    mask_k = sb("mask_k", [P, P], BF16)
    before_bf = sb("before_bf", [P, P], BF16)
    ones_bf = sb("ones_bf", [P, P], BF16)
    expert_i = sb("expert_i", [P, NE], mybir.dt.int32)
    expert = sb("expert", [P, NE], F32)
    dist_i = sb("dist_i", [P, L], mybir.dt.int32)
    bias_fac = sb("bias_fac", [P, L], F32)
    take_out = sb("take_out", [KS, 2, 2], F32)
    half_neg = sb("half_neg", [P, NT], F32)
    mv2 = sb("mv2", [P, NT, 2], F32)
    st2 = sb("st2", [P, NT, 6], F32)
    rs = {n: sb("rs_" + n, [P, NT], F32) for n in ("v", "r", "nmr", "v2", "v3", "r2", "z", "zr", "znmr")}
    nx1 = sb("nx1", [P, NT, P], F32)
    nx2 = sb("nx2", [P, NT, P], F32)
    hn = sb("hn", [P, NT, P], F32)

    loaded = sem("g_loaded")
    made = sem("g_made")
    by_term = sem("g_by_term")
    biased = sem("g_biased")
    N_MADE = 27
    S = {n: sem("g_" + n) for n in ("x_stat", "x_agg", "x_pool", "x_nx1", "x_nx2", "x_hn", "x_turned")}

    def load(sp):
        for dst, src in ((expand_sb[:, :], expand), (project_sb[:, :, :], project.rearrange("(a p) n -> p a n", a=2)),
                         (router_sb[:, :], router_T), (w1_sb[:, :], w1_T), (w2_sb[:, :, :], w2_T.rearrange("(f p) n -> p f n", f=NF)),
                         (b1_col[:, :], b1), (b2_row[:, :], bass.AP(tensor=b2.tensor, offset=0, ap=[[0, P], [1, P]])),
                         (mult_col[:, :], bass.AP(tensor=pos_mult.tensor, offset=0, ap=[[0, P], [1, 1]]))):
            sp.dma_start(dst, src).then_inc(loaded, 16)

    def constants(pool):
        count = [0]

        def step(ins):
            count[0] += 1
            ins.then_inc(made, 1)
            pool.wait_ge(made, count[0])

        def select(t, op, fill, base, per_partition, per_column):
            step(pool.affine_select(out=t, in_=t, compare_op=op, fill=fill, base=base,
                                    pattern=[[per_column, t.shape[-1]]], channel_multiplier=per_partition))

        step(pool.memset(ident[:, :], 0.0))
        select(ident[:, :], ALU.not_equal, 1.0, 0, 1, -1)
        step(pool.tensor_copy(ident_bf[:, :], ident[:, :]))
        step(pool.memset(half_neg[:, :], -0.5))
        step(pool.memset(mask_q[:, :], 0.0))
        select(mask_q[:, :], ALU.is_ge, NEG, 0, 1, -1)
        step(pool.memset(mask_k[:, :], 0.0))
        select(mask_k[:, :], ALU.is_ge, NEG, 0, -1, 1)
        step(pool.memset(before_bf[:, :], 1.0))
        select(before_bf[:, :], ALU.is_ge, 0.0, -1, -1, 1)
        step(pool.memset(ones_bf[:, :], 1.0))
        step(pool.memset(take_out[:, :, :], 0.0))
        for n, which, edges in ((0, 0, ((3, -1.0),)), (0, 1, ((5, -1.0),)),
                                (1, 0, ((1, -1.0), (3, 0.0), (4, -1.0), (5, 0.0))), (1, 1, ((2, -1.0), (3, 0.0)))):
            for term, fill in edges:
                select(take_out[:, n, which:which + 1], ALU.is_ge, fill, term * QK - 1, -1, 0)
        step(pool.iota(expert_i[:, :], pattern=[[1, NE]], base=0, channel_multiplier=0))
        step(pool.tensor_copy(expert[:, :], expert_i[:, :]))
        step(pool.iota(dist_i[:, :], pattern=[[-1, L]], base=0, channel_multiplier=1))
        step(pool.tensor_copy(bias_fac[:, :], dist_i[:, :]))
        pool.wait_ge(loaded, 16 * 8)
        step(pool.tensor_scalar(mult_col[:, :], mult_col[:, :], -1.0, None, ALU.mult))
        step(pool.tensor_scalar(bias_fac[:, :], bias_fac[:, :], -1.0, mult_col[:, 0:1], ALU.mult, ALU.add))
        step(pool.tensor_scalar(bias_fac[:, :], bias_fac[:, :], 80.0, None, ALU.min))
        assert count[0] == N_MADE

    def bias_exp(act, k):
        if k == 0:
            act.wait_ge(made, N_MADE)
        else:
            act.wait_ge(biased, 3)
        act.activation(bias_fac[:, :], bias_fac[:, :], ACT.Exp).then_inc(biased, 1)

    def bias_sigmoid(dve):
        dve.wait_ge(biased, 1)
        dve.tensor_scalar(bias_fac[:, :], bias_fac[:, :], 1.0, None, ALU.add).then_inc(biased, 1)
        dve.wait_ge(biased, 2)
        dve.reciprocal(bias_fac[:, :], bias_fac[:, :]).then_inc(biased, 1)

    def repeat_weights(dve):
        dve.wait_ge(loaded, 16 * 8)
        for j in range(2):
            dve.tensor_copy(qk_w[:, j, :, :], expand_sb[:, QK * j:QK * j + QK].unsqueeze(1).broadcast_to([P, 6, QK])).then_inc(by_term, 1)

    def statistics(dve, n, wait_apart):
        for t in range(NT):
            dve.bn_stats(st2[:, t, :], hall[:, bass.ds(n * LP + t * P, P)]).then_inc(S["x_stat"], 1)
        if not isinstance(n, int) or n > 0:
            wait_apart(dve, S["x_pool"], n * 9)
        wait_apart(dve, S["x_stat"], n * NT + NT)
        for t in range(NT):
            dve.bn_aggr(mv2[:, t, :], st2[:, t, :]).then_inc(S["x_agg"], 1)

    def scales(pool, n, wait_apart):
        def step(k, ins):
            ins.then_inc(S["x_pool"], 1)
            wait_apart(pool, S["x_pool"], n * 9 + k + 1)

        wait_apart(pool, S["x_agg"], n * NT + NT)
        if not isinstance(n, int) or n > 0:
            wait_apart(pool, S["x_nx1"], n)
        step(0, pool.tensor_scalar(rs["v"][:, :], mv2[:, :, 1], EPS, None, ALU.add))
        step(1, pool.tensor_tensor(rs["r"][:, :], rs["v"][:, :], half_neg[:, :], ALU.pow))
        step(2, pool.tensor_scalar(rs["v"][:, :], mv2[:, :, 0], -1.0, None, ALU.mult))
        step(3, pool.tensor_tensor(rs["nmr"][:, :], rs["v"][:, :], rs["r"][:, :], ALU.mult))
        step(4, pool.tensor_tensor(rs["v2"][:, :], rs["r"][:, :], rs["r"][:, :], ALU.mult))
        step(5, pool.tensor_tensor(rs["v3"][:, :], rs["v2"][:, :], mv2[:, :, 1], ALU.mult))
        step(6, pool.tensor_scalar(rs["v2"][:, :], rs["v3"][:, :], EPS, None, ALU.add))
        step(7, pool.tensor_tensor(rs["r2"][:, :], rs["v2"][:, :], half_neg[:, :], ALU.pow))
        step(8, pool.memset(rs["v3"][:, :], 0.0))
        wait_apart(pool, S["x_nx1"], n + 1)
        if not isinstance(n, int) or n > 0:
            wait_apart(pool, S["x_turned"], n)
        pool.tensor_tensor(nx2[:, :, :], nx1[:, :, :], rs["r2"][:, :].unsqueeze(2).broadcast_to([P, NT, P]),
                           ALU.mult).then_inc(S["x_nx2"], 1)

    def normalise(dve, n):
        dve.wait_ge(S["x_pool"], n * 9 + 4)
        if not isinstance(n, int) or n > 0:
            dve.wait_ge(S["x_hn"], n)
        for t in range(NT):
            last = dve.tensor_scalar(nx1[:, t, :], hall[:, bass.ds(n * LP + t * P, P)], rs["r"][:, t:t + 1],
                                     rs["nmr"][:, t:t + 1], ALU.mult, ALU.add)
        last.then_inc(S["x_nx1"], 1)

    def residual(pool, n):
        pool.tensor_tensor(hn[:, :, :], nx1[:, :, :], hall[:, bass.ds(n * LP, LP)].rearrange("p (t c) -> p t c", c=P),
                           ALU.add).then_inc(S["x_hn"], 1)

    return dict(
        expand_sb=expand_sb, by_term=by_term, biased=biased, bias_exp=bias_exp, bias_sigmoid=bias_sigmoid, repeat_weights=repeat_weights, qk_w=qk_w, project_sb=project_sb, router_sb=router_sb, w1_sb=w1_sb, w2_sb=w2_sb,
        b1_col=b1_col, b2_row=b2_row, mult_col=mult_col, ident=ident, ident_bf=ident_bf, mask_q=mask_q,
        mask_k=mask_k, before_bf=before_bf, ones_bf=ones_bf, expert_i=expert_i, expert=expert, dist_i=dist_i,
        bias_fac=bias_fac, take_out=take_out, half_neg=half_neg, mv2=mv2, st2=st2, rs=rs,
        nx1=nx1, nx2=nx2, hn=hn, loaded=loaded, made=made, S=S,
        N_MADE=N_MADE, load=load, constants=constants, statistics=statistics, scales=scales, normalise=normalise,
        residual=residual)


def gated_units(nc, ctx, G, hall, out):
    def sb(name, shape, dt):
        return ctx.enter_context(nc.sbuf_tensor(name, shape, dt))

    def sem(name):
        return ctx.enter_context(nc.semaphore(name))

    by_term, biased, bias_exp = (G[n] for n in ("by_term", "biased", "bias_exp"))
    expand_sb, qk_w, project_sb, router_sb, w1_sb, w2_sb, b1_col, b2_row = (G[n] for n in "expand_sb qk_w project_sb router_sb w1_sb w2_sb b1_col b2_row".split())
    mult_col, ident, ident_bf, mask_q, mask_k, before_bf, ones_bf, expert_i = (G[n] for n in "mult_col ident ident_bf mask_q mask_k before_bf ones_bf expert_i".split())
    expert, dist_i, bias_fac, take_out, half_neg, mv2, st2, rs = (G[n] for n in "expert dist_i bias_fac take_out half_neg mv2 st2 rs".split())
    nx1, nx2, hn, loaded, made = (G[n] for n in "nx1 nx2 hn loaded made".split())
    nx2T = sb("nx2T", [P, LP], F32)
    part_a = sb("part_a", [KS, L], BF16)
    left_a = sb("left_a", [KS, L], F32)
    part_b = sb("part_b", [KS, L], BF16)
    qk_rep = sb("qk_rep", [KM, 2, LP], BF16)
    gel = sb("gel", [P, 4, P], F32)
    vals = sb("vals", [P, NT, P + 1], F32)
    gel_l = sb("gel_l", [P, HALF], F32)
    localT = sb("localT", [P, LP], F32)
    nmax = sb("nmax", [P, NT], F32)
    nmax_parts = sb("nmax_parts", [P, P], BF16)
    nmax_T = sb("nmax_T", [2 * NT, P], BF16)
    p_raw = sb("p_raw", [P, 2, L], F32)
    p_off = [sum(LP - P * j for j in range(k)) for k in range(NT + 1)]
    p_T = sb("p_T", [P, p_off[NT]], F32)
    inv = sb("inv", [P, NT], F32)
    att = sb("att", [P, NT, P], F32)
    attT = sb("attT", [P, LP], F32)
    h2 = sb("h2", [P, NT, P], F32)
    mv3 = sb("mv3", [P, NT, 2], F32)
    st3 = sb("st3", [P, NT, 6], F32)
    nx3 = sb("nx3", [P, NT, P], F32)
    nx3T = sb("nx3T", [P, LP], F32)
    lg = sb("lg", [P, NT, NE], F32)
    top = sb("top", [P, NT, 8], F32)
    top_i = sb("top_i", [P, NT, 8], U32)
    top_f = sb("top_f", [P, NT, 2], F32)
    is_1 = sb("is_1", [P, NT, NE], F32)
    is_2 = sb("is_2", [P, NT, NE], F32)
    chosen = sb("chosen", [P, NT, NE], BF16)
    lg_d = sb("lg_d", [P, NT, NE + 1], F32)
    lg_e = sb("lg_e", [P, NT, NE + 1], F32)
    sum_e = sb("sum_e", [P, NT], F32)
    prob_1 = sb("prob_1", [P, NT], F32)
    prob_2 = sb("prob_2", [P, NT], F32)
    rank = sb("rank", [P, NT, NE], F32)
    kept = sb("kept", [P, NT, NE], F32)
    carry = sb("carry", [P, 2, NE], F32)
    gate = sb("gate", [P, NT], F32)
    hid = sb("hid", [P, NF, LP], F32)
    y_b = sb("y_b", [P, NT, P], F32)
    y_g = sb("y_g", [P, NT, P], F32)
    y_out = sb("y_out", [P, NT, P], F32)

    slots = ctx.enter_context(nc.psum_tensor("slots", [P, 4, 1024], F32))

    setup = sem("g_setup")
    N_SETUP = 8

    S = {n: sem("g_" + n) for n in (
        "x_nx2T", "x_qk", "x_part_a", "x_left",
        "x_part_b", "x_rep", "x_val", "x_gel", "x_vals", "x_loc", "x_gel_l", "x_localT",
        "y_sc", "y_max", "y_hi", "y_split", "y_turned_max", "y_maxT", "y_rows", "y_st", "y_raw", "y_p", "y_att",
        "y_inv", "y_norm", "y_turned", "y_attT", "y_proj", "y_h2",
        "z_stat", "z_agg", "z_pool", "z_nx3", "z_turned", "z_nx3T", "z_logit", "z_lg", "z_top", "z_topi", "z_topf",
        "z_is", "z_d", "z_e", "z_sum", "z_p1", "z_p2", "z_w", "z_chosen", "z_weights", "z_ranked", "z_rank",
        "z_kept", "z_gate", "z_f1", "z_hid", "z_f2", "z_yb", "z_yg", "z_out", "z_stored")} | G["S"]

    block = ctx.enter_context(nc.Block())

    def run(eng, body):
        body(-1, (True, False, False))
        body(0, (True, True, False))
        body(1, (True, True, True))
        with eng.Fori(2, B - 1) as r:
            body(r, (True, True, True))
        body(B - 1, (False, True, True))
        body(B, (False, False, True))

    def wait_apart(eng, sem, value):
        if not isinstance(value, int):
            value = eng.to_reg(value)
            eng.wait_ge(loaded, 16 * 8)
        eng.wait_ge(sem, value)

    def first(it, at):
        return isinstance(it, int) and it <= at

    @block.sync
    def _(sp):
        def body(it, stages):
            _, y, z = stages
            if y:
                wait_apart(sp, S["y_maxT"], it + 1)
                for j in range(2):
                    sp.dma_start(qk_rep[KS + j:KS + j + 1, 0, :], nmax_T[j * NT:(j + 1) * NT, :]).then_inc(S["y_rows"], 16)
            if z:
                wait_apart(sp, S["z_out"], it)
                sp.dma_start(out[bass.ds(it - 1, 1), 0:(NT - 1) * P, :].rearrange("b (t p) c -> p (b t) c", p=P),
                             y_out[:, 0:NT - 1, :]).then_inc(S["z_stored"], 16)
                sp.dma_start(out[bass.ds(it - 1, 1), (NT - 1) * P:L, :].rearrange("b p c -> p (b c)"),
                             y_out[0:REST, NT - 1, :]).then_inc(S["z_stored"], 16)

        run(sp, body)
        sp.wait_ge(S["z_stored"], 32 * B)

    @block.gpsimd
    def _(pool):
        count = [0]

        def step(ins):
            count[0] += 1
            ins.then_inc(setup, 1)
            pool.wait_ge(setup, count[0])

        step(pool.memset(carry[:, :, :], 0.0))
        step(pool.memset(nmax_parts[:, :], 0.0))
        step(pool.memset(qk_rep[KS:KM, 1, :], 1.0))
        step(pool.memset(vals[:, :, P:P + 1], 1.0))
        step(pool.memset(p_T[:, :], 1.0))
        step(pool.memset(localT[:, L:LP], 0.0))
        step(pool.memset(hid[:, :, L:LP], 0.0))
        step(pool.memset(nmax[:, :], 0.0))
        assert count[0] == N_SETUP

        def chain(sem, per, n, k, ins):
            ins.then_inc(sem, 1)
            wait_apart(pool, sem, n * per + k + 1)

        def body(it, stages):
            x, y, z = stages
            if z:
                n = it - 1
                wait_apart(pool, S["z_agg"], n * NT + NT)
                if not first(it, 1):
                    wait_apart(pool, S["z_nx3"], n)
                chain(S["z_pool"], 4, n, 0, pool.tensor_scalar(rs["z"][:, :], mv3[:, :, 1], EPS, None, ALU.add))
                chain(S["z_pool"], 4, n, 1, pool.tensor_tensor(rs["zr"][:, :], rs["z"][:, :], half_neg[:, :], ALU.pow))
                chain(S["z_pool"], 4, n, 2, pool.tensor_scalar(rs["z"][:, :], mv3[:, :, 0], -1.0, None, ALU.mult))
                pool.tensor_tensor(rs["znmr"][:, :], rs["z"][:, :], rs["zr"][:, :], ALU.mult).then_inc(S["z_pool"], 1)
            if x and not first(it, -1):
                G["scales"](pool, it + 1, wait_apart)
            if z:
                n = it - 1
                wait_apart(pool, S["z_top"], n * NT + NT)
                if not first(it, 1):
                    wait_apart(pool, S["z_e"], n)
                pool.tensor_tensor(lg_d[:, :, 0:NE], lg[:, :, :], top[:, :, 0:1].broadcast_to([P, NT, NE]),
                                   ALU.subtract).then_inc(S["z_d"], 1)
                pool.tensor_tensor(lg_d[:, :, NE:NE + 1], top[:, :, 1:2], top[:, :, 0:1], ALU.subtract).then_inc(S["z_d"], 1)
                wait_apart(pool, S["z_is"], n * 2 + 2)
                if not first(it, 1):
                    wait_apart(pool, S["z_ranked"], n)
                pool.tensor_tensor(chosen[:, :, :], is_1[:, :, :], is_2[:, :, :], ALU.add).then_inc(S["z_chosen"], 1)
            if y:
                if first(it, 0):
                    pool.wait_ge(biased, 4)
                for k in range(NT):
                    w = L - P * k
                    wait_apart(pool, S["y_raw"], it * NT + k + 1)
                    if k == 0 and not first(it, 0):
                        wait_apart(pool, S["y_att"], it)
                    pool.tensor_tensor(p_T[0:rows(k), p_off[k]:p_off[k] + w], p_raw[0:rows(k), k % 2, 0:w],
                                       bias_fac[0:rows(k), 0:w], ALU.mult).then_inc(S["y_p"], 1)
            if z:
                n = it - 1
                wait_apart(pool, S["z_p1"], n + 1)
                pool.tensor_tensor(prob_2[:, :], lg_e[:, :, NE], prob_1[:, :], ALU.mult).then_inc(S["z_p2"], 1)
                pool.tensor_tensor(is_1[:, :, :], is_1[:, :, :], prob_1[:, :].unsqueeze(2).broadcast_to([P, NT, NE]),
                                   ALU.mult).then_inc(S["z_w"], 1)
                wait_apart(pool, S["z_p2"], n + 1)
                pool.tensor_tensor(is_2[:, :, :], is_2[:, :, :], prob_2[:, :].unsqueeze(2).broadcast_to([P, NT, NE]),
                                   ALU.mult).then_inc(S["z_w"], 1)
                wait_apart(pool, S["z_w"], n * 2 + 2)
                pool.tensor_tensor(is_1[:, :, :], is_1[:, :, :], is_2[:, :, :], ALU.add).then_inc(S["z_weights"], 1)
                wait_apart(pool, S["z_gate"], n + 1)
                wait_apart(pool, S["z_yb"], n + 1)
                pool.tensor_tensor(y_g[:, :, :], y_b[:, :, :], gate[:, :].unsqueeze(2).broadcast_to([P, NT, P]),
                                   ALU.mult).then_inc(S["z_yg"], 1)
                wait_apart(pool, S["z_yg"], n + 1)
                if not first(it, 1):
                    wait_apart(pool, S["z_stored"], n * 32)
                pool.tensor_tensor(y_out[:, :, :], y_g[:, :, :], h2[:, :, :], ALU.add).then_inc(S["z_out"], 1)
            if x and not first(it, -1):
                if y:
                    wait_apart(pool, S["y_h2"], it + 1)
                G["residual"](pool, it + 1)

        run(pool, body)

    @block.scalar
    def _(act):
        act.wait_ge(loaded, 16 * 8)

        def body(it, stages):
            x, y, z = stages
            if z:
                n = it - 1
                act.wait_ge(S["z_turned"], n + 1)
                if not first(it, 1):
                    act.wait_ge(S["z_f1"], n * NF)
                act.copy(nx3T[:, :], slots[:, SLOT["turn3", 0], 0:LP]).then_inc(S["z_nx3T"], 1)
                for f in range(NF):
                    act.wait_ge(S["z_f1"], n * NF + f + 1)
                    if f == 0 and not first(it, 1):
                        act.wait_ge(S["z_f2"], n)
                    act.activation(hid[:, f, 0:L].rearrange("p (a l) -> p a l", a=2),
                                   slots[:, SLOT["ffn1", f], :].rearrange("p (a l) -> p a l", a=2)[:, :, 0:HALF],
                                   ACT.Gelu, bias=b1_col[:, f:f + 1]).then_inc(S["z_hid"], 1)
                    if y and f == 1:
                        maxima(it)
            elif y:
                maxima(it)
            if y:
                if first(it, 0):
                    bias_exp(act, 1)
                for k in range(NT):
                    w = L - P * k
                    act.wait_ge(S["y_st"], it * NT + k + 1)
                    if k >= 2:
                        act.wait_ge(S["y_p"], it * NT + k - 1)
                    act.activation(p_raw[0:rows(k), k % 2, 0:w], slots[0:rows(k), SLOT["scores_T", k], 0:w], ACT.Exp,
                                   scale=QK ** -0.5).then_inc(S["y_raw"], 1)
            if z:
                n = it - 1
                act.wait_ge(S["z_d"], n * 2 + 2)
                if not first(it, 1):
                    act.wait_ge(S["z_p2"], n)
                act.activation(lg_e[:, :, :], lg_d[:, :, :], ACT.Exp).then_inc(S["z_e"], 1)
            if x:
                n = it + 1
                act.wait_ge(S["x_turned"], n + 1)
                act.copy(nx2T[:, :], slots[:, SLOT["turn2", 0], 0:LP]).then_inc(S["x_nx2T"], 1)
            if y:
                act.wait_ge(S["y_turned"], it + 1)
                act.copy(attT[:, :], slots[:, SLOT["turn_att", 0], 0:LP]).then_inc(S["y_attT"], 1)
            if x:
                n = it + 1
                for j in range(2):
                    act.wait_ge(S["x_qk"], n * 2 + j + 1)
                    if n_prev(it, j):
                        act.wait_ge(S["x_rep"], n * 2 + j)
                    act.copy(part_a[:, :].rearrange("p (a l) -> p a l", a=2),
                             slots[0:KS, SLOT["qk", j], :].rearrange("p (a l) -> p a l", a=2)[:, :, 0:HALF]).then_inc(S["x_part_a"], 1)
                    act.wait_ge(S["x_left"], n * 2 + j + 1)
                    act.copy(part_b[:, :], left_a[:, :]).then_inc(S["x_part_b"], 1)
                for j, (t0, nt) in enumerate(((0, 4), (4, 2))):
                    act.wait_ge(S["x_val"], n * 2 + j + 1)
                    if n_prev(it, j):
                        act.wait_ge(S["x_vals"], n * 2 + j)
                    act.activation(gel[:, 0:nt, :], slots[:, SLOT["values", j], 0:nt * E2].rearrange("p (t c) -> p t c", c=E2)[:, :, P:E2],
                                   ACT.Gelu).then_inc(S["x_gel"], 1)
                for j in range(2):
                    act.wait_ge(S["x_loc"], n * 2 + j + 1)
                    if n_prev(it, j):
                        act.wait_ge(S["x_localT"], n * 2 + j)
                    act.activation(gel_l[:, :], slots[:, SLOT["local", j], 512:512 + HALF], ACT.Gelu).then_inc(S["x_gel_l"], 1)

        def n_prev(it, j):
            return j or not first(it, -1)

        def maxima(it):
            act.wait_ge(S["y_turned_max"], it + 1)
            if not first(it, 0):
                act.wait_ge(S["y_rows"], it * 32)
            act.copy(nmax_T[:, :], slots[0:2 * NT, SLOT["turn_max", 0], 0:P // 2].bitcast(BF16)).then_inc(S["y_maxT"], 1)

        run(act, body)

    @block.vector
    def _(dve):
        def body(it, stages):
            x, y, z = stages
            if y and first(it, 0):
                dve.wait_ge(setup, N_SETUP)
            if z:
                n = it - 1
                dve.wait_ge(S["y_h2"], n + 1)
                for t in range(NT):
                    dve.bn_stats(st3[:, t, :], h2[:, t, :]).then_inc(S["z_stat"], 1)
                wait_apart(dve, S["z_stat"], n * NT + NT)
                for t in range(NT):
                    dve.bn_aggr(mv3[:, t, :], st3[:, t, :]).then_inc(S["z_agg"], 1)
            if x and not first(it, -1):
                G["statistics"](dve, it + 1, wait_apart)

            def maxima(t):
                dve.wait_ge(S["y_sc"], it * NT + t + 1)
                dve.tensor_reduce(nmax[0:rows(t), t:t + 1], slots[0:rows(t), SLOT["scores", t], 0:min(P * (t + 1), L)],
                                  AX.X, ALU.max, negate=True).then_inc(S["y_max"], 1)

            if y:
                for t in range(3):
                    maxima(t)
            if z:
                n = it - 1
                dve.wait_ge(S["z_pool"], n * 4 + 4)
                if not first(it, 1):
                    dve.wait_ge(S["z_turned"], n)
                for t in range(NT):
                    last = dve.tensor_scalar(nx3[:, t, :], h2[:, t, :], rs["zr"][:, t:t + 1], rs["znmr"][:, t:t + 1], ALU.mult, ALU.add)
                last.then_inc(S["z_nx3"], 1)
            if x and not first(it, -1):
                G["normalise"](dve, it + 1)
            if y:
                for t in range(3, NT):
                    maxima(t)
                dve.wait_ge(S["y_max"], it * NT + NT)
                if not first(it, 0):
                    dve.wait_ge(S["y_turned_max"], it)
                dve.tensor_copy(nmax_parts[:, 0:NT], nmax[:, :]).then_inc(S["y_hi"], 1)
                dve.wait_ge(S["y_hi"], it + 1)
                dve.tensor_tensor(nmax_parts[:, NT:2 * NT], nmax[:, :], nmax_parts[:, 0:NT], ALU.subtract).then_inc(S["y_split"], 1)
            if z:
                n = it - 1
                dve.wait_ge(S["z_logit"], n + 1)
                if not first(it, 1):
                    dve.wait_ge(S["z_d"], n * 2)
                dve.tensor_copy(lg[:, :, :], slots[:, SLOT["logits", 0], 0:NT * NE].rearrange("p (t e) -> p t e", e=NE)).then_inc(S["z_lg"], 1)
                wait_apart(dve, S["z_lg"], n + 1)
                for t in range(NT):
                    dve.max(top[:, t, :], lg[:, t, :]).then_inc(S["z_top"], 1)
                wait_apart(dve, S["z_top"], n * NT + NT)
                for t in range(NT):
                    last = dve.max_index(top_i[:, t, :], top[:, t, :], lg[:, t, :])
                last.then_inc(S["z_topi"], 1)
                dve.wait_ge(S["z_topi"], n + 1)
                dve.tensor_copy(top_f[:, :, :], top_i[:, :, 0:2]).then_inc(S["z_topf"], 1)
                dve.wait_ge(S["z_topf"], n + 1)
                if not first(it, 1):
                    dve.wait_ge(S["z_kept"], n)
                for j, onehot in enumerate((is_1, is_2)):
                    dve.tensor_tensor(onehot[:, :, :], expert[:, :].unsqueeze(1).broadcast_to([P, NT, NE]),
                                      top_f[:, :, j:j + 1].broadcast_to([P, NT, NE]), ALU.is_equal).then_inc(S["z_is"], 1)
                dve.wait_ge(S["z_e"], n + 1)
                dve.tensor_reduce(sum_e[:, :], lg_e[:, :, 0:NE], AX.X, ALU.add).then_inc(S["z_sum"], 1)
                dve.wait_ge(S["z_sum"], n + 1)
                if not first(it, 1):
                    dve.wait_ge(S["z_w"], n * 2)
                dve.reciprocal(prob_1[:, :], sum_e[:, :]).then_inc(S["z_p1"], 1)
                dve.wait_ge(S["z_ranked"], n + 1)
                dve.tensor_tensor(rank[:, :, :], slots[:, SLOT["ranks", 0], 0:NT * NE].rearrange("p (t e) -> p t e", e=NE),
                                  carry[:, 0, :].unsqueeze(1).broadcast_to([P, NT, NE]), ALU.add).then_inc(S["z_rank"], 1)
                dve.tensor_tensor(carry[:, 1, :], carry[:, 0, :], slots[:, SLOT["ranks", 0], 512:512 + NE], ALU.add).then_inc(S["z_rank"], 1)
                dve.wait_ge(S["z_rank"], n * 3 + 2)
                dve.tensor_copy(carry[:, 0, :], carry[:, 1, :]).then_inc(S["z_rank"], 1)
                dve.wait_ge(S["z_weights"], n + 1)
                dve.scalar_tensor_tensor(kept[:, :, :], rank[:, :, :], float(CAP), is_1[:, :, :], ALU.is_lt, ALU.mult).then_inc(S["z_kept"], 1)
                dve.wait_ge(S["z_kept"], n + 1)
                if not first(it, 1):
                    dve.wait_ge(S["z_yg"], n)
                dve.tensor_reduce(gate[:, :], kept[:, :, :], AX.X, ALU.add).then_inc(S["z_gate"], 1)
                dve.wait_ge(S["z_f2"], n + 1)
                dve.tensor_tensor(y_b[:, :, :], slots[:, SLOT["ffn2", 0], 0:NT * P].rearrange("p (t c) -> p t c", c=P),
                                  b2_row[:, :].unsqueeze(1).broadcast_to([P, NT, P]), ALU.add).then_inc(S["z_yb"], 1)
            if y:
                dve.wait_ge(S["y_att"], it + 1)
                o = slots[:, SLOT["attend", 0], :].rearrange("p (a l) -> p a l", a=2)[:, :, 0:3 * (P + 1)].rearrange("p a (t c) -> p a t c", c=P + 1)
                dve.reciprocal(inv[:, :].rearrange("p (a t) -> p a t", a=2), o[:, :, :, P]).then_inc(S["y_inv"], 1)
                dve.wait_ge(S["y_inv"], it + 1)
                if not first(it, 0):
                    dve.wait_ge(S["y_turned"], it)
                for a in range(2):
                    last = dve.tensor_tensor(att[:, 3 * a:3 * a + 3, :], o[:, a, :, 0:P],
                                             inv[:, 3 * a:3 * a + 3].unsqueeze(2).broadcast_to([P, 3, P]), ALU.mult)
                last.then_inc(S["y_norm"], 1)

            def split(j):
                n = it + 1
                z_ps = slots[0:KS, SLOT["qk", j], :].rearrange("p (a l) -> p a l", a=2)[:, :, 0:HALF]
                dve.wait_ge(S["x_part_a"], n * 2 + j + 1)
                dve.scalar_tensor_tensor(left_a[:, :].rearrange("p (a l) -> p a l", a=2), part_a[:, :].rearrange("p (a l) -> p a l", a=2),
                                         take_out[:, j, 0:1], z_ps, ALU.mult, ALU.add).then_inc(S["x_left"], 1)
                dve.wait_ge(S["x_part_b"], n * 2 + j + 1)
                dve.scalar_tensor_tensor(qk_rep[0:KS, j, 0:L], part_b[:, :], take_out[:, j, 1:2], left_a[:, :],
                                         ALU.mult, ALU.add).then_inc(S["x_rep"], 1)

            if x:
                split(0)
                split(1)
            if y:
                dve.wait_ge(S["y_proj"], it + 1)
                dve.wait_ge(S["x_hn"], it + 1)
                if z:
                    dve.wait_ge(S["z_out"], it)
                dve.tensor_tensor(h2[:, :, :], slots[:, SLOT["project", 0], 0:NT * P].rearrange("p (t c) -> p t c", c=P), hn[:, :, :],
                                  ALU.add).then_inc(S["y_h2"], 1)
            if x:
                n = it + 1
                for j, (t0, nt) in enumerate(((0, 4), (4, 2))):
                    dve.wait_ge(S["x_gel"], n * 2 + j + 1)
                    dve.tensor_tensor(vals[:, t0:t0 + nt, 0:P], slots[:, SLOT["values", j], 0:nt * E2].rearrange("p (t c) -> p t c", c=E2)[:, :, 0:P],
                                      gel[:, 0:nt, :], ALU.mult).then_inc(S["x_vals"], 1)
                for j in range(2):
                    dve.wait_ge(S["x_gel_l"], n * 2 + j + 1)
                    dve.tensor_tensor(localT[:, HALF * j:HALF * j + HALF], slots[:, SLOT["local", j], 0:HALF], gel_l[:, :],
                                      ALU.mult).then_inc(S["x_localT"], 1)

        run(dve, body)

    @block.tensor
    def _(pe):
        pe.wait_ge(loaded, 16 * 8)
        pe.wait_ge(by_term, 2)
        tenants = {}

        def body(it, stages):
            x, y, z = stages
            if y and first(it, 0):
                pe.wait_ge(setup, N_SETUP)
            if not first(it, 0) and not (isinstance(it, int) and it > B - 1):
                for place, reader, value in ((("values", 0), "x_vals", it * 2 + 1), (("values", 1), "x_vals", it * 2 + 2),
                                             (("local", 0), "x_localT", it * 2 + 1), (("local", 1), "x_localT", it * 2 + 2)):
                    tenants[SLOT[place]] = (S[reader], value)

            def take(name, i, reader, value):
                k = SLOT[name, i]
                if k in tenants:
                    pe.wait_ge(*tenants[k])
                tenants[k] = (S[reader], value)
                return slots[:, k, :]

            def pieces(lo, hi):
                return [(a, min(b, hi)) for a, b in ((lo, 512), (512, 1024)) if a < min(b, hi)] if lo < 512 else [(lo, hi)]

            def turn(slot, src):
                for t in range(NT):
                    last = pe.transpose(slot[:, t * P:(t + 1) * P], src[:, t, :], ident[:, :])
                return last

            def ffn1(f):
                n = it - 1
                o = take("ffn1", f, "z_hid", n * NF + f + 1)
                for h in range(2):
                    last = pe.matmul(o[:, 512 * h:512 * h + HALF], w1_sb[:, f * P:(f + 1) * P], nx3T[:, h * HALF:(h + 1) * HALF],
                                     start=True, stop=True)
                last.then_inc(S["z_f1"], 1)

            if y:
                for t in range(NT):
                    o = take("scores", t, "y_max", it * NT + t + 1)
                    if t == 0:
                        pe.wait_ge(S["x_rep"], it * 2 + 2)
                    w = min(P * (t + 1), L)
                    for a, b in pieces(0, w):
                        diag = b == w
                        last = pe.matmul(o[0:rows(t), a:b], qk_rep[0:KS, 0, t * P:t * P + rows(t)], qk_rep[0:KS, 1, a:b],
                                         start=True, stop=not diag)
                        if diag:
                            last = pe.matmul(o[0:rows(t), t * P:w], ident_bf[0:rows(t), 0:rows(t)], mask_q[0:rows(t), 0:rows(t)],
                                             start=False, stop=True)
                    last.then_inc(S["y_sc"], 1)
            if z:
                n = it - 1
                o = take("turn3", 0, "z_nx3T", n + 1)
                pe.wait_ge(S["z_nx3"], n + 1)
                turn(o, nx3).then_inc(S["z_turned"], 1)
                o = take("logits", 0, "z_lg", n + 1)
                pe.wait_ge(S["z_nx3T"], n + 1)
                for t in range(NT):
                    last = pe.matmul(o[:, t * NE:(t + 1) * NE], nx3T[:, t * P:(t + 1) * P], router_sb[:, :], start=True, stop=True)
                last.then_inc(S["z_logit"], 1)
                ffn1(0)
                ffn1(1)
            if y:
                o = take("turn_max", 0, "y_maxT", it + 1)
                pe.wait_ge(S["y_split"], it + 1)
                pe.transpose(o[:, 0:P // 2].bitcast(BF16), nmax_parts[:, :], ident_bf[:, :]).then_inc(S["y_turned_max"], 1)
            if z:
                ffn1(2)
                ffn1(3)
            if y:
                for k in range(NT):
                    o = take("scores_T", k, "y_raw", it * NT + k + 1)
                    if k == 0:
                        pe.wait_ge(S["y_rows"], it * 32 + 32)
                    w = L - P * k
                    for a, b in pieces(0, w):
                        diag = a == 0
                        last = pe.matmul(o[0:rows(k), a:b], qk_rep[0:KM, 1, k * P:k * P + rows(k)], qk_rep[0:KM, 0, k * P + a:k * P + b],
                                         start=True, stop=not diag)
                        if diag:
                            last = pe.matmul(o[0:rows(k), 0:rows(k)], ident_bf[0:rows(k), 0:rows(k)], mask_k[0:rows(k), 0:rows(k)],
                                             start=False, stop=True)
                    last.then_inc(S["y_st"], 1)
            if z:
                n = it - 1
                o = take("ranks", 0, "z_rank", n * 3 + 2)
                pe.wait_ge(S["z_chosen"], n + 1)
                for t in range(NT):
                    for u in range(t + 1):
                        last = pe.matmul(o[:, t * NE:(t + 1) * NE], (before_bf if u == t else ones_bf)[0:rows(u), :],
                                         chosen[0:rows(u), u, :], start=(u == 0), stop=(u == t))
                for u in range(NT):
                    last = pe.matmul(o[:, 512:512 + NE], ones_bf[0:rows(u), :], chosen[0:rows(u), u, :], start=(u == 0), stop=(u == NT - 1))
                last.then_inc(S["z_ranked"], 1)
                o = take("ffn2", 0, "z_yb", n + 1)
                pe.wait_ge(S["z_hid"], n * NF + NF)
                for t in range(NT):
                    for f in range(NF):
                        last = pe.matmul(o[:, t * P:(t + 1) * P], hid[:, f, (t * P):(t + 1) * P], w2_sb[:, f, :],
                                         start=(f == 0), stop=(f == NF - 1))
                last.then_inc(S["z_f2"], 1)
            if y:
                o = take("attend", 0, "y_norm", it + 1)
                pe.wait_ge(S["x_vals"], it * 2 + 2)
                pe.wait_ge(S["y_p"], it * NT + NT)
                for t in range(NT):
                    c = 512 * (t // 3) + (P + 1) * (t % 3)
                    for k in range(t + 1):
                        q = p_off[k] + P * (t - k)
                        last = pe.matmul(o[:, c:c + P + 1], p_T[0:rows(k), q:q + P], vals[0:rows(k), k, :],
                                         start=(k == 0), stop=(k == t))
                last.then_inc(S["y_att"], 1)
            if x:
                n = it + 1
                o = take("turn2", 0, "x_nx2T", n + 1)
                pe.wait_ge(S["x_nx2"], n + 1)
                turn(o, nx2).then_inc(S["x_turned"], 1)
            if y:
                o = take("turn_att", 0, "y_attT", it + 1)
                pe.wait_ge(S["y_norm"], it + 1)
                turn(o, att).then_inc(S["y_turned"], 1)
            if x:
                for j in range(2):
                    o = take("qk", j, "x_left", n * 2 + j + 1)
                    if j == 0:
                        pe.wait_ge(S["x_nx2T"], n + 1)
                    for h in range(2):
                        last = pe.matmul(o[0:KS, 512 * h:512 * h + HALF], qk_w[:, j, :, :].rearrange("p a c -> p (a c)"),
                                         nx2T[:, h * HALF:(h + 1) * HALF], start=True, stop=True)
                    last.then_inc(S["x_qk"], 1)
            if y:
                o = take("project", 0, "y_h2", it + 1)
                pe.wait_ge(S["y_attT"], it + 1)
                pe.wait_ge(S["x_localT"], it * 2 + 2)
                for t in range(NT):
                    for a, src in enumerate((localT, attT)):
                        last = pe.matmul(o[:, t * P:(t + 1) * P], src[:, t * P:(t + 1) * P], project_sb[:, a, :],
                                         start=(a == 0), stop=(a == 1))
                last.then_inc(S["y_proj"], 1)
            if x:
                for j, (t0, nt) in enumerate(((0, 4), (4, 2))):
                    o = take("values", j, "x_vals", n * 2 + j + 1)
                    for t in range(t0, t0 + nt):
                        c = (t - t0) * E2
                        last = pe.matmul(o[:, c:c + E2].rearrange("p (a c) -> p a c", a=2), nx2T[:, t * P:(t + 1) * P],
                                         expand_sb[:, 2 * QK:2 * QK + 2 * E2].rearrange("p (a c) -> p a c", a=2)[:, :, P:E2],
                                         start=True, stop=True)
                    last.then_inc(S["x_val"], 1)
                for j in range(2):
                    o = take("local", j, "x_localT", n * 2 + j + 1)
                    for a in range(2):
                        c = 2 * QK + a * E2
                        last = pe.matmul(o[:, 512 * a:512 * a + HALF], expand_sb[:, c:c + P], nx2T[:, j * HALF:(j + 1) * HALF],
                                         start=True, stop=True)
                    last.then_inc(S["x_loc"], 1)

        run(pe, body)


def build(nc, x, wq, wk, wv, bq, bk, bv, expand, project, pos_mult, router_T, w1_T, b1, w2_T, b2, out):
    with ExitStack() as whole:
        hall = whole.enter_context(nc.sbuf_tensor("hall", [P, B * LP], F32))
        ahead = gated_ahead(nc, whole, hall, expand, project, pos_mult, router_T, w1_T, b1, w2_T, b2)
        with ExitStack() as ctx:
            token_attention(nc, ctx, hall, ahead, x, wq, wk, wv, bq, bk, bv)
        with ExitStack() as ctx:
            gated_units(nc, ctx, ahead, hall, out)


def kernel(**inputs):
    import numpy as np
    import concourse.bacc as bacc
    from concourse.bass_utils import run_bass_kernel_spmd

    def plain(name):
        return np.ascontiguousarray(inputs[name])

    nc = bacc.Bacc("TRN2", target_bir_lowering=False, num_devices=1)
    arrays = {
        "x": plain("x"),
        "wq": plain("L0_tok_WQ"), "wk": plain("L0_tok_WK"), "wv": plain("L0_tok_WV"),
        "bq": plain("L0_tok_BQ"), "bk": plain("L0_tok_BK"), "bv": plain("L0_tok_BV"),
        "expand": plain("L0_attn_expand"), "project": plain("L0_attn_project"),
        "pos_mult": plain("L0_attn_position_bias_mult").reshape(1),
        "router_T": np.ascontiguousarray(plain("L0_ffn_router_w").T),
        "w1_T": np.ascontiguousarray(plain("L0_ffn_w1").T),
        "b1": np.ascontiguousarray(plain("L0_ffn_b1").reshape(NF, P).T),
        "w2_T": np.ascontiguousarray(plain("L0_ffn_w2").T),
        "b2": plain("L0_ffn_b2"),
    }
    arrays = {"in_" + n: a for n, a in arrays.items()}
    args = [nc.dram_tensor(n, a.shape, mybir.dt.from_np(a.dtype), kind="ExternalInput").ap() for n, a in arrays.items()]
    args.append(nc.dram_tensor("out_h", (B, L, P), F32, kind="ExternalOutput").ap())
    build(nc, *args)
    return run_bass_kernel_spmd(nc, [arrays], core_ids=[0]).results[0]["out_h"]
```

```python
from contextlib import ExitStack

import concourse.bass as bass
from concourse import mybir

F32 = mybir.dt.float32
BF16 = mybir.dt.bfloat16
U32 = mybir.dt.uint32
ALU = mybir.AluOpType
ACT = mybir.ActivationFunctionType
AX = mybir.AxisListType

P = 128
B, LX = 8, 750
TAPS = 3
L = LX - TAPS + 1
NT = -(-L // P)
LP = NT * P
REST = L - (NT - 1) * P
XREST = LX - (NT - 1) * P
HALF = L // 2
QTR = L // 4
NH, DH = 8, 16
GH = 4
NG = NH // GH
KS = 6 * DH
KM = KS + 2
STEPS = NG * 2 * NT
LAG = 15
RING = 12


def rows(t):
    return P if t < NT - 1 else REST


def token_attention(nc, ctx, hall, ahead, x, wq, wk, wv, bq, bk, bv):
    def sb(name, shape, dt):
        return ctx.enter_context(nc.sbuf_tensor(name, shape, dt))

    def psum(name, shape, dt):
        return ctx.enter_context(nc.psum_tensor(name, shape, dt))

    def sem(name):
        return ctx.enter_context(nc.semaphore(name))

    w_sb = {n: sb("w_" + n, [P, TAPS, P], F32) for n in "qkv"}
    b_col = {n: sb("b_" + n, [P, 1], F32) for n in "qk"}
    bv_row = sb("bv_row", [P, P], F32)
    ident = sb("ident", [P, P], F32)
    ident_bf = sb("ident_bf", [P, P], BF16)
    warm = sb("warm", [P, 1], F32)
    x_in = sb("x_in", [P, NT, P], F32)
    xT = sb("xT", [P, 2, LX + 2], F32)
    elu_exp = sb("elu_exp", [P, 2, HALF], F32)
    elu_neg = sb("elu_neg", [P, 2, HALF], F32)
    elu_out = sb("elu_out", [P, 2, HALF], F32)
    resid = sb("resid", [P, 2, HALF], F32)
    parts = {n: sb("parts_" + n, [P, 3, LP], BF16) for n in "qk"}
    q_rep = sb("q_rep", [KM, 2, NH, LP], BF16)
    k_rep = sb("k_rep", [KM, 2, NH, LP], BF16)
    v_z = sb("v_z", [P, 4 * P], F32)
    v_exp = sb("v_exp", [P, 4 * P], F32)
    v_neg = sb("v_neg", [P, 4 * P], F32)
    v_hat = sb("v_hat", [P, 2, NT * NH, 32], F32)
    probs = sb("probs", [P, RING, HALF], F32)
    out_T = sb("out_T", [P, NG, LP], F32)
    inv_sum = sb("inv_sum", [P, 2, 4 * GH], F32)
    neg_max = sb("neg_max", [P, NH * NT], F32)
    max_parts = sb("max_parts", [P, P], BF16)
    max_T = sb("max_T", [2 * GH * NT, P], BF16)

    ps_max = psum("ps_max", [P, 2, 2, 512], F32)
    ps_st = psum("ps_st", [P, 2, 512], F32)
    ps_pv = psum("ps_pv", [P, 512], F32)
    ps_misc = psum("ps_misc", [P, 512], F32)

    scratch = {n: nc.dram_tensor("scratch_" + n, (3, DH, NH, LP), BF16, kind="Internal").ap() for n in "qk"}

    loaded = sem("a_loaded")
    ident_set = sem("a_ident_set")
    ones_set = sem("a_ones_set")
    padded = sem("a_padded")
    x_loaded = sem("a_x_loaded")
    x_turned = sem("a_x_turned")
    xT_ready = sem("a_xT_ready")
    qk_full = sem("a_qk_full")
    qk_exp = sem("a_qk_exp")
    qk_neg = sem("a_qk_neg")
    qk_elu = sem("a_qk_elu")
    part_1 = sem("a_part_1")
    qk_resid = sem("a_qk_resid")
    part_2 = sem("a_part_2")
    qk_split = sem("a_qk_split")
    ident_steps = sem("a_ident_steps")
    scr_done = {n: sem("a_scr_done_" + n) for n in "qk"}
    rep_done = [sem(f"a_rep_done{g}") for g in range(NG)]
    sc_full = sem("b_sc_full")
    sc_max = sem("b_sc_max")
    mx_hi = sem("b_mx_hi")
    mx_split = sem("b_mx_split")
    mx_turned = sem("b_mx_turned")
    mx_copied = sem("b_mx_copied")
    mx_rows = [sem(f"b_mx_rows{g}") for g in range(NG)]
    v_full = sem("b_v_full")
    v_biased = sem("b_v_biased")
    v_exped = sem("b_v_exped")
    v_negd = sem("b_v_negd")
    v_ready = sem("b_v_ready")
    st_full = sem("c_st_full")
    p_ready = sem("c_p_ready")
    pv_done = sem("c_pv_done")
    pv_copied = sem("c_pv_copied")
    o_turned = sem("c_o_turned")
    o_inv = sem("c_o_inv")
    o_done = sem("c_o_done")

    block = ctx.enter_context(nc.Block())
    PADDED = 7
    LOOP0, LOOPS = 1, 3

    def run(eng, body):
        for it in (-1, 0):
            body(it, it % 2, (True, it >= 0, False))
        with eng.Fori(0, LOOPS) as r:
            for u in range(2):
                body(r * 2 + (LOOP0 + u), (LOOP0 + u) % 2, (True, True, True))
        for it in (B - 1, B):
            body(it, it % 2, (False, it < B, True))

    def probs_step(it, s, stages):
        _, b, b1 = stages
        if s < LAG:
            return (it - 1, s + STEPS - LAG) if b1 else None
        return (it, s - LAG) if b and s < STEPS else None

    def first_of(it):
        return isinstance(it, int) and it < 0

    def last_of(it):
        return isinstance(it, int) and it == B

    def pair_slot(n):
        return (ps_max[:, 0, :, :], ps_max[:, 1, :, :], ps_st[:, :, :])[n // 2 % 3]

    def misc(it, task):
        if not first_of(it):
            return ps_misc
        return ps_max[:, task % 4 // 2, task % 2, :] if task < 6 else ps_st[:, 0, :]

    def wait_apart(eng, sem, value):
        if not isinstance(value, int):
            value = eng.to_reg(value)
            eng.wait_ge(loaded, 16 * 6)
        eng.wait_ge(sem, value)

    @block.sync
    def _(sp):
        sp.dma_start(x_in[:, 0:NT - 1, :], x[0, 0:(NT - 1) * P, :].rearrange("(t p) c -> p t c", p=P)).then_inc(x_loaded, 16)
        sp.dma_start(x_in[0:XREST, NT - 1, :], x[0, (NT - 1) * P:LX, :]).then_inc(x_loaded, 16)
        for n, w in (("q", wq), ("k", wk), ("v", wv)):
            sp.dma_start(w_sb[n][:, :, :], w.rearrange("t i o -> i t o")).then_inc(loaded, 16)
        for n, b in (("q", bq), ("k", bk)):
            sp.dma_start(b_col[n][:, :], b.rearrange("(c o) -> c o", o=1)).then_inc(loaded, 16)
        sp.dma_start(bv_row[:, :], bass.AP(tensor=bv.tensor, offset=0, ap=[[0, P], [1, P]])).then_inc(loaded, 16)

        def replicate(odd, g, names="qk"):
            gs = slice(GH * g, GH * g + GH)
            for n in names:
                rep = {"q": q_rep, "k": k_rep}[n]
                for r0, n_terms in ((0, 3), (3 * DH, 2), (5 * DH, 1)):
                    part = {0: 0, 3 * DH: 1, 5 * DH: 2}[r0] if n == "q" else 0
                    step = 0 if n == "q" else DH * NH * LP
                    src = bass.AP(tensor=scratch[n].tensor, offset=part * DH * NH * LP + GH * g * LP,
                                  ap=[[step, n_terms], [NH * LP, DH], [1, GH * LP]])
                    sp.dma_start(rep[r0:r0 + n_terms * DH, odd, gs, :], src).then_inc(rep_done[g], 16)

        def maxima_rows(it, odd, g):
            wait_apart(sp, mx_copied, it * NG + g + 1)
            for j in range(2):
                sp.dma_start(q_rep[KS + j:KS + j + 1, odd, GH * g:GH * g + GH, :],
                             max_T[j * GH * NT:(j + 1) * GH * NT, :]).then_inc(mx_rows[g], 16)

        def body(it, odd, stages):
            a, b, b1 = stages
            nxt = 1 - odd
            if a and not (isinstance(it, int) and it < 0):
                wait_apart(sp, x_turned, (it + 1) * 2)
                sp.dma_start(x_in[:, 0:NT - 1, :],
                             x[bass.ds(it + 1, 1), 0:(NT - 1) * P, :].rearrange("b (t p) c -> p (b t) c", p=P)).then_inc(x_loaded, 16)
                sp.dma_start(x_in[0:XREST, NT - 1, :],
                             x[bass.ds(it + 1, 1), (NT - 1) * P:LX, :].rearrange("b p c -> p (b c)")).then_inc(x_loaded, 16)
            if b:
                if b1:
                    wait_apart(sp, o_done, it * 4)
                replicate(odd, 1)
            if b1:
                maxima_rows(it - 1, nxt, 1)
            if b:
                maxima_rows(it, odd, 0)
            if a:
                if first_of(it):
                    sp.wait_ge(padded, PADDED)
                for i, n in enumerate("qk"):
                    wait_apart(sp, qk_split, (it + 1) * 4 + 2 * i + 2)
                    if i == 0 and not first_of(it):
                        wait_apart(sp, rep_done[1], (it + 1) * 96)
                    for j in range(3):
                        sp.dma_start(scratch[n][j].rearrange("d h l -> h d l"), parts[n][:, j, :]).then_inc(scr_done[n], 16)
                if b1:
                    wait_apart(sp, p_ready, (it - 1) * 96 + 48)
                for n in "qk":
                    wait_apart(sp, scr_done[n], (it + 1) * 48 + 48)
                    replicate(nxt, 0, n)
            if isinstance(it, int) and it == B - 1:
                ahead["load"](sp)

        run(sp, body)

    @block.gpsimd
    def _(pool):
        pool.memset(ident[:, :], 0.0).then_inc(ident_steps, 1)
        pool.wait_ge(ident_steps, 1)
        pool.affine_select(out=ident[:, :], in_=ident[:, :], compare_op=ALU.not_equal, fill=1.0, base=0,
                           pattern=[[-1, P]], channel_multiplier=1).then_inc(ident_steps, 1)
        pool.wait_ge(ident_steps, 2)
        pool.tensor_copy(ident_bf[:, :], ident[:, :]).then_inc(ident_set, 1)
        pool.wait_ge(ident_set, 1)

        pool.memset(k_rep[KS:KM, :, :, :], 1.0).then_inc(ones_set, 1)
        pool.wait_ge(ones_set, 1)
        ahead["start_scales"](pool)

        def body(it, odd, stages):
            a, b, b1 = stages
            if a:
                for i in range(4):
                    n, hh = "qk"[i // 2], i % 2
                    cols = slice(HALF * hh, HALF * hh + HALF)
                    k = (it + 1) * 4 + i + 1
                    wait_apart(pool, part_1, k)
                    pool.tensor_tensor(resid[:, i % 2, :], elu_out[:, i % 2, :], parts[n][:, 0, cols], ALU.subtract).then_inc(qk_resid, 1)
                    wait_apart(pool, part_2, k)
                    pool.tensor_tensor(parts[n][:, 2, cols], resid[:, i % 2, :], parts[n][:, 1, cols], ALU.subtract).then_inc(qk_split, 1)
                for r, nt in ((0, 4), (1, 2)):
                    wait_apart(pool, v_exped, (it + 1) * 2 + r + 1)
                    if r or not first_of(it):
                        wait_apart(pool, v_ready, (it + 1) * 2 + r)
                    pool.tensor_scalar(v_neg[:, 0:nt * P], v_exp[:, 0:nt * P], 1.0, -1.0, ALU.min, ALU.add).then_inc(v_negd, 1)
            if isinstance(it, int) and it == B - 1:
                ahead["constants"](pool)
            if b and b1:
                ahead["scales"](pool, it - 1, wait_apart)

        run(pool, body)
        ahead["second_norm"](pool, 0, wait_apart)
        ahead["residual"](pool, 0)

    @block.scalar
    def _(act):
        act.wait_ge(ident_set, 1)
        act.activation(warm[:, :], ident[:, 0:1], ACT.Exp)
        act.wait_ge(loaded, 16 * 6)

        def body(it, odd, stages):
            a, b, b1 = stages
            nxt = 1 - odd

            def before(s):
                if a and s in (2, 3):
                    r = s - 2
                    lo, hi = (0, 4 * P) if r == 0 else (4 * P, LX)
                    act.wait_ge(x_turned, (it + 1) * 2 + r + 1)
                    act.copy(xT[:, nxt, lo:hi], misc(it, r)[:, 0:hi - lo]).then_inc(xT_ready, 1)
                if a and s in (4, 6, 8, 10):
                    i = (s - 4) // 2
                    act.wait_ge(qk_full, (it + 1) * 4 + i + 1)
                    if i >= 2 or not first_of(it):
                        act.wait_ge(qk_neg, (it + 1) * 4 + i - 1)
                    act.activation(elu_exp[:, i % 2, :], misc(it, 2 + i)[:, 0:HALF], ACT.Exp,
                                   bias=b_col["qk"[i // 2]][:, 0:1]).then_inc(qk_exp, 1)
                if isinstance(it, int) and it == B and s == 2:
                    ahead["bias_exp"](act, 0)
                if a and s in (6, 8, 10, 12):
                    i = (s - 6) // 2
                    act.wait_ge(qk_elu, (it + 1) * 4 + i + 1)
                    if not first_of(it) and i % 2 == 0:
                        act.wait_ge(scr_done["qk"[i // 2]], (it + 1) * 48)
                    act.copy(parts["qk"[i // 2]][:, 0, HALF * (i % 2):HALF * (i % 2) + HALF], elu_out[:, i % 2, :]).then_inc(part_1, 1)
                if a and s in (7, 9, 11, 13):
                    i = (s - 7) // 2
                    act.wait_ge(qk_resid, (it + 1) * 4 + i + 1)
                    act.copy(parts["qk"[i // 2]][:, 1, HALF * (i % 2):HALF * (i % 2) + HALF], resid[:, i % 2, :]).then_inc(part_2, 1)
                if (b and s == 13) or (b1 and s == 1):
                    g, mb = (0, it) if s == 13 else (1, it - 1)
                    act.wait_ge(mx_turned, mb * NG + g + 1)
                    if g:
                        act.wait_ge(mx_rows[0], mb * 32 + 32)
                    elif b1:
                        act.wait_ge(mx_rows[1], (mb - 1) * 32 + 32)
                    act.copy(max_T[:, :], ps_misc[0:2 * GH * NT, 0:P // 2].bitcast(BF16)).then_inc(mx_copied, 1)
                if a and s in (18, 22):
                    r, nt = ((0, 4), (1, 2))[(s - 18) // 4]
                    act.wait_ge(v_biased, (it + 1) * 2 + r + 1)
                    if r or not first_of(it):
                        act.wait_ge(v_negd, (it + 1) * 2 + r)
                    act.activation(v_exp[:, 0:nt * P], v_z[:, 0:nt * P], ACT.Exp).then_inc(v_exped, 1)

            def copy_outputs(s):
                cs = (s - LAG) % STEPS
                if cs % NT == 1 and (b1 if s <= LAG + 1 else b):
                    cb, i = (it - 1, cs // NT - 1) if s < LAG else (it, cs // NT - 1)
                    if i < 0:
                        cb, i = cb - 1, NG * 2 - 1
                    if isinstance(cb, int) and cb < 0:
                        return
                    act.wait_ge(pv_done, cb * STEPS + NT * i + NT)
                    act.copy(out_T[:, i // 2, HALF * (i % 2):HALF * (i % 2) + HALF], ps_pv[:, 0:HALF]).then_inc(pv_copied, 1)

            for s in range(STEPS):
                before(s)
                c = probs_step(it, s, stages)
                if not c:
                    copy_outputs(s)
                if c:
                    cb, cs = c
                    kt = cs % NT
                    at_once = 2 if last_of(it) else 1
                    for j in range(0, GH, at_once):
                        n = GH * cs + j
                        if j == GH - at_once:
                            copy_outputs(s)
                        act.wait_ge(st_full, cb * 96 + n + at_once)
                        if j == 0 and not (isinstance(cb, int) and cb == 0 and cs < 3):
                            act.wait_ge(pv_done, cb * STEPS + cs - 2)
                        if at_once == 2:
                            act.activation(probs[0:rows(kt), n % RING:n % RING + 2, :], pair_slot(n)[0:rows(kt), :, 0:HALF], ACT.Exp,
                                           scale=DH ** -0.5).then_inc(p_ready, 2)
                        else:
                            act.activation(probs[0:rows(kt), n % RING, :], ps_st[0:rows(kt), n % 2, 0:HALF], ACT.Exp,
                                           scale=DH ** -0.5).then_inc(p_ready, 1)

        run(act, body)

    @block.vector
    def _(dve):
        for n in "qk":
            dve.memset(parts[n][:, :, L:LP], 0.0).then_inc(padded, 1)
        dve.memset(out_T[:, :, L:LP], 1.0).then_inc(padded, 1)
        dve.memset(neg_max[:, :], 0.0).then_inc(padded, 1)
        dve.memset(max_parts[:, :], 0.0).then_inc(padded, 1)
        dve.memset(inv_sum[:, :, :], 1.0).then_inc(o_done, 4)
        dve.memset(v_hat[:, :, :, DH:32], 0.0).then_inc(padded, 1)
        dve.wait_ge(padded, PADDED - 1)
        dve.memset(v_hat[:, :, :, DH:DH + 1], 1.0).then_inc(padded, 1)
        dve.wait_ge(loaded, 16 * 6)

        def body(it, odd, stages):
            a, b, b1 = stages
            nxt = 1 - odd

            def outputs(i, r):
                nt, k = ((4, 2)[r], 2 * i + r)
                dve.wait_ge(o_turned, (it - 1) * 4 + k + 1)
                o = ps_misc[:, 0:nt * P].rearrange("p (n d) -> p n d", d=32)
                dve.reciprocal(inv_sum[:, r, 0:nt * GH], o[:, :, DH]).then_inc(o_inv, 1)
                dve.wait_ge(o_inv, (it - 1) * 4 + k + 1)
                h = hall[:, bass.ds((it - 1) * LP + 4 * r * P, nt * P)].rearrange("p (t c) -> p t c", c=P)
                dve.tensor_tensor(h[:, :, GH * DH * i:GH * DH * (i + 1)].rearrange("p t (n d) -> p t n d", d=DH),
                                  o[:, :, 0:DH].rearrange("p (t n) d -> p t n d", t=nt),
                                  inv_sum[:, r, 0:nt * GH].rearrange("p (t n) -> p t n", t=nt).unsqueeze(3).broadcast_to([P, nt, GH, DH]),
                                  ALU.mult).then_inc(o_done, 1)

            def maxima(mb, g):
                w = GH * NT
                dve.wait_ge(sc_max, mb * 48 + 24 * g + 24)
                if not (isinstance(mb, int) and mb == 0 and g == 0):
                    dve.wait_ge(mx_turned, mb * NG + g)
                dve.tensor_copy(max_parts[:, 0:w], neg_max[:, w * g:w * g + w]).then_inc(mx_hi, 1)
                dve.wait_ge(mx_hi, mb * NG + g + 1)
                dve.tensor_tensor(max_parts[:, w:2 * w], neg_max[:, w * g:w * g + w], max_parts[:, 0:w], ALU.subtract).then_inc(mx_split, 1)

            def before(s):
                if a and s in (5, 7, 9, 11):
                    i = (s - 5) // 2
                    dve.wait_ge(qk_exp, (it + 1) * 4 + i + 1)
                    dve.tensor_scalar(elu_neg[:, i % 2, :], elu_exp[:, i % 2, :], 1.0, -1.0, ALU.min, ALU.add).then_inc(qk_neg, 1)
                    dve.wait_ge(qk_neg, (it + 1) * 4 + i + 1)
                    if i >= 2 or not first_of(it):
                        dve.wait_ge(qk_split, (it + 1) * 4 + i - 1)
                    dve.scalar_tensor_tensor(elu_out[:, i % 2, :], misc(it, 2 + i)[:, 0:HALF], b_col["qk"[i // 2]][:, 0:1],
                                             elu_neg[:, i % 2, :], ALU.add, ALU.max).then_inc(qk_elu, 1)
                if b and s == 12:
                    maxima(it, 0)
                if b1 and s == 0:
                    maxima(it - 1, 1)
                if isinstance(it, int) and it == B and s == 2:
                    ahead["repeat_weights"](dve)
                    ahead["normalise"](dve, 0)
                    ahead["bias_sigmoid"](dve)
                if b1 and s in (15, 16):
                    outputs(0, s - 15)
                if b1 and s in (LAG + 3, LAG + 4):
                    outputs(1, s - LAG - 3)
                if b and b1 and s >= STEPS - 4:
                    if s == STEPS - 4:
                        wait_apart(dve, o_done, it * 4 + 4)
                    ahead["statistics"](dve, it - 1, wait_apart, s - (STEPS - 4))
                if a and s in (19, 23):
                    r, nt = ((0, 4), (1, 2))[(s - 19) // 4]
                    dve.wait_ge(v_negd, (it + 1) * 2 + r + 1)
                    if b1 and r == 0:
                        dve.wait_ge(pv_done, it * STEPS)
                    dve.tensor_tensor(v_hat[:, nxt, 4 * r * NH:(4 * r + nt) * NH, 0:DH],
                                      v_z[:, 0:nt * P].rearrange("p (n d) -> p n d", d=DH),
                                      v_neg[:, 0:nt * P].rearrange("p (n d) -> p n d", d=DH), ALU.max).then_inc(v_ready, 1)
                if a and s in (17, 21):
                    r, nt = ((0, 4), (1, 2))[(s - 17) // 4]
                    dve.wait_ge(v_full, (it + 1) * 2 + r + 1)
                    if r or not first_of(it):
                        dve.wait_ge(v_ready, (it + 1) * 2 + r)
                    dve.tensor_tensor(v_z[:, 0:nt * P].rearrange("p (n d) -> p n d", d=P),
                                      misc(it, 6 + r)[:, 0:nt * P].rearrange("p (n d) -> p n d", d=P),
                                      bv_row[:, :].unsqueeze(1).broadcast_to([P, nt, P]), ALU.add).then_inc(v_biased, 1)

            for s in range(STEPS):
                before(s)
                if b:
                    for n in (2 * s, 2 * s + 1):
                        g, t, j = n // 24, n % 24 // GH, n % GH
                        col = (g * GH + j) * NT + t
                        dve.wait_ge(sc_full, it * 48 + n + 1)
                        dve.tensor_reduce(neg_max[0:rows(t), col:col + 1], ps_max[0:rows(t), n % 2, :, 0:HALF],
                                          AX.XY, ALU.max, negate=True).then_inc(sc_max, 1)

        run(dve, body)

    @block.tensor
    def _(pe):
        pe.wait_ge(ident_set, 1)

        def body(it, odd, stages):
            a, b, b1 = stages
            nxt = 1 - odd
            tenants = {}
            if not (isinstance(it, int) and it <= 0):
                tenants[0] = (v_biased, it * 2 + 2) if a or b else (o_done, it * 4)

            def take(task, reader, value):
                k = (4 if task >= 6 else task % 4) if first_of(it) else 0
                if k in tenants:
                    pe.wait_ge(*tenants[k])
                tenants[k] = (reader, value)
                return misc(it, task)

            def constants():
                pe.wait_ge(padded, PADDED)
                pe.wait_ge(ones_set, 1)
                pe.wait_ge(qk_elu, 4)

            def scores_T(cb, cs, j):
                g, qh, kt = cs // 12, cs % 12 // NT, cs % NT
                n, h = GH * cs + j, GH * g + j
                slot = odd if cb is it else nxt
                out = ps_st[:, n % 2, :]
                if last_of(it):
                    out = pair_slot(n)[:, j % 2, :]
                    if j % 2 == 0 and n < GH * (STEPS - LAG) + 4:
                        pe.wait_ge(sc_max, it * 48)
                    elif j % 2 == 0:
                        pe.wait_ge(p_ready, cb * 96 + n - 4)
                elif not (isinstance(cb, int) and cb == 0 and n < 2):
                    pe.wait_ge(p_ready, cb * 96 + n - 1)
                elif n == 0:
                    pe.wait_ge(v_biased, 2)
                if cs % 12 == 0 and j == 0:
                    pe.wait_ge(mx_rows[g], cb * 32 + 32)
                pe.matmul(out[0:rows(kt), 0:HALF], k_rep[0:KM, slot, h, kt * P:kt * P + rows(kt)],
                          q_rep[0:KM, slot, h, qh * HALF:qh * HALF + HALF], start=True, stop=True).then_inc(st_full, 1)

            def scores(n):
                g, t, j = n // 24, n % 24 // GH, n % GH
                h = GH * g + j
                if n >= 2 or not isinstance(it, int) or it > 0:
                    pe.wait_ge(sc_max, it * 48 + n - 1)
                if n % 24 == 0:
                    pe.wait_ge(rep_done[g], it * 96 + 96)
                for hh in range(2):
                    last = pe.matmul(ps_max[0:rows(t), n % 2, hh, 0:HALF], q_rep[0:KS, odd, h, t * P:t * P + rows(t)],
                                     k_rep[0:KS, odd, h, hh * HALF:hh * HALF + HALF], start=True, stop=True)
                last.then_inc(sc_full, 1)

            def apply(cb, s, half):
                g, kt = s // 12, s % NT
                slot = odd if cb is it else nxt
                cols = slice(QTR * half, QTR * half + QTR)
                if half == 0:
                    pe.wait_ge(p_ready, cb * 96 + 4 * s + 4)
                if s == 0 and half == 0:
                    pe.wait_ge(v_ready, cb * 2 + 2)
                if kt == 0 and half == 0 and not (isinstance(cb, int) and cb == 0 and s == 0):
                    pe.wait_ge(pv_copied, cb * 4 + s // NT)
                for j in range(GH):
                    n = GH * s + j
                    last = pe.matmul(ps_pv[32 * j:32 * j + 32, cols], v_hat[0:rows(kt), slot, kt * NH + GH * g + j, :],
                                     probs[0:rows(kt), n % RING, cols], start=(kt == 0 and half == 0),
                                     stop=(kt == NT - 1 and half == 1), tile_position=(0, 32 * j))
                if half == 1:
                    last.then_inc(pv_done, 1)

            def turn_outputs(g, r):
                nt = (4, 2)[r]
                bank = take(0, o_done, it * 4 + 2 * g + r + 1)
                pe.wait_ge(pv_copied, (it - 1) * 4 + 2 * g + 2)
                for t in range(nt):
                    last = pe.transpose(bank[:, t * P:(t + 1) * P], out_T[:, g, (4 * r + t) * P:(4 * r + t + 1) * P], ident[:, :])
                last.then_inc(o_turned, 1)

            def turn_maxima(mb, g):
                bank = take(0, mx_copied, mb * NG + g + 1)
                pe.wait_ge(mx_split, mb * NG + g + 1)
                pe.transpose(bank[:, 0:P // 2].bitcast(BF16), max_parts[:, :], ident_bf[:, :]).then_inc(mx_turned, 1)

            def after(s):
                if b1 and s == 0:
                    turn_maxima(it - 1, 1)
                if a and s in (1, 2):
                    bank = take(s - 1, xT_ready, (it + 1) * 2 + s)
                    if s == 1:
                        pe.wait_ge(x_loaded, (it + 1) * 32 + 32)
                    for t in ((0, 1, 2, 3), (4, 5))[s - 1]:
                        n = P if t < NT - 1 else XREST
                        last = pe.transpose(bank[:, (t % 4) * P:(t % 4) * P + n], x_in[0:n, t, :], ident[0:n, 0:n])
                    last.then_inc(x_turned, 1)
                if a and s in (3, 5, 7, 9):
                    i = (s - 3) // 2
                    bank = take(2 + i, qk_elu, (it + 1) * 4 + i + 1)
                    if i == 0:
                        if first_of(it):
                            pe.wait_ge(loaded, 16 * 6)
                        pe.wait_ge(xT_ready, (it + 1) * 2 + 2)
                    for tap in range(TAPS):
                        lo = tap + HALF * (i % 2)
                        last = pe.matmul(bank[:, 0:HALF], w_sb["qk"[i // 2]][:, tap, :], xT[:, nxt, lo:lo + HALF],
                                         start=(tap == 0), stop=(tap == TAPS - 1))
                    last.then_inc(qk_full, 1)
                if b and s == 12:
                    turn_maxima(it, 0)
                if b1 and s in (14, 15):
                    turn_outputs(0, s - 14)
                if b1 and s in (LAG + 2, LAG + 3):
                    turn_outputs(1, s - LAG - 2)
                if a and s in (16, 20):
                    r, nt = ((0, 4), (1, 2))[(s - 16) // 4]
                    bank = take(6 + r, v_biased, (it + 1) * 2 + r + 1)
                    for t in range(4 * r, 4 * r + nt):
                        for tap in range(TAPS):
                            last = pe.matmul(bank[0:rows(t), (t % 4) * P:(t % 4 + 1) * P], xT[:, nxt, tap + t * P:tap + t * P + rows(t)],
                                             w_sb["v"][:, tap, :], start=(tap == 0), stop=(tap == TAPS - 1))
                    last.then_inc(v_full, 1)

            if b and not b1:
                constants()
            for s in range(STEPS):
                c = probs_step(it, s, stages)

                def probs_apply(half):
                    if LAG <= s < LAG + 2:
                        if b1:
                            apply(it - 1, s - LAG + STEPS - 2, half)
                    elif c:
                        apply(c[0], c[1] - 2, half)

                if c:
                    scores_T(*c, 0)
                probs_apply(0)
                if c:
                    scores_T(*c, 1)
                if b:
                    scores(2 * s)
                if c:
                    scores_T(*c, 2)
                probs_apply(1)
                if c:
                    scores_T(*c, 3)
                if b:
                    scores(2 * s + 1)
                after(s)

        run(pe, body)


QK = 16
E2 = 256
NE, CAP = 64, 128
FFN = 512
NF = FFN // P
EPS = 1e-5
NEG = -1e30

PLACES = ([("values", 0), ("values", 1), ("local", 0), ("local", 1)] + [("scores", t) for t in range(NT)]
          + [("turn3", 0), ("logits", 0), ("turn_max", 0)]
          + [("ffn1", f) for f in range(NF)] + [("ranks", 0), ("scores_T", 0), ("scores_T", 1), ("scores_T", 2), ("ffn2", 0),
             ("scores_T", 3), ("scores_T", 4), ("scores_T", 5), ("ffn2", 1), ("turn2", 0), ("attend", 0), ("qk", 0),
             ("turn_att", 0), ("qk", 1), ("project", 0)])
SLOT = {place: n % 4 for n, place in enumerate(PLACES)}


def gated_ahead(nc, ctx, hall, expand, project, pos_mult, router_T, w1_T, b1, w2_T, b2):
    def sb(name, shape, dt):
        return ctx.enter_context(nc.sbuf_tensor(name, shape, dt))

    def sem(name):
        return ctx.enter_context(nc.semaphore(name))

    expand_sb = sb("expand_sb", [P, 2 * QK + 2 * E2], F32)
    qk_w = sb("qk_w", [P, 2, 6, QK], F32)
    project_sb = sb("project_sb", [P, 2, P], F32)
    router_sb = sb("router_sb", [P, NE], F32)
    w1_sb = sb("w1_sb", [P, FFN], F32)
    w2_sb = sb("w2_sb", [P, NF, P], F32)
    b1_col = sb("b1_col", [P, NF], F32)
    b2_row = sb("b2_row", [P, P], F32)
    mult_col = sb("mult_col", [P, 1], F32)
    ident = sb("ident2", [P, P], F32)
    ident_bf = sb("ident2_bf", [P, P], BF16)
    mask_q = sb("mask_q", [P, P], BF16)
    mask_k = sb("mask_k", [P, P], BF16)
    before_bf = sb("before_bf", [P, P], BF16)
    ones_bf = sb("ones_bf", [P, P], BF16)
    expert_i = sb("expert_i", [P, NE], mybir.dt.int32)
    expert = sb("expert", [P, NE], F32)
    dist_i = sb("dist_i", [P, L], mybir.dt.int32)
    bias_fac = sb("bias_fac", [P, L], F32)
    take_out = sb("take_out", [KS, 2, 2], F32)
    half_neg = sb("half_neg", [P, NT], F32)
    mv2 = sb("mv2", [P, NT, 2], F32)
    st2 = sb("st2", [P, NT, 6], F32)
    rs = {n: sb("rs_" + n, [P, NT], F32) for n in ("v", "v2", "v3", "z", "znm", "zr", "znmr")}
    rs_all = sb("rs_all", [P, B * 3 * NT], F32)
    nx1 = sb("nx1", [P, NT, P], F32)
    nx2 = sb("nx2", [P, NT, P], F32)
    hn = sb("hn", [P, NT, P], F32)

    loaded = sem("g_loaded")
    made = sem("g_made")
    by_term = sem("g_by_term")
    biased = sem("g_biased")
    N_MADE = 26
    S = {n: sem("g_" + n) for n in ("x_stat", "x_agg", "x_pool", "x_nx1", "x_nx2", "x_hn", "x_turned")}

    def scale(n, which, t=None):
        return rs_all[:, bass.ds((n * 3 + which) * NT + (t or 0), NT if t is None else 1)]

    def load(sp):
        for dst, src in ((expand_sb[:, :], expand), (project_sb[:, :, :], project.rearrange("(a p) n -> p a n", a=2)),
                         (router_sb[:, :], router_T), (w1_sb[:, :], w1_T), (w2_sb[:, :, :], w2_T.rearrange("(f p) n -> p f n", f=NF)),
                         (b1_col[:, :], b1), (b2_row[:, :], bass.AP(tensor=b2.tensor, offset=0, ap=[[0, P], [1, P]])),
                         (mult_col[:, :], bass.AP(tensor=pos_mult.tensor, offset=0, ap=[[0, P], [1, 1]]))):
            sp.dma_start(dst, src).then_inc(loaded, 16)

    def constants(pool):
        count = [0]

        def step(ins):
            count[0] += 1
            ins.then_inc(made, 1)
            pool.wait_ge(made, count[0])

        def select(t, op, fill, base, per_partition, per_column):
            step(pool.affine_select(out=t, in_=t, compare_op=op, fill=fill, base=base,
                                    pattern=[[per_column, t.shape[-1]]], channel_multiplier=per_partition))

        step(pool.memset(ident[:, :], 0.0))
        select(ident[:, :], ALU.not_equal, 1.0, 0, 1, -1)
        step(pool.tensor_copy(ident_bf[:, :], ident[:, :]))
        step(pool.memset(mask_q[:, :], 0.0))
        select(mask_q[:, :], ALU.is_ge, NEG, 0, 1, -1)
        step(pool.memset(mask_k[:, :], 0.0))
        select(mask_k[:, :], ALU.is_ge, NEG, 0, -1, 1)
        step(pool.memset(before_bf[:, :], 1.0))
        select(before_bf[:, :], ALU.is_ge, 0.0, -1, -1, 1)
        step(pool.memset(ones_bf[:, :], 1.0))
        step(pool.memset(take_out[:, :, :], 0.0))
        for n, which, edges in ((0, 0, ((3, -1.0),)), (0, 1, ((5, -1.0),)),
                                (1, 0, ((1, -1.0), (3, 0.0), (4, -1.0), (5, 0.0))), (1, 1, ((2, -1.0), (3, 0.0)))):
            for term, fill in edges:
                select(take_out[:, n, which:which + 1], ALU.is_ge, fill, term * QK - 1, -1, 0)
        step(pool.iota(expert_i[:, :], pattern=[[1, NE]], base=0, channel_multiplier=0))
        step(pool.tensor_copy(expert[:, :], expert_i[:, :]))
        step(pool.iota(dist_i[:, :], pattern=[[-1, L]], base=0, channel_multiplier=1))
        step(pool.tensor_copy(bias_fac[:, :], dist_i[:, :]))
        pool.wait_ge(loaded, 16 * 8)
        step(pool.tensor_scalar(mult_col[:, :], mult_col[:, :], -1.0, None, ALU.mult))
        step(pool.tensor_scalar(bias_fac[:, :], bias_fac[:, :], -1.0, mult_col[:, 0:1], ALU.mult, ALU.add))
        step(pool.tensor_scalar(bias_fac[:, :], bias_fac[:, :], 80.0, None, ALU.min))
        assert count[0] == N_MADE

    def bias_exp(act, k):
        if k == 0:
            act.wait_ge(made, N_MADE)
        else:
            act.wait_ge(biased, 3)
        act.activation(bias_fac[:, :], bias_fac[:, :], ACT.Exp).then_inc(biased, 1)

    def bias_sigmoid(dve):
        dve.wait_ge(biased, 1)
        dve.tensor_scalar(bias_fac[:, :], bias_fac[:, :], 1.0, None, ALU.add).then_inc(biased, 1)
        dve.wait_ge(biased, 2)
        dve.reciprocal(bias_fac[:, :], bias_fac[:, :]).then_inc(biased, 1)

    def repeat_weights(dve):
        dve.wait_ge(loaded, 16 * 8)
        for j in range(2):
            dve.tensor_copy(qk_w[:, j, :, :], expand_sb[:, QK * j:QK * j + QK].unsqueeze(1).broadcast_to([P, 6, QK])).then_inc(by_term, 1)

    def statistics(dve, n, wait_apart, part=None):
        for t in range(NT):
            if part in (None, t // 2):
                dve.bn_stats(st2[:, t, :], hall[:, bass.ds(n * LP + t * P, P)]).then_inc(S["x_stat"], 1)
        if part in (None, 3):
            wait_apart(dve, S["x_pool"], n * 8 + 8)
            wait_apart(dve, S["x_stat"], n * NT + NT)
            for t in range(NT):
                dve.bn_aggr(mv2[:, t, :], st2[:, t, :]).then_inc(S["x_agg"], 1)

    def start_scales(pool):
        pool.memset(half_neg[:, :], -0.5).then_inc(S["x_pool"], 8)

    def scales(pool, n, wait_apart):
        def step(k, ins):
            ins.then_inc(S["x_pool"], 1)
            wait_apart(pool, S["x_pool"], n * 8 + k + 9)

        r, nmr, r2 = (scale(n, i) for i in range(3))
        wait_apart(pool, S["x_agg"], n * NT + NT)
        step(0, pool.tensor_scalar(rs["v"][:, :], mv2[:, :, 1], EPS, None, ALU.add))
        step(1, pool.tensor_tensor(r, rs["v"][:, :], half_neg[:, :], ALU.pow))
        step(2, pool.tensor_scalar(rs["v"][:, :], mv2[:, :, 0], -1.0, None, ALU.mult))
        step(3, pool.tensor_tensor(nmr, rs["v"][:, :], r, ALU.mult))
        step(4, pool.tensor_tensor(rs["v2"][:, :], r, r, ALU.mult))
        step(5, pool.tensor_tensor(rs["v3"][:, :], rs["v2"][:, :], mv2[:, :, 1], ALU.mult))
        step(6, pool.tensor_scalar(rs["v2"][:, :], rs["v3"][:, :], EPS, None, ALU.add))
        step(7, pool.tensor_tensor(r2, rs["v2"][:, :], half_neg[:, :], ALU.pow))

    def second_norm(pool, n, wait_apart):
        wait_apart(pool, S["x_nx1"], n + 1)
        if not isinstance(n, int) or n > 0:
            wait_apart(pool, S["x_turned"], n)
        pool.tensor_tensor(nx2[:, :, :], nx1[:, :, :], scale(n, 2).unsqueeze(2).broadcast_to([P, NT, P]),
                           ALU.mult).then_inc(S["x_nx2"], 1)

    def normalise(dve, n):
        dve.wait_ge(S["x_pool"], n * 8 + 12)
        if not isinstance(n, int) or n > 0:
            dve.wait_ge(S["x_hn"], n)
        for t in range(NT):
            last = dve.tensor_scalar(nx1[:, t, :], hall[:, bass.ds(n * LP + t * P, P)], scale(n, 0, t),
                                     scale(n, 1, t), ALU.mult, ALU.add)
        last.then_inc(S["x_nx1"], 1)

    def residual(pool, n):
        pool.tensor_tensor(hn[:, :, :], nx1[:, :, :], hall[:, bass.ds(n * LP, LP)].rearrange("p (t c) -> p t c", c=P),
                           ALU.add).then_inc(S["x_hn"], 1)

    return dict(
        expand_sb=expand_sb, by_term=by_term, biased=biased, bias_exp=bias_exp,
        bias_sigmoid=bias_sigmoid, repeat_weights=repeat_weights, qk_w=qk_w, project_sb=project_sb,
        router_sb=router_sb, w1_sb=w1_sb, w2_sb=w2_sb, b1_col=b1_col, b2_row=b2_row,
        mult_col=mult_col, ident=ident, ident_bf=ident_bf, mask_q=mask_q, mask_k=mask_k,
        before_bf=before_bf, ones_bf=ones_bf, expert_i=expert_i, expert=expert, dist_i=dist_i,
        bias_fac=bias_fac, take_out=take_out, half_neg=half_neg, mv2=mv2, st2=st2, rs=rs, nx1=nx1,
        nx2=nx2, hn=hn, loaded=loaded, made=made, S=S, N_MADE=N_MADE, load=load,
        constants=constants, statistics=statistics, scales=scales, start_scales=start_scales,
        second_norm=second_norm, normalise=normalise, residual=residual)


def gated_units(nc, ctx, G, hall, out):
    def sb(name, shape, dt):
        return ctx.enter_context(nc.sbuf_tensor(name, shape, dt))

    def sem(name):
        return ctx.enter_context(nc.semaphore(name))

    by_term, biased, bias_exp = (G[n] for n in ("by_term", "biased", "bias_exp"))
    expand_sb, qk_w, project_sb, router_sb = (
        G[n] for n in "expand_sb qk_w project_sb router_sb".split())
    w1_sb, w2_sb, b1_col, b2_row = (
        G[n] for n in "w1_sb w2_sb b1_col b2_row".split())
    mult_col, ident, ident_bf, mask_q = (
        G[n] for n in "mult_col ident ident_bf mask_q".split())
    mask_k, before_bf, ones_bf, expert_i = (
        G[n] for n in "mask_k before_bf ones_bf expert_i".split())
    expert, dist_i, bias_fac, take_out = (
        G[n] for n in "expert dist_i bias_fac take_out".split())
    half_neg, mv2, st2, rs = (
        G[n] for n in "half_neg mv2 st2 rs".split())
    nx1, nx2, hn, loaded, made = (G[n] for n in "nx1 nx2 hn loaded made".split())
    nx2T = sb("nx2T", [P, LP], F32)
    part_a = sb("part_a", [KS, 2, L], BF16)
    left_a = sb("left_a", [KS, 2, L], F32)
    part_b = sb("part_b", [KS, 2, L], BF16)
    qk_rep = sb("qk_rep", [KM, 2, LP], BF16)
    gel = sb("gel", [P, 4, P], F32)
    vals = sb("vals", [P, NT, P + 1], F32)
    gel_l = sb("gel_l", [P, HALF], F32)
    localT = sb("localT", [P, LP], F32)
    nmax = sb("nmax", [P, NT], F32)
    nmax_parts = sb("nmax_parts", [P, P], BF16)
    nmax_T = sb("nmax_T", [2 * NT, P], BF16)
    p_raw = sb("p_raw", [P, 2, L], F32)
    p_off = [sum(LP - P * j for j in range(k)) for k in range(NT + 1)]
    p_T = sb("p_T", [P, p_off[NT]], F32)
    inv = sb("inv", [P, NT], F32)
    att = sb("att", [P, NT, P], F32)
    attT = sb("attT", [P, LP], F32)
    h2 = sb("h2", [P, NT, P], F32)
    mv3 = sb("mv3", [P, NT, 2], F32)
    st3 = sb("st3", [P, NT, 6], F32)
    nx3 = sb("nx3", [P, NT, P], F32)
    nx3T = sb("nx3T", [P, LP], F32)
    lg = sb("lg", [P, NT, NE], F32)
    top = sb("top", [P, NT, 8], F32)
    top_i = sb("top_i", [P, NT, 8], U32)
    top_f = sb("top_f", [P, NT, 2], F32)
    is_1 = sb("is_1", [P, NT, NE], F32)
    is_2 = sb("is_2", [P, NT, NE], F32)
    chosen = sb("chosen", [P, NT, NE], BF16)
    lg_d = sb("lg_d", [P, NT, NE + 1], F32)
    lg_e = sb("lg_e", [P, NT, NE + 1], F32)
    sum_e = sb("sum_e", [P, NT], F32)
    prob_1 = sb("prob_1", [P, NT], F32)
    prob_2 = sb("prob_2", [P, NT], F32)
    rank = sb("rank", [P, NT, NE], F32)
    kept = sb("kept", [P, NT, NE], F32)
    carry = sb("carry", [P, 2, NE], F32)
    gate = sb("gate", [P, NT], F32)
    hid = sb("hid", [P, NF, LP], F32)
    y_b = sb("y_b", [P, NT, P], F32)
    y_g = sb("y_g", [P, NT, P], F32)
    y_out = sb("y_out", [P, NT, P], F32)

    slots = ctx.enter_context(nc.psum_tensor("slots", [P, 4, 1024], F32))

    setup = sem("g_setup")
    N_SETUP = 8

    S = {n: sem("g_" + n) for n in (
        "x_nx2T", "x_qk", "x_part_a", "x_left",
        "x_part_b", "x_rep", "x_val", "x_gel", "x_vals", "x_loc", "x_gel_l", "x_localT",
        "y_sc", "y_max", "y_hi", "y_split", "y_turned_max", "y_maxT", "y_rows", "y_st", "y_raw", "y_p", "y_att",
        "y_inv", "y_norm", "y_turned", "y_attT", "y_proj", "y_h2",
        "z_stat", "z_agg", "z_pool", "z_nx3", "z_turned", "z_nx3T", "z_logit", "z_lg", "z_top", "z_topi", "z_topf",
        "z_is", "z_d", "z_e", "z_sum", "z_p1", "z_p2", "z_w", "z_chosen", "z_weights", "z_ranked", "z_rank",
        "z_kept", "z_gate", "z_f1", "z_hid", "z_f2", "z_yb", "z_yg", "z_out", "z_stored")} | G["S"]

    block = ctx.enter_context(nc.Block())

    def run(eng, body):
        body(-1, (True, False, False))
        body(0, (True, True, False))
        body(1, (True, True, True))
        with eng.Fori(2, B - 1) as r:
            body(r, (True, True, True))
        body(B - 1, (False, True, True))
        body(B, (False, False, True))

    def wait_apart(eng, sem, value):
        if not isinstance(value, int):
            value = eng.to_reg(value)
            eng.wait_ge(loaded, 16 * 8)
        eng.wait_ge(sem, value)

    def first(it, at):
        return isinstance(it, int) and it <= at

    @block.sync
    def _(sp):
        def body(it, stages):
            _, y, z = stages
            if y:
                wait_apart(sp, S["y_maxT"], it + 1)
                for j in range(2):
                    sp.dma_start(qk_rep[KS + j:KS + j + 1, 0, :], nmax_T[j * NT:(j + 1) * NT, :]).then_inc(S["y_rows"], 16)
            if z:
                wait_apart(sp, S["z_out"], it)
                sp.dma_start(out[bass.ds(it - 1, 1), 0:(NT - 1) * P, :].rearrange("b (t p) c -> p (b t) c", p=P),
                             y_out[:, 0:NT - 1, :]).then_inc(S["z_stored"], 16)
                sp.dma_start(out[bass.ds(it - 1, 1), (NT - 1) * P:L, :].rearrange("b p c -> p (b c)"),
                             y_out[0:REST, NT - 1, :]).then_inc(S["z_stored"], 16)

        run(sp, body)
        sp.wait_ge(S["z_stored"], 32 * B)

    @block.gpsimd
    def _(pool):
        count = [0]

        def step(ins):
            count[0] += 1
            ins.then_inc(setup, 1)
            pool.wait_ge(setup, count[0])

        step(pool.memset(carry[:, :, :], 0.0))
        step(pool.memset(nmax_parts[:, :], 0.0))
        step(pool.memset(qk_rep[KS:KM, 1, :], 1.0))
        step(pool.memset(vals[:, :, P:P + 1], 1.0))
        step(pool.memset(p_T[:, :], 1.0))
        step(pool.memset(localT[:, L:LP], 0.0))
        step(pool.memset(hid[:, :, L:LP], 0.0))
        step(pool.memset(nmax[:, :], 0.0))
        assert count[0] == N_SETUP

        def chain(sem, per, n, k, ins):
            ins.then_inc(sem, 1)
            wait_apart(pool, sem, n * per + k + 1)

        def body(it, stages):
            x, y, z = stages
            if z:
                n = it - 1
                wait_apart(pool, S["z_agg"], n * NT + NT)
                if not first(it, 1):
                    wait_apart(pool, S["z_nx3"], n)
                pool.tensor_scalar(rs["znm"][:, :], mv3[:, :, 0], -1.0, None, ALU.mult).then_inc(S["z_pool"], 1)
                chain(S["z_pool"], 4, n, 1, pool.tensor_scalar(rs["z"][:, :], mv3[:, :, 1], EPS, None, ALU.add))
                chain(S["z_pool"], 4, n, 2, pool.tensor_tensor(rs["zr"][:, :], rs["z"][:, :], half_neg[:, :], ALU.pow))
                pool.tensor_tensor(rs["znmr"][:, :], rs["znm"][:, :], rs["zr"][:, :], ALU.mult).then_inc(S["z_pool"], 1)
            if first(it, -1):
                G["scales"](pool, B - 1, wait_apart)
            if z:
                n = it - 1
                wait_apart(pool, S["z_top"], n * NT + NT)
                if not first(it, 1):
                    wait_apart(pool, S["z_e"], n)
                pool.tensor_tensor(lg_d[:, :, 0:NE], lg[:, :, :], top[:, :, 0:1].broadcast_to([P, NT, NE]),
                                   ALU.subtract).then_inc(S["z_d"], 1)
                pool.tensor_tensor(lg_d[:, :, NE:NE + 1], top[:, :, 1:2], top[:, :, 0:1], ALU.subtract).then_inc(S["z_d"], 1)
            if x and not first(it, -1):
                G["second_norm"](pool, it + 1, wait_apart)
            if y:
                if first(it, 0):
                    pool.wait_ge(biased, 4)
                for k in range(NT):
                    w = L - P * k
                    wait_apart(pool, S["y_raw"], it * NT + k + 1)
                    if k == 0 and not first(it, 0):
                        wait_apart(pool, S["y_att"], it)
                    pool.tensor_tensor(p_T[0:rows(k), p_off[k]:p_off[k] + w], p_raw[0:rows(k), k % 2, 0:w],
                                       bias_fac[0:rows(k), 0:w], ALU.mult).then_inc(S["y_p"], 1)
            if z:
                n = it - 1
                wait_apart(pool, S["z_p1"], n + 1)
                pool.tensor_tensor(prob_2[:, :], lg_e[:, :, NE], prob_1[:, :], ALU.mult).then_inc(S["z_p2"], 1)
                pool.tensor_tensor(is_1[:, :, :], is_1[:, :, :], prob_1[:, :].unsqueeze(2).broadcast_to([P, NT, NE]),
                                   ALU.mult).then_inc(S["z_w"], 1)
                wait_apart(pool, S["z_p2"], n + 1)
                pool.tensor_tensor(is_2[:, :, :], is_2[:, :, :], prob_2[:, :].unsqueeze(2).broadcast_to([P, NT, NE]),
                                   ALU.mult).then_inc(S["z_w"], 1)
                wait_apart(pool, S["z_w"], n * 2 + 2)
                pool.tensor_tensor(is_1[:, :, :], is_1[:, :, :], is_2[:, :, :], ALU.add).then_inc(S["z_weights"], 1)
                wait_apart(pool, S["z_gate"], n + 1)
                wait_apart(pool, S["z_yb"], n * 2 + 2)
                pool.tensor_tensor(y_g[:, :, :], y_b[:, :, :], gate[:, :].unsqueeze(2).broadcast_to([P, NT, P]),
                                   ALU.mult).then_inc(S["z_yg"], 1)
                wait_apart(pool, S["z_yg"], n + 1)
                if not first(it, 1):
                    wait_apart(pool, S["z_stored"], n * 32)
                pool.tensor_tensor(y_out[:, :, :], y_g[:, :, :], h2[:, :, :], ALU.add).then_inc(S["z_out"], 1)
            if x and not first(it, -1):
                if y:
                    wait_apart(pool, S["y_h2"], it + 1)
                G["residual"](pool, it + 1)

        run(pool, body)

    @block.scalar
    def _(act):
        act.wait_ge(loaded, 16 * 8)

        def body(it, stages):
            x, y, z = stages

            def local(j):
                act.wait_ge(S["x_loc"], it * 2 + j + 1)
                if j or not first(it, 0):
                    act.wait_ge(S["x_localT"], it * 2 + j)
                act.activation(gel_l[:, :], slots[:, SLOT["local", j], 512:512 + HALF], ACT.Gelu).then_inc(S["x_gel_l"], 1)

            def logits(n):
                act.wait_ge(S["z_d"], n * 2 + 2)
                if not first(it, 1):
                    act.wait_ge(S["z_p2"], n)
                act.activation(lg_e[:, :, :], lg_d[:, :, :], ACT.Exp).then_inc(S["z_e"], 1)

            if y:
                for j, (t0, nt) in enumerate(((0, 4), (4, 2))):
                    act.wait_ge(S["x_val"], it * 2 + j + 1)
                    if j or not first(it, 0):
                        act.wait_ge(S["x_vals"], it * 2 + j)
                    act.activation(gel[:, 0:nt, :], slots[:, SLOT["values", j], 0:nt * E2].rearrange("p (t c) -> p t c", c=E2)[:, :, P:E2],
                                   ACT.Gelu).then_inc(S["x_gel"], 1)
                local(0)
                local(1)
            if z:
                n = it - 1
                act.wait_ge(S["z_pool"], n * 4 + 4)
                for t in range(NT if y else NT // 2):
                    last = act.activation(nx3[:, t, :], h2[:, t, :], ACT.Identity,
                                          scale=rs["zr"][:, t:t + 1], bias=rs["znmr"][:, t:t + 1])
                last.then_inc(S["z_nx3"], 1)
                act.wait_ge(S["z_turned"], n + 1)
                if not first(it, 1):
                    act.wait_ge(S["z_f1"], n * NF)
                act.copy(nx3T[:, :], slots[:, SLOT["turn3", 0], 0:LP]).then_inc(S["z_nx3T"], 1)
            if y:
                maxima(it)
            if z:
                for f in range(NF):
                    act.wait_ge(S["z_f1"], n * NF + f + 1)
                    if f == 0 and not first(it, 1):
                        act.wait_ge(S["z_f2"], n * 2)
                    act.activation(hid[:, f, 0:L].rearrange("p (a l) -> p a l", a=2),
                                   slots[:, SLOT["ffn1", f], :].rearrange("p (a l) -> p a l", a=2)[:, :, 0:HALF],
                                   ACT.Gelu, bias=b1_col[:, f:f + 1]).then_inc(S["z_hid"], 1)
            if z and not y:
                logits(it - 1)
            if y:
                if first(it, 0):
                    bias_exp(act, 1)
                for k in range(NT):
                    w = L - P * k
                    act.wait_ge(S["y_st"], it * NT + k + 1)
                    if k >= 2:
                        act.wait_ge(S["y_p"], it * NT + k - 1)
                    act.activation(p_raw[0:rows(k), k % 2, 0:w], slots[0:rows(k), SLOT["scores_T", k], 0:w], ACT.Exp,
                                   scale=QK ** -0.5).then_inc(S["y_raw"], 1)
                    if z and k == 1:
                        logits(it - 1)

            def split(j, second):
                n = it + 1
                if second:
                    act.wait_ge(S["x_left"], n * 2 + j + 1)
                    act.copy(part_b[:, j, :], left_a[:, j, :]).then_inc(S["x_part_b"], 1)
                    return
                act.wait_ge(S["x_qk"], n * 2 + j + 1)
                if not first(it, -1):
                    act.wait_ge(S["x_rep"], n * 2 + j - 1)
                act.copy(part_a[:, j, :].rearrange("p (a l) -> p a l", a=2),
                         slots[0:KS, SLOT["qk", j], :].rearrange("p (a l) -> p a l", a=2)[:, :, 0:HALF]).then_inc(S["x_part_a"], 1)

            if x:
                act.wait_ge(S["x_turned"], it + 2)
                act.copy(nx2T[:, :], slots[:, SLOT["turn2", 0], 0:LP]).then_inc(S["x_nx2T"], 1)
                split(0, False)
            if y:
                act.wait_ge(S["y_turned"], it + 1)
                act.copy(attT[:, :], slots[:, SLOT["turn_att", 0], 0:LP]).then_inc(S["y_attT"], 1)
            if x:
                split(0, True)
                split(1, False)
                split(1, True)

        def maxima(it):
            act.wait_ge(S["y_turned_max"], it + 1)
            if not first(it, 0):
                act.wait_ge(S["y_rows"], it * 32)
            act.copy(nmax_T[:, :], slots[0:2 * NT, SLOT["turn_max", 0], 0:P // 2].bitcast(BF16)).then_inc(S["y_maxT"], 1)

        run(act, body)

    @block.vector
    def _(dve):
        def split_first(n, j):
            z_ps = slots[0:KS, SLOT["qk", j], :].rearrange("p (a l) -> p a l", a=2)[:, :, 0:HALF]
            dve.wait_ge(S["x_part_a"], n * 2 + j + 1)
            dve.scalar_tensor_tensor(left_a[:, j, :].rearrange("p (a l) -> p a l", a=2), part_a[:, j, :].rearrange("p (a l) -> p a l", a=2),
                                     take_out[:, j, 0:1], z_ps, ALU.mult, ALU.add).then_inc(S["x_left"], 1)

        def split_rest(n, j):
            dve.wait_ge(S["x_part_b"], n * 2 + j + 1)
            dve.scalar_tensor_tensor(qk_rep[0:KS, j, 0:L], part_b[:, j, :], take_out[:, j, 1:2], left_a[:, j, :],
                                     ALU.mult, ALU.add).then_inc(S["x_rep"], 1)

        def body(it, stages):
            x, y, z = stages
            if y and first(it, 0):
                dve.wait_ge(setup, N_SETUP)
            def maxima(t):
                dve.wait_ge(S["y_sc"], it * NT + t + 1)
                dve.tensor_reduce(nmax[0:rows(t), t:t + 1], slots[0:rows(t), SLOT["scores", t], 0:min(P * (t + 1), L)],
                                  AX.X, ALU.max, negate=True).then_inc(S["y_max"], 1)

            def values(j):
                t0, nt = ((0, 4), (4, 2))[j]
                dve.wait_ge(S["x_gel"], it * 2 + j + 1)
                dve.tensor_tensor(vals[:, t0:t0 + nt, 0:P], slots[:, SLOT["values", j], 0:nt * E2].rearrange("p (t c) -> p t c", c=E2)[:, :, 0:P],
                                  gel[:, 0:nt, :], ALU.mult).then_inc(S["x_vals"], 1)

            def transform(j):
                n, ts = it - 1, slice(3 * j, 3 * j + 3)
                dve.wait_ge(S["z_f2"], n * 2 + j + 1)
                if not first(it, 1):
                    dve.wait_ge(S["z_yg"], n)
                dve.tensor_tensor(y_b[:, ts, :], slots[:, SLOT["ffn2", j], 0:3 * P].rearrange("p (t c) -> p t c", c=P),
                                  b2_row[:, :].unsqueeze(1).broadcast_to([P, 3, P]), ALU.add).then_inc(S["z_yb"], 1)

            def local(j):
                dve.wait_ge(S["x_gel_l"], it * 2 + j + 1)
                dve.tensor_tensor(localT[:, HALF * j:HALF * j + HALF], slots[:, SLOT["local", j], 0:HALF], gel_l[:, :],
                                  ALU.mult).then_inc(S["x_localT"], 1)

            if z:
                n = it - 1
                dve.wait_ge(S["y_h2"], n + 1)
                for t in range(NT):
                    dve.bn_stats(st3[:, t, :], h2[:, t, :]).then_inc(S["z_stat"], 1)
                wait_apart(dve, S["z_stat"], n * NT + NT)
                for t in range(NT):
                    dve.bn_aggr(mv3[:, t, :], st3[:, t, :]).then_inc(S["z_agg"], 1)
                if not y:
                    dve.wait_ge(S["z_turned"], n)
                    dve.wait_ge(S["z_pool"], n * 4 + 4)
                    for t in range(NT // 2, NT):
                        last = dve.tensor_scalar(nx3[:, t, :], h2[:, t, :], rs["zr"][:, t:t + 1], rs["znmr"][:, t:t + 1],
                                                 ALU.mult, ALU.add)
                    last.then_inc(S["z_nx3"], 1)
            if y:
                if not first(it, 0):
                    split_rest(it, 1)
                for j in range(2):
                    values(j)
                for j in range(2):
                    local(j)
                for t in range(NT):
                    maxima(t)
                dve.wait_ge(S["y_max"], it * NT + NT)
                if not first(it, 0):
                    dve.wait_ge(S["y_turned_max"], it)
                dve.tensor_copy(nmax_parts[:, 0:NT], nmax[:, :]).then_inc(S["y_hi"], 1)
                dve.wait_ge(S["y_hi"], it + 1)
                dve.tensor_tensor(nmax_parts[:, NT:2 * NT], nmax[:, :], nmax_parts[:, 0:NT], ALU.subtract).then_inc(S["y_split"], 1)
            if first(it, -1):
                G["statistics"](dve, B - 1, wait_apart)
            if z:
                n = it - 1
                dve.wait_ge(S["z_logit"], n + 1)
                if not first(it, 1):
                    dve.wait_ge(S["z_d"], n * 2)
                dve.tensor_copy(lg[:, :, :], slots[:, SLOT["logits", 0], 0:NT * NE].rearrange("p (t e) -> p t e", e=NE)).then_inc(S["z_lg"], 1)
                wait_apart(dve, S["z_lg"], n + 1)
                for t in range(NT):
                    dve.max(top[:, t, :], lg[:, t, :]).then_inc(S["z_top"], 1)
                wait_apart(dve, S["z_top"], n * NT + NT)
                for t in range(NT):
                    last = dve.max_index(top_i[:, t, :], top[:, t, :], lg[:, t, :])
                last.then_inc(S["z_topi"], 1)
                dve.wait_ge(S["z_topi"], n + 1)
                dve.tensor_copy(top_f[:, :, :], top_i[:, :, 0:2]).then_inc(S["z_topf"], 1)
                dve.wait_ge(S["z_topf"], n + 1)
                if not first(it, 1):
                    dve.wait_ge(S["z_kept"], n)
                for j, onehot in enumerate((is_1, is_2)):
                    dve.tensor_tensor(onehot[:, :, :], expert[:, :].unsqueeze(1).broadcast_to([P, NT, NE]),
                                      top_f[:, :, j:j + 1].broadcast_to([P, NT, NE]), ALU.is_equal).then_inc(S["z_is"], 1)
                dve.wait_ge(S["z_is"], n * 2 + 2)
                if not first(it, 1):
                    dve.wait_ge(S["z_ranked"], n)
                dve.tensor_tensor(chosen[:, :, :], is_1[:, :, :], is_2[:, :, :], ALU.add).then_inc(S["z_chosen"], 1)
            if x and not first(it, -1):
                G["normalise"](dve, it + 1)
            if z:
                dve.wait_ge(S["z_ranked"], n + 1)
                dve.tensor_tensor(rank[:, :, :], slots[:, SLOT["ranks", 0], 0:NT * NE].rearrange("p (t e) -> p t e", e=NE),
                                  carry[:, 0, :].unsqueeze(1).broadcast_to([P, NT, NE]), ALU.add).then_inc(S["z_rank"], 1)
                dve.tensor_tensor(carry[:, 1, :], carry[:, 0, :], slots[:, SLOT["ranks", 0], 512:512 + NE], ALU.add).then_inc(S["z_rank"], 1)
                dve.wait_ge(S["z_rank"], n * 3 + 2)
                dve.tensor_copy(carry[:, 0, :], carry[:, 1, :]).then_inc(S["z_rank"], 1)
                transform(0)
                dve.wait_ge(S["z_e"], n + 1)
                dve.tensor_reduce(sum_e[:, :], lg_e[:, :, 0:NE], AX.X, ALU.add).then_inc(S["z_sum"], 1)
                dve.wait_ge(S["z_sum"], n + 1)
                if not first(it, 1):
                    dve.wait_ge(S["z_w"], n * 2)
                dve.reciprocal(prob_1[:, :], sum_e[:, :]).then_inc(S["z_p1"], 1)
                transform(1)
                dve.wait_ge(S["z_weights"], n + 1)
                dve.scalar_tensor_tensor(kept[:, :, :], rank[:, :, :], float(CAP), is_1[:, :, :], ALU.is_lt, ALU.mult).then_inc(S["z_kept"], 1)
                dve.wait_ge(S["z_kept"], n + 1)
                if not first(it, 1):
                    dve.wait_ge(S["z_yg"], n)
                dve.tensor_reduce(gate[:, :], kept[:, :, :], AX.X, ALU.add).then_inc(S["z_gate"], 1)
            if y:
                dve.wait_ge(S["y_att"], it + 1)
                o = slots[:, SLOT["attend", 0], :].rearrange("p (a l) -> p a l", a=2)[:, :, 0:3 * (P + 1)].rearrange("p a (t c) -> p a t c", c=P + 1)
                dve.reciprocal(inv[:, :].rearrange("p (a t) -> p a t", a=2), o[:, :, :, P]).then_inc(S["y_inv"], 1)
                dve.wait_ge(S["y_inv"], it + 1)
                if not first(it, 0):
                    dve.wait_ge(S["y_turned"], it)
                for a in range(2):
                    last = dve.tensor_tensor(att[:, 3 * a:3 * a + 3, :], o[:, a, :, 0:P],
                                             inv[:, 3 * a:3 * a + 3].unsqueeze(2).broadcast_to([P, 3, P]), ALU.mult)
                last.then_inc(S["y_norm"], 1)

            if x:
                split_first(it + 1, 0)
                split_rest(it + 1, 0)
                split_first(it + 1, 1)
                if not y:
                    split_rest(it + 1, 1)
            if y:
                dve.wait_ge(S["y_proj"], it + 1)
                dve.wait_ge(S["x_hn"], it + 1)
                if z:
                    dve.wait_ge(S["z_out"], it)
                dve.tensor_tensor(h2[:, :, :], slots[:, SLOT["project", 0], 0:NT * P].rearrange("p (t c) -> p t c", c=P), hn[:, :, :],
                                  ALU.add).then_inc(S["y_h2"], 1)

        run(dve, body)

    @block.tensor
    def _(pe):
        pe.wait_ge(loaded, 16 * 8)
        pe.wait_ge(by_term, 2)
        tenants = {}

        def body(it, stages):
            x, y, z = stages
            if y and first(it, 0):
                pe.wait_ge(setup, N_SETUP)
            if not first(it, 0):
                before = [("turn_att", 0, "y_attT", it), ("project", 0, "y_h2", it)]
                if x or y:
                    before += [("qk", j, "x_left", it * 2 + j + 1) for j in range(2)]
                for name, j, reader, value in before:
                    tenants[SLOT[name, j]] = (S[reader], value)

            def take(name, i, reader, value):
                k = SLOT[name, i]
                if k in tenants:
                    pe.wait_ge(*tenants[k])
                tenants[k] = (S[reader], value)
                return slots[:, k, :]

            def pieces(lo, hi):
                return [(a, min(b, hi)) for a, b in ((lo, 512), (512, 1024)) if a < min(b, hi)] if lo < 512 else [(lo, hi)]

            def turn(slot, src):
                for t in range(NT):
                    last = pe.transpose(slot[:, t * P:(t + 1) * P], src[:, t, :], ident[:, :])
                return last

            def ffn1(f):
                n = it - 1
                o = take("ffn1", f, "z_hid", n * NF + f + 1)
                for h in range(2):
                    last = pe.matmul(o[:, 512 * h:512 * h + HALF], w1_sb[:, f * P:(f + 1) * P], nx3T[:, h * HALF:(h + 1) * HALF],
                                     start=True, stop=True)
                last.then_inc(S["z_f1"], 1)

            def ffn2(j):
                n = it - 1
                o = take("ffn2", j, "z_yb", n * 2 + j + 1)
                if j == 0:
                    pe.wait_ge(S["z_hid"], n * NF + NF)
                for t in range(3 * j, 3 * j + 3):
                    for f in range(NF):
                        last = pe.matmul(o[:, (t % 3) * P:(t % 3 + 1) * P], hid[:, f, (t * P):(t + 1) * P], w2_sb[:, f, :],
                                         start=(f == 0), stop=(f == NF - 1))
                last.then_inc(S["z_f2"], 1)

            def scores(t):
                o = take("scores", t, "y_max", it * NT + t + 1)
                if t == 0:
                    pe.wait_ge(S["x_rep"], it * 2 + 2)
                w = min(P * (t + 1), L)
                for a, b in pieces(0, w):
                    diag = b == w
                    last = pe.matmul(o[0:rows(t), a:b], qk_rep[0:KS, 0, t * P:t * P + rows(t)], qk_rep[0:KS, 1, a:b],
                                     start=True, stop=not diag)
                    if diag:
                        last = pe.matmul(o[0:rows(t), t * P:w], ident_bf[0:rows(t), 0:rows(t)], mask_q[0:rows(t), 0:rows(t)],
                                         start=False, stop=True)
                last.then_inc(S["y_sc"], 1)

            def values(j):
                t0, nt = ((0, 4), (4, 2))[j]
                o = take("values", j, "x_vals", it * 2 + j + 1)
                for t in range(t0, t0 + nt):
                    c = (t - t0) * E2
                    last = pe.matmul(o[:, c:c + E2].rearrange("p (a c) -> p a c", a=2), nx2T[:, t * P:(t + 1) * P],
                                     expand_sb[:, 2 * QK:2 * QK + 2 * E2].rearrange("p (a c) -> p a c", a=2)[:, :, P:E2],
                                     start=True, stop=True)
                last.then_inc(S["x_val"], 1)

            def local(j):
                o = take("local", j, "x_localT", it * 2 + j + 1)
                for a in range(2):
                    c = 2 * QK + a * E2
                    last = pe.matmul(o[:, 512 * a:512 * a + HALF], expand_sb[:, c:c + P], nx2T[:, j * HALF:(j + 1) * HALF],
                                     start=True, stop=True)
                last.then_inc(S["x_loc"], 1)

            def scores_T(k):
                o = take("scores_T", k, "y_raw", it * NT + k + 1)
                if k == 0:
                    pe.wait_ge(S["y_rows"], it * 32 + 32)
                w = L - P * k
                for a, b in pieces(0, w):
                    diag = a == 0
                    last = pe.matmul(o[0:rows(k), a:b], qk_rep[0:KM, 1, k * P:k * P + rows(k)], qk_rep[0:KM, 0, k * P + a:k * P + b],
                                     start=True, stop=not diag)
                    if diag:
                        last = pe.matmul(o[0:rows(k), 0:rows(k)], ident_bf[0:rows(k), 0:rows(k)], mask_k[0:rows(k), 0:rows(k)],
                                         start=False, stop=True)
                last.then_inc(S["y_st"], 1)

            def qk(j):
                n = it + 1
                o = take("qk", j, "x_left", n * 2 + j + 1)
                if j == 0:
                    pe.wait_ge(S["x_nx2T"], n + 1)
                for h in range(2):
                    last = pe.matmul(o[0:KS, 512 * h:512 * h + HALF], qk_w[:, j, :, :].rearrange("p a c -> p (a c)"),
                                     nx2T[:, h * HALF:(h + 1) * HALF], start=True, stop=True)
                last.then_inc(S["x_qk"], 1)

            if y:
                values(0)
                values(1)
                local(0)
                local(1)
                for t in range(NT):
                    scores(t)
            if z:
                n = it - 1
                o = take("turn3", 0, "z_nx3T", n + 1)
                pe.wait_ge(S["z_nx3"], n + 1 if y else n + 2)
                turn(o, nx3).then_inc(S["z_turned"], 1)
                o = take("logits", 0, "z_lg", n + 1)
                pe.wait_ge(S["z_nx3T"], n + 1)
                for t in range(NT):
                    last = pe.matmul(o[:, t * NE:(t + 1) * NE], nx3T[:, t * P:(t + 1) * P], router_sb[:, :], start=True, stop=True)
                last.then_inc(S["z_logit"], 1)
            if y:
                o = take("turn_max", 0, "y_maxT", it + 1)
                pe.wait_ge(S["y_split"], it + 1)
                pe.transpose(o[:, 0:P // 2].bitcast(BF16), nmax_parts[:, :], ident_bf[:, :]).then_inc(S["y_turned_max"], 1)
            if z:
                for f in range(NF):
                    ffn1(f)
            if z:
                n = it - 1
                o = take("ranks", 0, "z_rank", n * 3 + 2)
                pe.wait_ge(S["z_chosen"], n + 1)
                for t in range(NT):
                    for u in range(t + 1):
                        last = pe.matmul(o[:, t * NE:(t + 1) * NE], (before_bf if u == t else ones_bf)[0:rows(u), :],
                                         chosen[0:rows(u), u, :], start=(u == 0), stop=(u == t))
                for u in range(NT):
                    last = pe.matmul(o[:, 512:512 + NE], ones_bf[0:rows(u), :], chosen[0:rows(u), u, :], start=(u == 0), stop=(u == NT - 1))
                last.then_inc(S["z_ranked"], 1)
            if y:
                for k in range(3):
                    scores_T(k)
            if z:
                ffn2(0)
            if y:
                for k in range(3, NT):
                    scores_T(k)
            if z:
                ffn2(1)
            if x:
                n = it + 1
                o = take("turn2", 0, "x_nx2T", n + 1)
                pe.wait_ge(S["x_nx2"], n + 1)
                turn(o, nx2).then_inc(S["x_turned"], 1)
            if y:
                o = take("attend", 0, "y_norm", it + 1)
                pe.wait_ge(S["x_vals"], it * 2 + 2)
                pe.wait_ge(S["y_p"], it * NT + NT)
                for t in range(NT):
                    c = 512 * (t // 3) + (P + 1) * (t % 3)
                    for k in range(t + 1):
                        q = p_off[k] + P * (t - k)
                        last = pe.matmul(o[:, c:c + P + 1], p_T[0:rows(k), q:q + P], vals[0:rows(k), k, :],
                                         start=(k == 0), stop=(k == t))
                last.then_inc(S["y_att"], 1)
            if x:
                qk(0)
            if y:
                o = take("turn_att", 0, "y_attT", it + 1)
                pe.wait_ge(S["y_norm"], it + 1)
                turn(o, att).then_inc(S["y_turned"], 1)
            if x:
                qk(1)
            if y:
                o = take("project", 0, "y_h2", it + 1)
                pe.wait_ge(S["y_attT"], it + 1)
                pe.wait_ge(S["x_localT"], it * 2 + 2)
                for t in range(NT):
                    for a, src in enumerate((localT, attT)):
                        last = pe.matmul(o[:, t * P:(t + 1) * P], src[:, t * P:(t + 1) * P], project_sb[:, a, :],
                                         start=(a == 0), stop=(a == 1))
                last.then_inc(S["y_proj"], 1)

        run(pe, body)


def build(nc, x, wq, wk, wv, bq, bk, bv, expand, project, pos_mult, router_T, w1_T, b1, w2_T, b2, out):
    with ExitStack() as whole:
        hall = whole.enter_context(nc.sbuf_tensor("hall", [P, B * LP], F32))
        ahead = gated_ahead(nc, whole, hall, expand, project, pos_mult, router_T, w1_T, b1, w2_T, b2)
        with ExitStack() as ctx:
            token_attention(nc, ctx, hall, ahead, x, wq, wk, wv, bq, bk, bv)
        with ExitStack() as ctx:
            gated_units(nc, ctx, ahead, hall, out)


def kernel(**inputs):
    import numpy as np
    import concourse.bacc as bacc
    from concourse.bass_utils import run_bass_kernel_spmd

    def plain(name):
        return np.ascontiguousarray(inputs[name])

    nc = bacc.Bacc("TRN2", target_bir_lowering=False, num_devices=1)
    arrays = {
        "x": plain("x"),
        "wq": plain("L0_tok_WQ"), "wk": plain("L0_tok_WK"), "wv": plain("L0_tok_WV"),
        "bq": plain("L0_tok_BQ"), "bk": plain("L0_tok_BK"), "bv": plain("L0_tok_BV"),
        "expand": plain("L0_attn_expand"), "project": plain("L0_attn_project"),
        "pos_mult": plain("L0_attn_position_bias_mult").reshape(1),
        "router_T": np.ascontiguousarray(plain("L0_ffn_router_w").T),
        "w1_T": np.ascontiguousarray(plain("L0_ffn_w1").T),
        "b1": np.ascontiguousarray(plain("L0_ffn_b1").reshape(NF, P).T),
        "w2_T": np.ascontiguousarray(plain("L0_ffn_w2").T),
        "b2": plain("L0_ffn_b2"),
    }
    arrays = {"in_" + n: a for n, a in arrays.items()}
    args = [nc.dram_tensor(n, a.shape, mybir.dt.from_np(a.dtype), kind="ExternalInput").ap() for n, a in arrays.items()]
    args.append(nc.dram_tensor("out_h", (B, L, P), F32, kind="ExternalOutput").ap())
    build(nc, *args)
    return run_bass_kernel_spmd(nc, [arrays], core_ids=[0]).results[0]["out_h"]
```
